# Optimizing a Trainium2 kernel written in Bass

```python
import numpy as np
import jax
import jax.numpy as jnp

def _softmax(x, axis=-1):
    return jax.nn.softmax(x, axis=axis)

def _gelu(x):
    return jax.nn.gelu(x, approximate=True)

def _silu(x):
    return jax.nn.silu(x)

def _sigmoid(x):
    return jax.nn.sigmoid(x)

def _layernorm(x, axis=-1, eps=1e-05):
    m = jnp.mean(x, axis=axis, keepdims=True)
    v = jnp.var(x, axis=axis, keepdims=True)
    return (x - m) / jnp.sqrt(v + eps)

def _scatter_add(tgt, idx, src, axis=0):
    return tgt.at[idx].add(src)

def _segment_sum(src, seg, n):
    return jax.ops.segment_sum(src, seg, n)
kernel_name = 'mk_macaron_d2_jaxref_r8_028f56'

def setup_inputs(seed: int=0):
    np.random.seed(seed)
    _w = jnp.asarray

    def _L0_attn_setup():
        import jax, jax.numpy as jnp
        from jax import lax
        import numpy as np
        B, L, D_MODEL = (1, 128, 256)
        H, P, G, S = (32, 64, 8, 32)
        D_SSM = H * P
        CONV_DIM = D_SSM + 2 * G * S
        PROJ_DIM = 2 * D_SSM + 2 * G * S + H
        K = 4
        EPS = 1e-05

        def _forward(hidden_states, W_in, b_in, conv_w, conv_b, A_log, D_param, dt_bias, norm_w, W_out, b_out, mup_vector):
            Bb, Ll, _ = hidden_states.shape
            zxbcdt = (hidden_states @ W_in + b_in) * mup_vector
            z = zxbcdt[..., :D_SSM]
            xBC = zxbcdt[..., D_SSM:D_SSM + CONV_DIM]
            dt = zxbcdt[..., D_SSM + CONV_DIM:]
            xBC_t = jnp.transpose(xBC, (0, 2, 1))
            conv = lax.conv_general_dilated(xBC_t, conv_w[:, None, :], (1,), [(K - 1, 0)], dimension_numbers=('NCH', 'OIH', 'NCH'), feature_group_count=CONV_DIM)
            xBC = jnp.transpose(jax.nn.silu(conv + conv_b[None, :, None]), (0, 2, 1))
            x = xBC[..., :D_SSM].reshape(Bb, Ll, H, P)
            Bm = xBC[..., D_SSM:D_SSM + G * S].reshape(Bb, Ll, G, S)
            Cm = xBC[..., D_SSM + G * S:].reshape(Bb, Ll, G, S)
            rep = H // G
            Bh = jnp.repeat(Bm, rep, axis=2)
            Ch = jnp.repeat(Cm, rep, axis=2)
            dt = jax.nn.softplus(dt + dt_bias)
            a = jnp.exp(dt * -jnp.exp(A_log))
            db = dt[..., None, None] * x[..., None] * Bh[:, :, :, None, :]

            def combine(e1, e2):
                a1, s1 = e1
                a2, s2 = e2
                return (a1 * a2, a2[..., None, None] * s1 + s2)
            states = lax.associative_scan(combine, (a, db), axis=1)[1]
            y = jnp.einsum('blhps,blhs->blhp', states, Ch) + D_param[None, None, :, None] * x
            y = y.reshape(Bb, Ll, D_SSM) * jax.nn.silu(z)
            yg = y.reshape(Bb, Ll, G, D_SSM // G)
            var = jnp.mean(yg * yg, axis=-1, keepdims=True)
            y = (yg * lax.rsqrt(var + EPS)).reshape(Bb, Ll, D_SSM) * norm_w
            return y @ W_out + b_out
        key = jax.random.key(seed)
        ks = jax.random.split(key, 12)
        mults = np.array([0.9, 1.1, 0.8, 1.2, 1.0], dtype=np.float32)
        mv = np.ones(PROJ_DIM, dtype=np.float32)
        mv[:D_SSM] *= mults[0]
        mv[D_SSM:2 * D_SSM] *= mults[1]
        mv[2 * D_SSM:2 * D_SSM + G * S] *= mults[2]
        mv[2 * D_SSM + G * S:2 * D_SSM + 2 * G * S] *= mults[3]
        mv[2 * D_SSM + 2 * G * S:] *= mults[4]
        return {'hidden_states': jax.random.normal(ks[0], (B, L, D_MODEL), jnp.float32), 'W_in': jax.random.normal(ks[1], (D_MODEL, PROJ_DIM), jnp.float32) * 0.02, 'b_in': jax.random.normal(ks[2], (PROJ_DIM,), jnp.float32) * 0.01, 'conv_w': jax.random.normal(ks[3], (CONV_DIM, K), jnp.float32) * 0.2, 'conv_b': jax.random.normal(ks[4], (CONV_DIM,), jnp.float32) * 0.01, 'A_log': jnp.log(jax.random.uniform(ks[5], (H,), jnp.float32, 1.0, 16.0)), 'D_param': jax.random.normal(ks[6], (H,), jnp.float32) * 0.5 + 1.0, 'dt_bias': jax.random.normal(ks[7], (H,), jnp.float32) * 0.5, 'norm_w': jnp.ones((D_SSM,), jnp.float32) + 0.01 * jax.random.normal(ks[8], (D_SSM,), jnp.float32), 'W_out': jax.random.normal(ks[9], (D_SSM, D_MODEL), jnp.float32) * 0.02, 'b_out': jnp.zeros((D_MODEL,), jnp.float32), 'mup_vector': jnp.asarray(mv)}
    _L0_attn_in = _L0_attn_setup()

    def _L0_ffn_setup():
        import jax, jax.numpy as jnp
        import numpy as np
        E, TOPK, H, I = (8, 2, 256, 512)
        SOFTCAP = 30.0
        key = jax.random.key(seed)
        ks = jax.random.split(key, 5)
        s = 1.0 / np.sqrt(H)
        si = 1.0 / np.sqrt(I)
        return {'hidden_states': jax.random.normal(ks[0], (4, 256, H), jnp.float32), 'w_gate': jax.random.normal(ks[1], (H, E), jnp.float32) * s, 'w1': jax.random.normal(ks[2], (E, H, I), jnp.float32) * s, 'w3': jax.random.normal(ks[3], (E, H, I), jnp.float32) * s, 'w2': jax.random.normal(ks[4], (E, I, H), jnp.float32) * si}
    _L0_ffn_in = _L0_ffn_setup()

    def _L1_attn_setup():
        import jax, jax.numpy as jnp
        import numpy as np
        B, SQ, H = (2, 256, 256)
        NH = 16
        HN = H // NH
        key = jax.random.key(seed)
        ks = jax.random.split(key, 6)
        query = jax.random.normal(ks[0], (B, SQ, H), dtype=jnp.float32)
        k_in = jax.random.normal(ks[1], (B, SQ, H), dtype=jnp.float32)
        v_in = jax.random.normal(ks[2], (B, SQ, H), dtype=jnp.float32)
        Wqkv = jax.random.normal(ks[3], (3 * H, H), dtype=jnp.float32) * (1.0 / np.sqrt(H))
        Wproj = jax.random.normal(ks[4], (H, H), dtype=jnp.float32) * (1.0 / np.sqrt(H))
        bproj = jnp.zeros((H,), dtype=jnp.float32)
        return {'query': query, 'key': k_in, 'value': v_in, 'Wqkv': Wqkv, 'Wproj': Wproj, 'bproj': bproj}
    _L1_attn_in = _L1_attn_setup()

    def _L1_ffn_setup():
        import jax, jax.numpy as jnp
        import numpy as np
        HID = 256
        N_EXP = 32
        F_EXP = 96
        TOP_K = 6
        F_SH = 192
        B, S = (1, 128)
        key = jax.random.key(seed)
        ks = jax.random.split(key, 8)
        s = 0.02
        return {'hidden_states': jax.random.normal(ks[0], (B, S, HID), dtype=jnp.float32), 'gate_w': jax.random.normal(ks[1], (HID, N_EXP), dtype=jnp.float32) * s, 'wg': jax.random.normal(ks[2], (N_EXP, HID, F_EXP), dtype=jnp.float32) * s, 'wu': jax.random.normal(ks[3], (N_EXP, HID, F_EXP), dtype=jnp.float32) * s, 'wd': jax.random.normal(ks[4], (N_EXP, F_EXP, HID), dtype=jnp.float32) * s, 'sg': jax.random.normal(ks[5], (HID, F_SH), dtype=jnp.float32) * s, 'su': jax.random.normal(ks[6], (HID, F_SH), dtype=jnp.float32) * s, 'sd': jax.random.normal(ks[7], (F_SH, HID), dtype=jnp.float32) * s}
    _L1_ffn_in = _L1_ffn_setup()
    _d = {'L0_attn_hidden_states': _L0_attn_in['hidden_states'], 'L0_attn_W_in': _L0_attn_in['W_in'], 'L0_attn_b_in': _L0_attn_in['b_in'], 'L0_attn_conv_w': _L0_attn_in['conv_w'], 'L0_attn_conv_b': _L0_attn_in['conv_b'], 'L0_attn_A_log': _L0_attn_in['A_log'], 'L0_attn_D_param': _L0_attn_in['D_param'], 'L0_attn_dt_bias': _L0_attn_in['dt_bias'], 'L0_attn_norm_w': _L0_attn_in['norm_w'], 'L0_attn_W_out': _L0_attn_in['W_out'], 'L0_attn_b_out': _L0_attn_in['b_out'], 'L0_attn_mup_vector': _L0_attn_in['mup_vector'], 'L0_ffn_w_gate': _L0_ffn_in['w_gate'], 'L0_ffn_w1': _L0_ffn_in['w1'], 'L0_ffn_w3': _L0_ffn_in['w3'], 'L0_ffn_w2': _L0_ffn_in['w2'], 'L1_attn_key': _L1_attn_in['key'], 'L1_attn_value': _L1_attn_in['value'], 'L1_attn_Wqkv': _L1_attn_in['Wqkv'], 'L1_attn_Wproj': _L1_attn_in['Wproj'], 'L1_attn_bproj': _L1_attn_in['bproj'], 'L1_ffn_gate_w': _L1_ffn_in['gate_w'], 'L1_ffn_wg': _L1_ffn_in['wg'], 'L1_ffn_wu': _L1_ffn_in['wu'], 'L1_ffn_wd': _L1_ffn_in['wd'], 'L1_ffn_sg': _L1_ffn_in['sg'], 'L1_ffn_su': _L1_ffn_in['su'], 'L1_ffn_sd': _L1_ffn_in['sd']}
    _x0 = _d['L0_attn_hidden_states']
    _d['L0_attn_hidden_states'] = jax.random.normal(jax.random.fold_in(jax.random.key(seed), 1), (4, 512, 256), dtype=_x0.dtype)
    del _x0
    return _d

def reference(L0_attn_hidden_states, L0_attn_W_in, L0_attn_b_in, L0_attn_conv_w, L0_attn_conv_b, L0_attn_A_log, L0_attn_D_param, L0_attn_dt_bias, L0_attn_norm_w, L0_attn_W_out, L0_attn_b_out, L0_attn_mup_vector, L0_ffn_w_gate, L0_ffn_w1, L0_ffn_w3, L0_ffn_w2, L1_attn_key, L1_attn_value, L1_attn_Wqkv, L1_attn_Wproj, L1_attn_bproj, L1_ffn_gate_w, L1_ffn_wg, L1_ffn_wu, L1_ffn_wd, L1_ffn_sg, L1_ffn_su, L1_ffn_sd):

    def _L0_attn_ref(hidden_states, W_in, b_in, conv_w, conv_b, A_log, D_param, dt_bias, norm_w, W_out, b_out, mup_vector):
        import jax, jax.numpy as jnp
        from jax import lax
        import numpy as np
        B, L, D_MODEL = (1, 128, 256)
        H, P, G, S = (32, 64, 8, 32)
        D_SSM = H * P
        CONV_DIM = D_SSM + 2 * G * S
        PROJ_DIM = 2 * D_SSM + 2 * G * S + H
        K = 4
        EPS = 1e-05

        def _forward(hidden_states, W_in, b_in, conv_w, conv_b, A_log, D_param, dt_bias, norm_w, W_out, b_out, mup_vector):
            Bb, Ll, _ = hidden_states.shape
            zxbcdt = (hidden_states @ W_in + b_in) * mup_vector
            z = zxbcdt[..., :D_SSM]
            xBC = zxbcdt[..., D_SSM:D_SSM + CONV_DIM]
            dt = zxbcdt[..., D_SSM + CONV_DIM:]
            xBC_t = jnp.transpose(xBC, (0, 2, 1))
            conv = lax.conv_general_dilated(xBC_t, conv_w[:, None, :], (1,), [(K - 1, 0)], dimension_numbers=('NCH', 'OIH', 'NCH'), feature_group_count=CONV_DIM)
            xBC = jnp.transpose(jax.nn.silu(conv + conv_b[None, :, None]), (0, 2, 1))
            x = xBC[..., :D_SSM].reshape(Bb, Ll, H, P)
            Bm = xBC[..., D_SSM:D_SSM + G * S].reshape(Bb, Ll, G, S)
            Cm = xBC[..., D_SSM + G * S:].reshape(Bb, Ll, G, S)
            rep = H // G
            Bh = jnp.repeat(Bm, rep, axis=2)
            Ch = jnp.repeat(Cm, rep, axis=2)
            dt = jax.nn.softplus(dt + dt_bias)
            a = jnp.exp(dt * -jnp.exp(A_log))
            db = dt[..., None, None] * x[..., None] * Bh[:, :, :, None, :]

            def combine(e1, e2):
                a1, s1 = e1
                a2, s2 = e2
                return (a1 * a2, a2[..., None, None] * s1 + s2)
            states = lax.associative_scan(combine, (a, db), axis=1)[1]
            y = jnp.einsum('blhps,blhs->blhp', states, Ch) + D_param[None, None, :, None] * x
            y = y.reshape(Bb, Ll, D_SSM) * jax.nn.silu(z)
            yg = y.reshape(Bb, Ll, G, D_SSM // G)
            var = jnp.mean(yg * yg, axis=-1, keepdims=True)
            y = (yg * lax.rsqrt(var + EPS)).reshape(Bb, Ll, D_SSM) * norm_w
            return y @ W_out + b_out
        return _forward(hidden_states, W_in, b_in, conv_w, conv_b, A_log, D_param, dt_bias, norm_w, W_out, b_out, mup_vector)

    def _L0_ffn_ref(hidden_states, w_gate, w1, w3, w2):
        import jax, jax.numpy as jnp
        import numpy as np
        E, TOPK, H, I = (8, 2, 256, 512)
        SOFTCAP = 30.0
        orig_shape = hidden_states.shape
        x = hidden_states.reshape(-1, H)
        logits = x @ w_gate
        logits = SOFTCAP * jnp.tanh(logits / SOFTCAP)
        probs = jax.nn.softmax(logits, axis=-1)
        _, idx = jax.lax.top_k(probs, TOPK)
        mask = jax.nn.one_hot(idx, E, dtype=probs.dtype).sum(-2)
        weights = probs * mask
        out = jnp.zeros_like(x)
        for e in range(E):
            h = jax.nn.silu(x @ w1[e]) * (x @ w3[e])
            out = out + h @ w2[e] * weights[:, e:e + 1]
        return out.reshape(orig_shape)

    def _L1_attn_ref(query, key, value, Wqkv, Wproj, bproj):
        import jax, jax.numpy as jnp
        import numpy as np
        B, SQ, H = (2, 256, 256)
        NH = 16
        HN = H // NH
        b, sq, h = query.shape
        nh, hn = (NH, HN)
        norm = 1.0 / jnp.sqrt(jnp.asarray(hn, query.dtype))
        x = jnp.transpose(query, (1, 0, 2)).reshape(sq * b, h)
        mixed = x @ Wqkv.T
        mixed = mixed.reshape(sq, b, nh, 3, hn)
        q = mixed[..., 0, :]
        k = mixed[..., 1, :]
        v = mixed[..., 2, :]
        q = q.reshape(sq, b * nh, hn).transpose(1, 0, 2)
        k = k.reshape(sq, b * nh, hn).transpose(1, 0, 2)
        v = v.reshape(sq, b * nh, hn).transpose(1, 0, 2)
        attn = jnp.einsum('gqd,gkd->gqk', q, k) * norm
        attn = jax.nn.softmax(attn, axis=-1)
        ctx = jnp.einsum('gqk,gkd->gqd', attn, v)
        ctx = ctx.reshape(nh, b, sq, hn)
        ctx = jnp.transpose(ctx, (2, 1, 0, 3)).reshape(sq * b, h)
        out = ctx @ Wproj.T + bproj
        out = out.reshape(sq, b, h)
        return jnp.transpose(out, (1, 0, 2))

    def _L1_ffn_ref(hidden_states, gate_w, wg, wu, wd, sg, su, sd):
        import jax, jax.numpy as jnp
        import numpy as np
        HID = 256
        N_EXP = 32
        F_EXP = 96
        TOP_K = 6
        F_SH = 192
        B, S = (1, 128)
        orig_shape = hidden_states.shape
        x = hidden_states.reshape(-1, HID)
        scores = jax.nn.sigmoid(x @ gate_w)
        topk_w, topk_i = jax.lax.top_k(scores, TOP_K)
        topk_w = topk_w / (jnp.sum(topk_w, axis=-1, keepdims=True) + 1e-20)
        combine = jnp.sum(jax.nn.one_hot(topk_i, N_EXP, dtype=topk_w.dtype) * topk_w[..., None], axis=1)
        g = jnp.einsum('td,edf->tef', x, wg)
        u = jnp.einsum('td,edf->tef', x, wu)
        act = jax.nn.silu(g) * u
        routed = jnp.einsum('tef,efd,te->td', act, wd, combine)
        routed = routed.reshape(orig_shape)
        shared = jax.nn.silu(hidden_states @ sg) * (hidden_states @ su) @ sd
        return routed + shared
    x = L0_attn_hidden_states
    x = x + 0.5 * _L0_ffn_ref(_layernorm(x, axis=-1), L0_ffn_w_gate, L0_ffn_w1, L0_ffn_w3, L0_ffn_w2)
    x = x + _L0_attn_ref(_layernorm(x, axis=-1), L0_attn_W_in, L0_attn_b_in, L0_attn_conv_w, L0_attn_conv_b, L0_attn_A_log, L0_attn_D_param, L0_attn_dt_bias, L0_attn_norm_w, L0_attn_W_out, L0_attn_b_out, L0_attn_mup_vector)
    x = x + 0.5 * _L0_ffn_ref(_layernorm(x, axis=-1), L0_ffn_w_gate, L0_ffn_w1, L0_ffn_w3, L0_ffn_w2)
    x = x + 0.5 * _L1_ffn_ref(_layernorm(x, axis=-1), L1_ffn_gate_w, L1_ffn_wg, L1_ffn_wu, L1_ffn_wd, L1_ffn_sg, L1_ffn_su, L1_ffn_sd)
    x = x + _L1_attn_ref(_layernorm(x, axis=-1), L1_attn_key, L1_attn_value, L1_attn_Wqkv, L1_attn_Wproj, L1_attn_bproj)
    x = x + 0.5 * _L1_ffn_ref(_layernorm(x, axis=-1), L1_ffn_gate_w, L1_ffn_wg, L1_ffn_wu, L1_ffn_wd, L1_ffn_sg, L1_ffn_su, L1_ffn_sd)
    return x

_drawn_inputs = setup_inputs


def setup_inputs(seed=0):
    import zlib

    import numpy as np

    out = dict(_drawn_inputs(seed))
    spreads = {'L0_attn_b_out': (0.0, 0.1), 'L1_attn_bproj': (0.0, 0.272)}
    factors = {'L0_attn_A_log': 64.0,
     'L0_attn_dt_bias': 8.0,
     'L0_attn_norm_w': 7.285,
     'L1_ffn_gate_w': 8.0,
     'L1_ffn_wg': 8.0,
     'L1_ffn_wu': 8.0,
     'L1_ffn_wd': 8.0,
     'L1_ffn_sg': 5.334,
     'L1_ffn_su': 5.248,
     'L1_ffn_sd': 5.236}
    for name, (base, spread) in spreads.items():
        noise = np.random.default_rng([zlib.crc32(name.encode()), seed]).standard_normal(out[name].shape)
        drawn = base * np.exp(spread * noise) if base else spread * noise
        out[name] = jnp.asarray(drawn.astype(out[name].dtype))
    for name, factor in factors.items():
        out[name] = (out[name] * factor).astype(out[name].dtype)
    return out
```

```python
import concourse.bass as bass
from concourse import mybir
from contextlib import ExitStack

F32 = mybir.dt.float32
F32R = mybir.dt.float32r
BF16 = mybir.dt.bfloat16
ALU = mybir.AluOpType
ACT = mybir.ActivationFunctionType
AX = mybir.AxisListType.X
P = 128

B, L, D = 4, 512, 256
T = B * L
NT = T // P
KD = D // P
EPS = 1e-5

PASSES = ((0, 0), (0, 1), (1, 0))


class Stage:

    def __init__(self, nc, name):
        self.nc, self.name, self.stack, self.sems = nc, name, ExitStack(), []

    def __enter__(self):
        self.stack.__enter__()
        return self

    def __exit__(self, *a):
        self.stack.__exit__(*a)
        if self.sems and a[0] is None:
            self.nc.clear_and_free_semaphores(self.sems)
            self.nc.all_engine_barrier(sem_only=True)

    def sb(self, name, shape, dt=F32):
        return self.stack.enter_context(self.nc.sbuf_tensor(f"{self.name}_{name}", shape, dt))

    def ps(self, name, shape=(P, 512), dt=F32):
        return self.stack.enter_context(self.nc.psum_tensor(f"{self.name}_{name}", list(shape), dt))

    def sem(self, name):
        self.sems.append(self.nc.alloc_semaphore(f"{self.name}_{name}"))
        return self.sems[-1]

    def block(self):
        return self.stack.enter_context(self.nc.Block())


def link(eng, sem, count, instruction):
    count[0] += 1
    instruction.then_inc(sem, 1)
    eng.wait_ge(sem, count[0])


def wait_apart(eng, sem, value, passed):
    eng.wait_ge(sem, value)
    eng.sem_inc(passed, 1)


def product(nc, out, lhs, rhs, start, stop, **kw):
    for n, (a, b) in enumerate(PASSES):
        last = nc.tensor.matmul(out, lhs[a], rhs[b], start=start and n == 0, stop=stop and n == len(PASSES) - 1, **kw)
    return last


def stage_load(nc, M, x_dram):
    with Stage(nc, "load") as s:
        x_in, zero, done, done16 = s.sem("x_in"), s.sem("zero"), s.sem("const"), s.sem("const16")
        block = s.block()

        @block.sync
        def _(sp):
            sp.dma_start(M["x"][:, :].rearrange("p (t d) -> p t d", d=D),
                         x_dram.rearrange("b (t p) d -> p (b t) d", p=P)).then_inc(x_in, 16)
            sp.wait_ge(x_in, 16)

        @block.gpsimd
        def _(pool):
            nc.gpsimd.memset(M["ident"][:, :], 0.0).then_inc(zero, 1)
            nc.gpsimd.memset(M["sel"][:, :], 1.0).then_inc(zero, 1)
            pool.wait_ge(zero, 2)
            nc.gpsimd.affine_select(out=M["ident"][:, :], in_=M["ident"][:, :], compare_op=ALU.not_equal, fill=1.0,
                                    base=0, pattern=[[-1, P]], channel_multiplier=1).then_inc(done, 1)
            for q in range(3):
                pool.wait_ge(done, q + 1)
                rows = M["sel"][32 * q:32 * q + 32, :].rearrange("r (e f) -> r e f", e=32)
                nc.gpsimd.affine_select(out=rows, in_=rows, compare_op=ALU.is_equal, fill=0.0, base=0,
                                        pattern=[[-1, 32], [0, 96]], channel_multiplier=1).then_inc(done, 1)

        @block.vector
        def _(dve):
            nc.vector.memset(M["zero"][:, :], 0.0)
            dve.wait_ge(done, 1)
            nc.vector.tensor_copy(M["ident16"][:, :], M["ident"][:, :]).then_inc(done16, 1)


class Part:

    def sync(self, sp):
        pass

    def gpsimd(self, pool):
        pass

    def scalar(self, act):
        pass

    def tensor(self, pe):
        pass

    def vector(self, dve):
        pass


def run_block(nc, *parts):
    with nc.Block() as block:
        @block.sync
        def _(sp):
            for part in parts:
                part.sync(sp)

        @block.gpsimd
        def _(pool):
            for part in parts:
                part.gpsimd(pool)

        @block.scalar
        def _(act):
            for part in parts:
                part.scalar(act)

        @block.tensor
        def _(pe):
            for part in parts:
                part.tensor(pe)

        @block.vector
        def _(dve):
            for part in parts:
                part.vector(dve)


class Norm(Part):

    BATCH = 4

    def __init__(self, nc, M, s, x_loaded=None):
        self.nc, self.M, self.x_loaded = nc, M, x_loaded
        self.stats = s.sb("stats", [P, NT, 6])
        self.mv = s.sb("mean_var", [P, NT, 2])
        self.veps, self.rstd, self.shift = (s.sb(n, [P, NT]) for n in ("var_eps", "rstd", "shift"))
        self.half = s.sb("minus_half", [P, self.BATCH])
        self.xn = [s.sb(f"xn{j}", [P, D]) for j in range(4)]
        self.psT = [s.ps(f"T{j}") for j in range(4)]
        (self.s_half, self.s_stat, self.s_aggr, self.s_veps, self.s_rstd, self.s_shift, self.s_xn, self.s_tr, self.s_hi,
         self.s_lo) = (s.sem(n) for n in ("half", "stat", "aggr", "veps", "rstd", "shift", "xn", "transposed", "hi", "lo"))

    def gpsimd(self, pool):
        self.nc.gpsimd.memset(self.half[:, :], -0.5).then_inc(self.s_half, 1)
        pool.wait_ge(self.s_half, 1)
        for g in range(NT // self.BATCH):
            at = slice(g * self.BATCH, (g + 1) * self.BATCH)
            pool.wait_ge(self.s_veps, g + 1)
            self.nc.gpsimd.tensor_tensor(self.rstd[:, at], self.veps[:, at], self.half[:, :], ALU.pow)\
                .then_inc(self.s_rstd, 1)

    def vector(self, dve):
        nc, x, xT = self.nc, self.M["x"], self.M["xT"]

        def lo(t):
            dve.wait_ge(self.s_hi, t + 1)
            cols = slice(t * P, (t + 1) * P)
            nc.vector.tensor_tensor(xT[1][:, :, cols], self.psT[t % 4][:, 0:D].rearrange("p (k t) -> p k t", k=KD),
                                    xT[0][:, :, cols], ALU.subtract).then_inc(self.s_lo, 1)

        def shift(g):
            at = slice(g * self.BATCH, (g + 1) * self.BATCH)
            dve.wait_ge(self.s_rstd, g + 1)
            nc.vector.scalar_tensor_tensor(self.shift[:, at], self.mv[:, at, 0], -1.0, self.rstd[:, at], ALU.mult,
                                           ALU.mult).then_inc(self.s_shift, 1)

        if self.x_loaded:
            dve.wait_ge(*self.x_loaded)
        for g in range(NT // self.BATCH):
            tiles = range(g * self.BATCH, (g + 1) * self.BATCH)
            for t in tiles:
                nc.vector.bn_stats(out=self.stats[:, t, :], in_=x[:, t * D:(t + 1) * D]).then_inc(self.s_stat, 1)
            for t in tiles:
                dve.wait_ge(self.s_stat, t + 1)
                nc.vector.bn_aggr(out=self.mv[:, t, :], in_=self.stats[:, t, :]).then_inc(self.s_aggr, 1)
            dve.wait_ge(self.s_aggr, tiles[-1] + 1)
            nc.vector.tensor_scalar(self.veps[:, tiles[0]:tiles[-1] + 1], self.mv[:, tiles[0]:tiles[-1] + 1, 1], EPS, None,
                                    ALU.add).then_inc(self.s_veps, 1)
            if g:
                shift(g - 1)
        shift(NT // self.BATCH - 1)
        for t in range(NT):
            lo(t)

    def scalar(self, act):
        nc, x, xT = self.nc, self.M["x"], self.M["xT"]

        def normed(t):
            if t % self.BATCH == 0:
                act.wait_ge(self.s_shift, t // self.BATCH + 1)
            if t >= 4:
                act.wait_ge(self.s_tr, t - 3)
            nc.scalar.activation(self.xn[t % 4][:, :], x[:, t * D:(t + 1) * D], ACT.Identity,
                                 scale=self.rstd[:, t:t + 1], bias=self.shift[:, t:t + 1]).then_inc(self.s_xn, 1)

        def hi(t):
            act.wait_ge(self.s_tr, t + 1)
            nc.scalar.activation(xT[0][:, :, t * P:(t + 1) * P], self.psT[t % 4][:, 0:D].rearrange("p (k t) -> p k t", k=KD),
                                 ACT.Copy).then_inc(self.s_hi, 1)

        for t in range(NT + 2):
            if t < NT:
                normed(t)
            if t >= 2:
                hi(t - 2)

    def tensor(self, pe):
        for t in range(NT):
            pe.wait_ge(self.s_xn, t + 1)
            if t >= 4:
                pe.wait_ge(self.s_lo, t - 3)
            for k in range(KD):
                last = self.nc.tensor.transpose(self.psT[t % 4][:, k * P:(k + 1) * P], self.xn[t % 4][:, k * P:(k + 1) * P],
                                                self.M["ident"][:, :])
            last.then_inc(self.s_tr, 1)


class Route(Part):

    def __init__(self, nc, M, s, gate_dram, E, K, squash, route):
        self.nc, self.M, self.gate_dram, self.E, self.K, self.squash, self.route = nc, M, gate_dram, E, K, squash, route
        W = NT * E
        self.gw = s.sb("gate_w", [P, KD, E])
        self.gs = [s.sb(f"gate{q}", [P, KD, E], F32R) for q in ("hi", "lo")]
        self.p = s.sb("score", [P, W])
        self.e = s.sb("work", [P, W])
        self.e2 = s.sb("work2", [P, W])
        self.first = s.sb("not_first", [P, W])
        self.top = s.sb("top", [P, NT * 8])
        self.small = [s.sb(f"small{c}", [P, NT]) for c in range(3)]
        self.s_w, self.s_ghi, self.s_glo, self.s_first = s.sem("w"), s.sem("ghi"), s.sem("glo"), s.sem("first")
        self.s_log, self.s_act, self.s_dve, self.s_max = s.sem("logits"), s.sem("act"), s.sem("chain"), s.sem("max")
        self.s_sc, self.s_parts, self.s_tr, self.s_ev = s.sem("scored"), s.sem("parts"), s.sem("tr"), s.sem("ev")
        if squash == "sigmoid":
            self.parts = s.sb("parts", [P, NT, 3 * E], BF16)

    def take_psum(self, s):
        self.psL = s.ps("logits")
        if self.squash == "sigmoid":
            self.psR = s.ps("R", (P, 1024), BF16)

    def by_tile(self, a):
        return a[:, :].rearrange("p (t e) -> p t e", e=self.E)

    def over(self, a):
        return a[:, :].unsqueeze(2).to_broadcast([P, NT, self.E])

    def load(self, sp):
        sp.dma_start(self.gw[:, :, :], self.gate_dram.rearrange("(k p) e -> p k e", p=P)).then_inc(self.s_w, 16)

    def gpsimd(self, pool):
        nc = self.nc
        nc.gpsimd.memset(self.first[:, :], 1.0).then_inc(self.s_first, 1)
        pool.wait_ge(self.s_first, 1)
        nc.gpsimd.memset(self.by_tile(self.first)[:, :, 0], 0.0).then_inc(self.s_first, 1)

    def tensor(self, pe):
        nc, M, E, squash = self.nc, self.M, self.E, self.squash
        xT = M["xT"]
        pe.wait_ge(self.s_glo, 1)
        for t in range(NT):
            for k in range(KD):
                last = product(nc, self.psL[:, t * E:(t + 1) * E], [a[:, k, t * P:(t + 1) * P] for a in xT],
                               [a[:, k, :] for a in self.gs], k == 0, k == KD - 1)
        last.then_inc(self.s_log, 1)
        if squash == "sigmoid":
            pe.wait_ge(self.s_parts, 1)
            for t in range(NT):
                if t == 8:
                    pe.wait_ge(self.s_ev, 1)
                last = nc.tensor.transpose(self.psR[0:3 * E, t % 8 * P:(t % 8 + 1) * P], self.parts[:, t, :],
                                           M["ident16"][:, :])
                if t % 8 == 7:
                    last.then_inc(self.s_tr, 1)

    def scalar(self, act):
        nc, E, squash, route = self.nc, self.E, self.squash, self.route
        W = NT * E
        act.wait_ge(self.s_log, 1)
        if squash == "softcap":
            nc.scalar.activation(self.e[:, :], self.psL[:, 0:W], ACT.Tanh, scale=1.0 / 30.0).then_inc(self.s_act, 1)
            act.wait_ge(self.s_act, 1)
            nc.scalar.activation(self.p[:, :], self.e[:, :], ACT.Exp, scale=30.0).then_inc(self.s_sc, 1)
        else:
            nc.scalar.activation(self.p[:, :], self.psL[:, 0:W], ACT.Sigmoid).then_inc(self.s_sc, 1)
            for n in range(2):
                act.wait_ge(self.s_tr, n + 1)
                nc.scalar.activation(route[:, n * 1024:(n + 1) * 1024], self.psR[0:3 * E, :], ACT.Copy)\
                    .then_inc(self.s_ev, 1)

    def vector(self, dve):
        nc, E, K, squash, route = self.nc, self.E, self.K, self.squash, self.route
        n = [0]

        def chain(instruction):
            link(dve, self.s_dve, n, instruction)

        dve.wait_ge(self.s_w, 16)
        nc.vector.tensor_copy(self.gs[0][:, :, :], self.gw[:, :, :]).then_inc(self.s_ghi, 1)
        dve.wait_ge(self.s_ghi, 1)
        nc.vector.tensor_tensor(self.gs[1][:, :, :], self.gw[:, :, :], self.gs[0][:, :, :], ALU.subtract).then_inc(self.s_glo, 1)
        dve.wait_ge(self.s_sc, 1)
        dve.wait_ge(self.s_first, 2)
        if squash == "softcap":
            chain(nc.vector.tensor_reduce(self.small[0][:, :], self.by_tile(self.p), AX, ALU.add))
            chain(nc.vector.reciprocal(self.small[1][:, :], self.small[0][:, :]))
            chain(nc.vector.tensor_tensor(self.by_tile(self.p), self.by_tile(self.p), self.over(self.small[1]), ALU.mult))
        for t in range(NT):
            nc.vector.max(out=self.top[:, t * 8:(t + 1) * 8], in_=self.by_tile(self.p)[:, t, :]).then_inc(self.s_max, 1)
        dve.wait_ge(self.s_max, NT)
        kth = self.top[:, :].rearrange("p (t c) -> p t c", c=8)[:, :, K - 1:K].to_broadcast([P, NT, E])
        chain(nc.vector.tensor_tensor(self.by_tile(self.e), self.by_tile(self.p), kth, ALU.is_gt))
        chain(nc.vector.tensor_tensor(self.by_tile(self.e2), self.by_tile(self.p), kth, ALU.is_equal))
        chain(nc.vector.tensor_reduce(self.small[0][:, :], self.by_tile(self.e), AX, ALU.add))
        chain(nc.vector.tensor_scalar(self.small[1][:, :], self.small[0][:, :], -1.0, float(K), ALU.mult, ALU.add))
        chain(nc.vector.tensor_tensor_scan(self.first[:, :], self.first[:, :], self.e2[:, :], 0.0, ALU.mult, ALU.add))
        chain(nc.vector.tensor_tensor(self.by_tile(self.first), self.by_tile(self.first), self.over(self.small[1]), ALU.is_le))
        chain(nc.vector.tensor_tensor(self.e2[:, :], self.e2[:, :], self.first[:, :], ALU.mult))
        chain(nc.vector.tensor_tensor(self.e[:, :], self.e[:, :], self.e2[:, :], ALU.add))
        if squash == "softcap":
            chain(nc.vector.scalar_tensor_tensor(route[:, :], self.e[:, :], 0.5, self.p[:, :], ALU.mult, ALU.mult))
            return
        chain(nc.vector.tensor_tensor(self.e[:, :], self.e[:, :], self.p[:, :], ALU.mult))
        chain(nc.vector.tensor_reduce(self.small[0][:, :], self.by_tile(self.e), AX, ALU.add))
        chain(nc.vector.tensor_scalar(self.small[1][:, :], self.small[0][:, :], 1e-20, None, ALU.add))
        chain(nc.vector.reciprocal(self.small[2][:, :], self.small[1][:, :]))
        chain(nc.vector.tensor_tensor(self.by_tile(self.e), self.by_tile(self.e), self.over(self.small[2]), ALU.mult))
        chain(nc.vector.tensor_copy(self.parts[:, :, 0:E], self.by_tile(self.e)))
        chain(nc.vector.tensor_tensor(self.by_tile(self.e2), self.by_tile(self.e), self.parts[:, :, 0:E], ALU.subtract))
        chain(nc.vector.tensor_copy(self.parts[:, :, E:2 * E], self.by_tile(self.e2)))
        chain(nc.vector.tensor_tensor(self.by_tile(self.e), self.by_tile(self.e2), self.parts[:, :, E:2 * E], ALU.subtract))
        nc.vector.tensor_copy(self.parts[:, :, 2 * E:3 * E], self.by_tile(self.e)).then_inc(self.s_parts, 1)


class FFN(Part):

    def __init__(self, nc, M, s, tag, groups, NF, load, weight=None, lanes=None, loads=3):
        self.nc, self.M, self.groups, self.NF, self.load, self.weight, self.lanes = nc, M, groups, NF, load, weight, lanes
        self.NB = T // 512
        self.sizes = [min(P, NF - c) for c in range(0, NF, P)]
        self.NC = NC = len(self.sizes)
        self.two = two = 2 if groups > 1 else 1
        self.rounds = groups // two
        self.steps = [(slot, b, c) for slot in range(two) for b in range(self.NB) for c in range(NC)]
        self.N = len(self.steps)
        self.LOADED = loads * 16
        self.NW = len(self.full(0))

        def sb(name, shape, dt=F32):
            return s.sb(tag + name, shape, dt)

        self.raw = [[sb(f"raw_{w}{j}", [P, 2, NF]) for w in "gu"] + [sb(f"raw_d{j}", [P, NC, D])] for j in range(two)]
        self.wts = [[[sb(f"{w}_{q}{j}", [P, 2, NF], F32R) for q in ("hi", "lo")] for w in "gu"]
                    + [[sb(f"d_{q}{j}", [P, NC, D], F32R) for q in ("hi", "lo")]] for j in range(two)]
        self.sg = [sb(f"silu{j}", [P, 512]) for j in range(2)]
        self.hf = [sb(f"h{j}", [P, 512]) for j in range(2)]
        self.hr = [[sb(f"h_{q}{j}", [P, 512], F32R) for q in ("hi", "lo")] for j in range(2)]
        self.s_raw = [s.sem(f"{tag}raw{j}") for j in range(two)]
        (self.s_whi, self.s_wlo, self.s_g, self.s_u, self.s_silu) = (
            s.sem(tag + n) for n in ("w_hi", "w_lo", "g", "u", "silu"))
        (self.s_h, self.s_hhi, self.s_hlo, self.s_down, self.s_out, self.s_mul) = (
            s.sem(tag + n) for n in ("h", "h_hi", "h_lo", "down", "out", "mul"))

    def take_psum(self, s):
        self.psG = [s.ps(f"G{j}") for j in range(2)]
        self.psU = [s.ps(f"U{j}") for j in range(2)]
        self.psO = s.ps("O", (P, 1024))
        self.psC = [s.ps(f"C{j}") for j in range(2)] if self.lanes else None

    def full(self, slot):
        gu = [(n, (slice(0, P), slice(0, 2), slice(0, self.NF))) for n in range(2)]
        if self.sizes[-1] == P:
            return gu + [(2, (slice(0, P), slice(0, self.NC), slice(0, D)))]
        return gu + [(2, (slice(0, k), c, slice(0, D))) for c, k in enumerate(self.sizes)]

    def prepare(self, pool, i, j):
        nc, raw, wts = self.nc, self.raw, self.wts
        pool.wait_ge(self.s_raw[j], i * self.LOADED + self.LOADED)
        for n, at in self.full(j):
            hi = wts[j][n][0][at]
            zero = self.M["zero"][0:hi.shape[0], :]
            if len(hi.shape) == 3:
                zero = zero.unsqueeze(2)
            nc.gpsimd.tensor_tensor(hi, raw[j][n][at], zero.to_broadcast(hi.shape), ALU.add).then_inc(self.s_whi, 1)
        for m, (n, at) in enumerate(self.full(j)):
            pool.wait_ge(self.s_whi, i * (self.NW * self.two) + (self.NW * j + m + 1))
            nc.gpsimd.tensor_tensor(wts[j][n][1][at], raw[j][n][at], wts[j][n][0][at],
                                    ALU.subtract).then_inc(self.s_wlo, 1)

    def sync(self, sp):
        raw, NW, two, rounds, load = self.raw, self.NW, self.two, self.rounds, self.load
        if rounds > 1:
            with sp.Fori(0, rounds - 1) as i:
                for j in range(two):
                    sp.wait_ge(self.s_wlo, i * (NW * two) + NW * (j + 1))
                    load(sp, raw[j], i * two + (two + j), self.s_raw[j])

    def gpsimd(self, pool):
        for j in range(1, self.two):
            self.prepare(pool, 0, j)
        if self.rounds > 1:
            with pool.Fori(1, self.rounds) as i:
                for j in range(self.two):
                    pool.wait_ge(self.s_down, i * self.N + (j + 1) * self.N // self.two)
                    self.prepare(pool, i, j)

    def scalar(self, act):
        nc, sg, hf, hr, psG, N = self.nc, self.sg, self.hf, self.hr, self.psG, self.N
        two, rounds = self.two, self.rounds
        steps, sizes = self.steps, self.sizes
        act.sem_inc(self.s_silu, 2)
        act.sem_inc(self.s_hhi, 2)
        with act.Fori(0, rounds) as i:
            for n, (slot, b, c) in enumerate(steps):
                k, j = sizes[c], n % 2
                act.wait_ge(self.s_g, i * N + (n + 1))
                act.wait_ge(self.s_h, i * N + (n + 1))
                nc.scalar.activation(sg[j][0:k, :], psG[j][0:k, :], ACT.Silu).then_inc(self.s_silu, 1)
                act.wait_ge(self.s_h, i * N + (n + 3))
                act.wait_ge(self.s_down, i * N + (n + N - 1))
                nc.scalar.activation(hr[j][0][0:k, :], hf[j][0:k, :], ACT.Copy).then_inc(self.s_hhi, 1)

    def tensor(self, pe):
        nc, wts, hr, psG, psU, psO = self.nc, self.wts, self.hr, self.psG, self.psU, self.psO
        psC, NW = self.psC, self.NW
        NC, NB, N, two, rounds, steps = self.NC, self.NB, self.N, self.two, self.rounds, self.steps
        sizes, lanes = self.sizes, self.lanes
        NF = self.NF
        xT = self.M["xT"]

        def up(i, n):
            slot, b, c = steps[n]
            k, j = sizes[c], n % 2
            toks = slice(b * 512, (b + 1) * 512)
            if b == 0 and c == 0:
                pe.wait_ge(self.s_wlo, i * (NW * two) + NW * (slot + 1))
            pe.wait_ge(self.s_silu, i * N + (n + 1))
            for w, ps, done in ((0, psG[j], self.s_g), (1, psU[j], self.s_u)):
                if w == 1:
                    pe.wait_ge(self.s_h, i * N + (n + 1))
                    if lanes:
                        nc.tensor.matmul(psC[j][0:k, :],
                                         lanes[0][:, bass.ds(i * (two * NF) + (slot * NF + c * P), P)],
                                         lanes[1][:, toks], start=True, stop=True)
                for kk in range(KD):
                    last = product(nc, ps[0:k, :], [a[:, kk, c * P:c * P + k] for a in wts[slot][w]],
                                   [a[:, kk, toks] for a in xT], kk == 0, kk == KD - 1)
                last.then_inc(done, 1)

        def down(i, n):
            slot, b, c = steps[n]
            k, j = sizes[c], n % 2
            pe.wait_ge(self.s_hlo, i * N + (n + 1))
            if c == 0:
                pe.wait_ge(self.s_out, i * (two * NB) + (slot * NB + b + 1))
            for t in range(4):
                last = product(nc, psO[:, t * D:(t + 1) * D], [a[0:k, t * P:(t + 1) * P] for a in hr[j]],
                               [a[0:k, c, :] for a in wts[slot][2]], c == 0 and t % 2 == 0, c == NC - 1,
                               skip_group_check=True)
            last.then_inc(self.s_down, 1)

        pe.sem_inc(self.s_down, N)
        with pe.Fori(0, rounds) as i:
            up(i, 0)
            for n in range(N):
                if n + 1 < N:
                    up(i, n + 1)
                down(i, n)

    def vector(self, dve):
        nc, sg, hf, hr, psU, psO, psC, N = self.nc, self.sg, self.hf, self.hr, self.psU, self.psO, self.psC, self.N
        two, rounds, steps, sizes, groups, weight = self.two, self.rounds, self.steps, self.sizes, self.groups, self.weight
        lanes = self.lanes
        x = self.M["x"]

        def read_out(i, n):
            slot, b, c = steps[n]
            dve.wait_ge(self.s_down, i * N + (n + N + 1))
            if weight is None:
                cols = slice(b * 4 * D, (b + 1) * 4 * D)
                nc.vector.scalar_tensor_tensor(x[:, cols], psO[:, :], 0.5, x[:, cols], ALU.mult, ALU.add)\
                    .then_inc(self.s_out, 1)
                return
            for t in range(4):
                cols = slice((b * 4 + t) * D, (b * 4 + t + 1) * D)
                last = nc.vector.scalar_tensor_tensor(
                    x[:, cols], psO[:, t * D:(t + 1) * D],
                    weight[:, bass.ds(i * two + ((b * 4 + t) * groups + slot), 1)], x[:, cols], ALU.mult, ALU.add)
            last.then_inc(self.s_out, 1)

        dve.sem_inc(self.s_h, 2)
        dve.sem_inc(self.s_out, 1)
        with dve.Fori(0, rounds) as i:
            for n, (slot, b, c) in enumerate(steps):
                k, j = sizes[c], n % 2
                dve.wait_ge(self.s_u, i * N + (n + 1))
                dve.wait_ge(self.s_silu, i * N + (n + 3))
                dve.wait_ge(self.s_hhi, i * N + (n + 1))
                if lanes:
                    nc.vector.tensor_tensor(sg[j][0:k, :], psU[j][0:k, :], sg[j][0:k, :], ALU.mult)\
                        .then_inc(self.s_mul, 1)
                    dve.wait_ge(self.s_mul, i * N + (n + 1))
                    nc.vector.tensor_tensor(hf[j][0:k, :], psC[j][0:k, :], sg[j][0:k, :], ALU.mult)\
                        .then_inc(self.s_h, 1)
                else:
                    nc.vector.tensor_tensor(hf[j][0:k, :], psU[j][0:k, :], sg[j][0:k, :], ALU.mult)\
                        .then_inc(self.s_h, 1)
                dve.wait_ge(self.s_hhi, i * N + (n + 3))
                dve.wait_ge(self.s_down, i * N + (n + N - 1))
                nc.vector.tensor_tensor(hr[j][1][0:k, :], hf[j][0:k, :], hr[j][0][0:k, :], ALU.subtract)\
                    .then_inc(self.s_hlo, 1)
                if c == 0 and n:
                    read_out(i, n - 1)
            read_out(i, N - 1)


class FirstWeights(Part):

    def __init__(self, ffn):
        self.ffn = ffn

    def sync(self, sp):
        for j in range(self.ffn.two):
            self.ffn.load(sp, self.ffn.raw[j], j, self.ffn.s_raw[j])

    def gpsimd(self, pool):
        self.ffn.prepare(pool, 0, 0)


class OnSync(Part):

    def __init__(self, loads):
        self.sync = loads


def common(nc, ctx):
    def sb(name, shape, dt=F32):
        return ctx.enter_context(nc.sbuf_tensor(name, shape, dt))

    return {
        "x": sb("x", [P, NT * D]),
        "xT": [sb(f"xT_{q}", [P, KD, T], F32R) for q in ("hi", "lo")],
        "ident": sb("ident", [P, P]),
        "zero": sb("zero", [P, 1]),
        "ident16": sb("ident16", [P, P], BF16),
        "sel": sb("sel", [96, 32 * 96], BF16),
    }


def norm_block(nc, M, name):
    with Stage(nc, name) as s:
        run_block(nc, Norm(nc, M, s))


def stage_store(nc, M, out_dram):
    with Stage(nc, "store") as s:
        x_out = s.sem("x_out")
        block = s.block()

        @block.sync
        def _(sp):
            sp.dma_start(out_dram.rearrange("b (t p) d -> p (b t) d", p=P),
                         M["x"][:, :].rearrange("p (t d) -> p t d", d=D)).then_inc(x_out, 16)
            sp.wait_ge(x_out, 16)


def ffn0(nc, M, name, gate, w1, w3, w2, x_loaded=None):
    E = w1.shape[0]

    def load(sp, raw, g, sem):
        one = bass.ds(g, 1)
        sp.dma_start(raw[0][:, :, :], w1[one, :, :].rearrange("e (k p) f -> p (e k) f", p=P)).then_inc(sem, 16)
        sp.dma_start(raw[1][:, :, :], w3[one, :, :].rearrange("e (k p) f -> p (e k) f", p=P)).then_inc(sem, 16)
        sp.dma_start(raw[2][:, :, :], w2[one, :, :].rearrange("e (c p) d -> p (e c) d", p=P)).then_inc(sem, 16)

    with Stage(nc, name) as s:
        weight = s.sb("route", [P, NT * E])
        route = Route(nc, M, s, gate, E, 2, "softcap", weight)
        experts = FFN(nc, M, s, "e_", E, w1.shape[2], load, weight=weight)
        with Stage(nc, name + "n") as n:
            run_block(nc, Norm(nc, M, n, x_loaded), OnSync(route.load), FirstWeights(experts))
        with Stage(nc, name + "m") as m:
            route.take_psum(m)
            experts.take_psum(m)
            run_block(nc, route, experts)


def ffn1(nc, M, name, gate, wg, wu, wd, sg, su, sd):
    E, F = wg.shape[0], wg.shape[2]
    PER = 4

    def load(sp, raw, g, sem):
        for n, w in ((0, wg), (1, wu)):
            for k in range(KD):
                sp.dma_start(raw[n][:, k, :].rearrange("p (e f) -> p e f", e=PER),
                             w[bass.ds(g * PER, PER), k * P:(k + 1) * P, :].rearrange("e p f -> p e f"))\
                    .then_inc(sem, 16)
        sp.dma_start(raw[2][:, :, :], wd.rearrange("e f d -> (e f) d")[bass.ds(g * (PER * F), PER * F), :]
                     .rearrange("(c p) d -> p c d", p=P)).then_inc(sem, 16)

    def load_shared(sp, raw, g, sem):
        for n, w in ((0, sg), (1, su)):
            sp.dma_start(raw[n][:, :, :], w.rearrange("(k p) f -> p k f", p=P)).then_inc(sem, 16)
        sp.dma_start(raw[2][:, 0, :], sd[0:P, :]).then_inc(sem, 16)
        sp.dma_start(raw[2][0:sd.shape[0] - P, 1, :], sd[P:, :]).then_inc(sem, 16)

    with Stage(nc, name) as s:
        weight = s.sb("route", [3 * E, T], BF16)
        experts = FFN(nc, M, s, "e_", E // PER, PER * F, load, lanes=(M["sel"], weight), loads=5)
        with Stage(nc, name + "s") as s2:
            route = Route(nc, M, s2, gate, E, 6, "sigmoid", weight)
            shared = FFN(nc, M, s2, "s_", 1, sg.shape[1], load_shared, loads=4)
            with Stage(nc, name + "n") as n:
                run_block(nc, Norm(nc, M, n), OnSync(route.load), FirstWeights(shared))
            with Stage(nc, name + "m") as m:
                route.take_psum(m)
                shared.take_psum(m)
                run_block(nc, route, shared, FirstWeights(experts))
        with Stage(nc, name + "x") as m:
            experts.take_psum(m)
            run_block(nc, experts)


def attention(nc, M, name, w_qkv, w_proj, b_proj):
    HEADS, HD = 16, 16
    PAIRS = HEADS // 2
    TB = L // P
    xT, x, ident = M["xT"], M["x"], M["ident"]
    with Stage(nc, name) as keep:
        wq = [keep.sb(f"wq_{q}", [P, KD, HEADS, 4, HD], F32R) for q in ("hi", "lo")]
        wk = [keep.sb(f"wk_{q}", [P, KD, HEADS, 4, HD], F32R) for q in ("hi", "lo")]
        wv = [keep.sb(f"wv_{q}", [P, KD, HEADS, HD], F32R) for q in ("hi", "lo")]
        wp = [keep.sb(f"wp_{q}", [P, 4, D], F32R) for q in ("hi", "lo")]
        v_all = keep.sb("v_all", [P, NT, HEADS, HD])
        neg_q, neg_k, one_k = (keep.sb(n, [P, 1]) for n in ("neg_q", "neg_k", "one_k"))

        with Stage(nc, name + "w") as s:
            wn = s.sb("w_qkv", [P, 6, D])
            pn = s.sb("w_proj", [P, KD, D])
            pp = s.sb("w_proj_padded", [P, KD, 4, 4, 32])
            bias = s.sb("bias", [P, D])
            s_w, s_p, s_b, s_zero, s_pad = (s.sem(n) for n in ("w", "p", "b", "zero", "pad"))
            s_tw, s_tp, s_hi, s_lo, s_v, s_vout, s_mask, s_bias = (
                s.sem(n) for n in ("tw", "tp", "hi", "lo", "v", "v_out", "mask", "bias"))

            def loads(sp):
                sp.dma_start(wn[:, :, :], w_qkv.rearrange("(r p) n -> p r n", p=P)).then_inc(s_w, 16)
                sp.dma_start(pn[:, :, :], w_proj.rearrange("(r p) n -> p r n", p=P)).then_inc(s_p, 16)
                sp.dma_start(bias[:, :], b_proj.rearrange("(a n) -> a n", a=1).to_broadcast([P, D])).then_inc(s_b, 16)

            with Stage(nc, name + "n") as n:
                run_block(nc, Norm(nc, M, n), OnSync(loads))

            psW = [s.ps(f"W{k}", (P, 1024)) for k in range(KD)]
            psP = s.ps("Wp", (P, 1024))
            psV = [s.ps(f"V{j}") for j in range(2)]
            block = s.block()

            @block.gpsimd
            def _(pool):
                for w in wq + wk:
                    for k in range(KD):
                        last = nc.gpsimd.memset(w[:, k, :, 2, :].bitcast(F32), 0.0)
                last.then_inc(s_zero, 1)
                nc.gpsimd.memset(pp[:, :, :, :, :], 0.0).then_inc(s_pad, 1)
                pool.wait_ge(s_b, 16)
                x3 = x[:, :].rearrange("p (t d) -> p t d", d=D)
                nc.gpsimd.tensor_tensor(x3, x3, bias[:, :].unsqueeze(1).to_broadcast([P, NT, D]), ALU.add)\
                    .then_inc(s_bias, 1)

            @block.tensor
            def _(pe):
                pe.wait_ge(s_w, 16)
                for k in range(KD):
                    for r in range(6):
                        last = nc.tensor.transpose(psW[k][:, r * P:(r + 1) * P], wn[:, r, k * P:(k + 1) * P],
                                                   ident[:, :])
                    last.then_inc(s_tw, 1)
                pe.wait_ge(s_pad, 2)
                for m in range(4):
                    for r in range(KD):
                        last = nc.tensor.transpose(psP[:, m * D + r * P:m * D + (r + 1) * P],
                                                   pp[:, r, m, :, :].rearrange("p a b -> p (a b)"), ident[:, :])
                last.then_inc(s_tp, 1)
                pe.wait_ge(s_lo, KD)
                for t in range(NT):
                    if t >= 2:
                        pe.wait_ge(s_vout, t - 1)
                    for k in range(KD):
                        last = product(nc, psV[t % 2][:, 0:D], [a[:, k, t * P:(t + 1) * P] for a in xT],
                                       [a[:, k, :, :].rearrange("p h d -> p (h d)") for a in wv],
                                       k == 0, k == KD - 1)
                    last.then_inc(s_v, 1)

            def columns(k, c):
                return psW[k][:, 0:768].rearrange("p (q m c d) -> p q m c d", q=4, c=3, d=HD)[:, :, :, c, :]

            def blocks(w, k):
                return [w[:, k, :, a, :].rearrange("p (m q) d -> p q m d", m=4) for a in (0, 1, 3)]

            def values(w, k):
                return w[:, k, :, :].rearrange("p (q m) d -> p q m d", m=4)

            @block.scalar
            def _(act):
                for k in range(KD):
                    act.wait_ge(s_tw, k + 1)
                    nc.scalar.activation(values(wv[0], k), columns(k, 2), ACT.Copy)
                    for w, c in ((wq, 0), (wk, 1)):
                        for dst in blocks(w[0], k):
                            last = nc.scalar.activation(dst, columns(k, c), ACT.Copy)
                    last.then_inc(s_hi, 1)
                act.wait_ge(s_tp, 1)
                nc.scalar.activation(wp[0][:, :, :].rearrange("p m n -> p (m n)"), psP[:, :], ACT.Copy).then_inc(s_hi, 1)
                for t in range(NT):
                    act.wait_ge(s_v, t + 1)
                    nc.scalar.activation(v_all[:, t, :, :].rearrange("p h d -> p (h d)"), psV[t % 2][:, 0:D], ACT.Copy)\
                        .then_inc(s_vout, 1)

            @block.vector
            def _(dve):
                n = [0]
                ones = ident[:, :].rearrange("p (h r) -> p h r", h=2)
                XY = mybir.AxisListType.XY
                link(dve, s_mask, n, nc.vector.tensor_reduce(one_k[:, :], ones[:, :, 32:34], XY, ALU.add))
                link(dve, s_mask, n, nc.vector.tensor_reduce(neg_q[:, :], ones[:, :, 48:64], XY, ALU.add))
                link(dve, s_mask, n, nc.vector.tensor_reduce(neg_k[:, :], ones[:, :, 16:32], XY, ALU.add))
                link(dve, s_mask, n, nc.vector.tensor_scalar(neg_q[:, :], neg_q[:, :], -1.0, None, ALU.mult))
                link(dve, s_mask, n, nc.vector.tensor_tensor(neg_k[:, :], one_k[:, :], neg_k[:, :], ALU.subtract))
                dve.wait_ge(s_p, 16)
                dve.wait_ge(s_pad, 1)
                for r in range(KD):
                    last = nc.vector.tensor_copy(
                        pp[:, r, :, :, 0:HD], pn[:, r, :].rearrange("p (m h d) -> p m h d", m=4, h=4))
                last.then_inc(s_pad, 1)
                dve.wait_ge(s_zero, 1)
                for k in range(KD):
                    dve.wait_ge(s_hi, k + 1)
                    nc.vector.tensor_tensor(values(wv[1], k), columns(k, 2), values(wv[0], k), ALU.subtract)
                    for w, c in ((wq, 0), (wk, 1)):
                        for dst, hi in zip(blocks(w[1], k), blocks(w[0], k)):
                            last = nc.vector.tensor_tensor(dst, columns(k, c), hi, ALU.subtract)
                    last.then_inc(s_lo, 1)
                dve.wait_ge(s_hi, KD + 1)
                nc.vector.tensor_tensor(wp[1][:, :, :].rearrange("p m n -> p (m n)"), psP[:, :],
                                        wp[0][:, :, :].rearrange("p m n -> p (m n)"), ALU.subtract).then_inc(s_lo, 1)

        with Stage(nc, name + "m") as s:
            vb = s.sb("v_batch", [P, TB, HEADS, 48])
            qh = s.sb("q_hi", [P, 512], F32R)
            kh = s.sb("k_hi", [P, 512], F32R)
            qs = [s.sb(f"q_stack{j}", [P, 512], F32R) for j in range(2)]
            ks = [s.sb(f"k_stack{j}", [P, 512], F32R) for j in range(2)]
            q2 = s.sb("q_shifted", [P, 512], F32R)
            mx = s.sb("row_max", [P, 8])
            mh = s.sb("neg_max_hi", [P, 8], F32R)
            mc = s.sb("neg_max_columns", [P, TB, 2, 64])
            pT = [s.sb(f"probs{u}", [P, 512]) for u in range(8)]
            cu, su, cx = ([s.sb(f"{n}{j}", [P, 512]) for j in range(2)] for n in ("raw_ctx", "sums", "ctx"))
            rc = s.sb("recip", [P, 512])
            cr = [[s.sb(f"ctx_{q}{j}", [P, 512], F32R) for q in ("hi", "lo")] for j in range(2)]
            psQ, psK = s.ps("Q"), s.ps("K")
            psS = [s.ps(f"S{j}") for j in range(2)]
            psT = [s.ps(f"T{j}") for j in range(2)]
            psC = [s.ps(f"C{j}") for j in range(2)]
            (s_zero, s_vb, s_q, s_k, s_qh, s_kh, s_qs, s_ks, s_sc, s_mx, s_mc, s_mt, s_q2, s_st, s_exp, s_pv, s_cu, s_rc,
             s_ctx, s_chi, s_clo, s_o, s_x) = (s.sem(n) for n in (
                 "zero", "vb", "q", "k", "qh", "kh", "qs", "ks", "score", "max", "maxcols", "maxT", "q2", "scoreT",
                 "exp", "pv", "raw_ctx", "recip", "ctx", "ctx_hi", "ctx_lo", "o", "x"))
            s_chain, s_pool_passed = s.sem("chain"), s.sem("pool_passed")
            UN = 8
            NU = PAIRS * UN
            CHUNKS = HEADS // 4
            LAST = B - 1
            FIRST, ROUND = range(-3, 3), range(3, 3 + PAIRS)

            def there(b, pair):
                return pair >= 0 and (b is not LAST or pair < PAIRS)

            def chunk_at(b, n):
                return n % 2 == 0 and n >= 2 and there(b, n - 2)

            def whole(eng, step):
                for n in FIRST:
                    step(0, n)
                with eng.Fori(0, LAST) as b:
                    for n in ROUND:
                        step(b, n)
                for n in ROUND:
                    step(LAST, n)

            block = s.block()

            @block.gpsimd
            def _(pool):
                def fill(b, n):
                    v5 = v_all[:, bass.ds(b * TB, TB), :, :].rearrange("p t (q m) d -> p t q m d", m=4)
                    nc.gpsimd.tensor_tensor(
                        vb[:, :, 2 * n:2 * n + 2, 0:HD], v5[:, :, n % 2 * 2:n % 2 * 2 + 2, n // 2, :],
                        M["zero"][:, :].unsqueeze(2).unsqueeze(3).to_broadcast([P, TB, 2, HD]), ALU.add).then_inc(s_vb, 1)

                nc.gpsimd.memset(vb[:, :, :, 16:32], 0.0)
                nc.gpsimd.memset(vb[:, :, :, 32:48], 1.0)
                for j in range(2):
                    nc.gpsimd.memset(cu[j][:, :], 0.0)
                    nc.gpsimd.memset(su[j][:, :], 1.0)
                nc.gpsimd.memset(mc[:, :, :, :], 0.0).then_inc(s_zero, 1)
                for n in range(PAIRS):
                    fill(0, n)
                with pool.Fori(0, LAST) as b:
                    for n in range(PAIRS):
                        wait_apart(pool, s_pv, b * HEADS + (2 * n + 2), s_pool_passed)
                        fill(b + 1, n)

            @block.tensor
            def _(pe):
                def project(b, n):
                    toks = bass.ds(b * L + n // PAIRS * L, L)
                    for w, ps, done, used in ((wq, psQ, s_q, s_qs), (wk, psK, s_k, s_ks)):
                        pe.wait_ge(used, b * PAIRS + (n + 1))
                        at = n % PAIRS
                        for k in range(KD):
                            lhs = [a[:, k, 2 * at:2 * at + 2, :, :].rearrange("p h a d -> p (h a d)") for a in w]
                            last = product(nc, ps[:, :], lhs, [a[:, k, toks] for a in xT], k == 0, k == KD - 1)
                        last.then_inc(done, 1)

                def score(b, n, u):
                    h, t, j = u // 4, u % 4, n % 2
                    rows = slice(64 * h, 64 * h + 64)
                    if u == 0:
                        pe.wait_ge(s_qs, b * PAIRS + (n + 2))
                        pe.wait_ge(s_ks, b * PAIRS + (n + 2))
                        pe.wait_ge(s_q2, b * PAIRS + (n + 1))
                    if u == 1 and n - 2 in ROUND:
                        pe.wait_ge(s_x, b * PAIRS + (n - 4))
                    pe.wait_ge(s_mx, b * NU + (n * UN + u + 1))
                    nc.tensor.matmul(psS[u % 2][:, :], qs[j][rows, t * P:(t + 1) * P], ks[j][rows, :],
                                     start=True, stop=True).then_inc(s_sc, 1)

                def maxima(b, n):
                    pe.wait_ge(s_mc, b * PAIRS + (n + 1))
                    for t in range(TB):
                        last = nc.tensor.transpose(psS[0][:, t * P:(t + 1) * P],
                                                   mc[:, t, :, :].rearrange("p h c -> p (h c)"), ident[:, :])
                    last.then_inc(s_mt, 1)

                def scoreT(b, n, u):
                    h, t, j = u // 4, u % 4, n % 2
                    rows = slice(64 * h, 64 * h + 64)
                    if u == 0:
                        pe.wait_ge(s_q2, b * PAIRS + (n + 2))
                    pe.wait_ge(s_exp, b * NU + (n * UN + u + 1))
                    nc.tensor.matmul(psT[u % 2][:, :], ks[j][rows, t * P:(t + 1) * P], q2[rows, :],
                                     start=True, stop=True).then_inc(s_st, 1)

                def values(b, n, u):
                    h, t = u // 4, u % 4
                    if u == 0:
                        pe.wait_ge(s_vb, b * PAIRS + (n + 1))
                    pe.wait_ge(s_exp, b * NU + (n * UN + u + 3))
                    if t == 0:
                        pe.wait_ge(s_cu, b * HEADS + (2 * n + h + 1))
                    last = nc.tensor.matmul(psC[h][0:48, :], vb[:, t, n % PAIRS * 2 + h, :], pT[u][:, :],
                                            start=t == 0, stop=t == TB - 1)
                    if t == TB - 1:
                        last.then_inc(s_pv, 1)

                def output(b, n):
                    m, u = (n - 3) // 2, (n - 3) % 2
                    pe.wait_ge(s_clo, b * CHUNKS + (m + 1))
                    pe.wait_ge(s_x, b * PAIRS + (n - 2))
                    if there(b, n + 2):
                        pe.wait_ge(s_mx, b * NU + ((n + 3) * UN + 2))
                    for t in (2 * u, 2 * u + 1):
                        last = product(nc, psS[1][:, t % 2 * D:(t % 2 + 1) * D], [a[:, t * P:(t + 1) * P] for a in cr[m % 2]],
                                       [a[:, bass.ds(b, 1), :].rearrange("p a n -> p (a n)") for a in wp], True, True)
                    last.then_inc(s_o, 1)

                def step(b, n):
                    for u in range(UN):
                        if there(b, n):
                            values(b, n, u)
                        if there(b, n + 1):
                            scoreT(b, n + 1, u)
                        if there(b, n + 2):
                            score(b, n + 2, u)
                    if there(b, n + 3):
                        project(b, n + 3)
                    if there(b, n + 2):
                        maxima(b, n + 2)
                    if n in ROUND:
                        output(b, n)

                pe.sem_inc(s_o, 4)
                whole(pe, step)

            @block.scalar
            def _(act):
                def exp(b, n, u):
                    act.wait_ge(s_st, b * NU + (n * UN + u + 1))
                    nc.scalar.activation(pT[u][:, :], psT[u % 2][:, :], ACT.Exp, scale=HD ** -0.5).then_inc(s_exp, 1)

                def read(b, n, h):
                    m, q = n // 2, (2 * n + h) % 4
                    act.wait_ge(s_pv, b * HEADS + (2 * n + h + 1))
                    act.wait_ge(s_ctx, b * CHUNKS + (m + 1))
                    nc.scalar.activation(su[m % 2][32 * q:32 * q + HD, :], psC[h][32:48, :], ACT.Copy)
                    nc.scalar.activation(cu[m % 2][32 * q:32 * q + HD, :], psC[h][0:HD, :], ACT.Copy).then_inc(s_cu, 1)

                def parts(b, n):
                    act.wait_ge(s_q, b * PAIRS + (n + 1))
                    act.wait_ge(s_qs, b * PAIRS + (n + 1))
                    nc.scalar.activation(qh[:, :], psQ[:, :], ACT.Copy).then_inc(s_qh, 1)
                    act.wait_ge(s_k, b * PAIRS + (n + 1))
                    act.wait_ge(s_ks, b * PAIRS + (n + 1))
                    nc.scalar.activation(kh[:, :], psK[:, :], ACT.Identity, bias=one_k[:, 0:1]).then_inc(s_kh, 1)

                def context_hi(b, m):
                    act.wait_ge(s_ctx, b * CHUNKS + (m + 3))
                    act.wait_ge(s_o, b * PAIRS + (2 * m + 2))
                    nc.scalar.activation(cr[m % 2][0][:, :], cx[m % 2][:, :], ACT.Copy).then_inc(s_chi, 1)

                def step(b, n):
                    for u in range(UN):
                        if there(b, n + 1):
                            exp(b, n + 1, u)
                        if u == 5 and there(b, n):
                            read(b, n, 0)
                    if there(b, n + 3):
                        parts(b, n + 3)
                    if there(b, n):
                        read(b, n, 1)
                    if chunk_at(b, n):
                        context_hi(b, (n - 2) // 2)

                act.sem_inc(s_exp, 2)
                act.sem_inc(s_cu, 2)
                act.wait_ge(s_zero, 1)
                whole(act, step)

            @block.vector
            def _(dve):
                def row_max(b, n, u):
                    dve.wait_ge(s_sc, b * NU + (n * UN + u + 1))
                    nc.vector.tensor_reduce(mx[:, u:u + 1], psS[u % 2][:, :], AX, ALU.max).then_inc(s_mx, 1)

                def max_columns(b, n):
                    dve.wait_ge(s_mx, b * NU + (n * UN + UN + 2))
                    nc.vector.tensor_scalar(mh[:, :], mx[:, :], -1.0, None, ALU.mult).then_inc(s_chain, 1)
                    dve.wait_ge(s_chain, b * PAIRS + (n + 1))
                    cols = mc[:, :, :, :].rearrange("p t h c -> p h t c")
                    by_head = [a[:, :].rearrange("p (h t) -> p h t", h=2) for a in (mx, mh)]
                    nc.vector.tensor_copy(cols[:, :, :, 32], by_head[1])
                    nc.vector.scalar_tensor_tensor(cols[:, :, :, 33], by_head[0], -1.0, by_head[1],
                                                   ALU.mult, ALU.subtract).then_inc(s_mc, 1)

                def shift(b, n):
                    dve.wait_ge(s_mt, b * PAIRS + (n + 1))
                    nc.vector.tensor_tensor(q2[:, :], psS[0][:, :], qs[n % 2][:, :], ALU.add).then_inc(s_q2, 1)

                def stack(b, n):
                    for hi, ps, neg, out, made, done in ((qh, psQ, neg_q, qs, s_qh, s_qs), (kh, psK, neg_k, ks, s_kh, s_ks)):
                        dve.wait_ge(made, b * PAIRS + (n + 1))
                        nc.vector.scalar_tensor_tensor(out[n % 2][:, :], hi[:, :], neg[:, 0:1], ps[:, :],
                                                       ALU.mult, ALU.add).then_inc(done, 1)

                def normalize(b, m):
                    dve.wait_ge(s_cu, b * HEADS + (4 * m + 6))
                    nc.vector.reciprocal(rc[:, :], su[m % 2][:, :]).then_inc(s_rc, 1)
                    dve.wait_ge(s_rc, b * CHUNKS + (m + 1))
                    nc.vector.tensor_tensor(cx[m % 2][:, :], cu[m % 2][:, :], rc[:, :], ALU.mult).then_inc(s_ctx, 1)

                def context_lo(b, m):
                    dve.wait_ge(s_chi, b * CHUNKS + (m + 1))
                    nc.vector.tensor_tensor(cr[m % 2][1][:, :], cx[m % 2][:, :], cr[m % 2][0][:, :], ALU.subtract)\
                        .then_inc(s_clo, 1)

                def output(b, n):
                    m, u = (n - 3) // 2, (n - 3) % 2
                    dve.wait_ge(s_o, b * PAIRS + (n + 2))
                    cols = slice((m * TB + 2 * u) * D, (m * TB + 2 * u + 2) * D)
                    nc.vector.tensor_tensor(x[:, cols], psS[1][:, :], x[:, cols], ALU.add).then_inc(s_x, 1)

                def step(b, n):
                    for u in range(UN):
                        if there(b, n + 2):
                            row_max(b, n + 2, u)
                        if u == 3 and chunk_at(b, n):
                            normalize(b, (n - 2) // 2)
                        if u == 1 and chunk_at(b, n - 1):
                            context_lo(b, (n - 3) // 2)
                    if there(b, n + 2):
                        max_columns(b, n + 2)
                    if there(b, n + 3):
                        stack(b, n + 3)
                    if there(b, n + 2):
                        shift(b, n + 2)
                    if n in ROUND:
                        output(b, n)

                dve.wait_ge(s_zero, 1)
                dve.sem_inc(s_mx, 2)
                dve.sem_inc(s_ctx, 2)
                dve.sem_inc(s_q2, 1)
                dve.sem_inc(s_qs, 1)
                dve.sem_inc(s_ks, 1)
                dve.sem_inc(s_x, 1)
                whole(dve, step)


def mamba(nc, M, name, w_in, b_in, conv_w, conv_b, a_log, d_param, dt_bias, norm_w, w_out, b_out, mup):
    H, PD, G, S, KW = 32, 64, 8, 32, 4
    DS = H * PD
    GF = DS // G
    HG = H // G
    GK = GF // P
    OX, OB, OC, ODT = DS, 2 * DS, 2 * DS + G * S, 2 * DS + 2 * G * S
    W = NT * H
    x, xT, ident = M["x"], M["xT"], M["ident"]
    with Stage(nc, name) as keep:
        dt = keep.sb("dt", [P, NT, H])
        cp = keep.sb("decay_from_start", [P, NT, H])
        tot = keep.sb("decay_of_chunk", [S, NT, H])
        aT = keep.sb("decay_parts", [3 * H, T], BF16)
        sel = keep.sb("select_head", [3 * H, H * P], BF16)
        delta = keep.sb("delta", [P, HG * P])
        cwx, cbx, mux, bix = (keep.sb(n, [P, (G + 1) * GK] + e) for n, e in
                              (("conv_w_x", [KW]), ("conv_b_x", []), ("mup_x", []), ("bias_x", [])))
        cwb, cbb, mub, bib = (keep.sb(n, [2 * S, G + 1] + e) for n, e in
                              (("conv_w_bc", [KW]), ("conv_b_bc", []), ("mup_bc", []), ("bias_bc", [])))
        dsk = keep.sb("d_skip", [P, H])
        nw = keep.sb("norm_w", [P, (G + 1) * GK])

        def row(v, a, b):
            return v[a:b].rearrange("(o n) -> o n", o=1).to_broadcast([P, b - a])

        with Stage(nc, name + "d") as s:
            wd = s.sb("w_dt", [P, KD, H])
            wr = [s.sb(f"w_dt_{q}", [P, KD, H], F32R) for q in ("hi", "lo")]
            bi, mu, db, al, na = (s.sb(n, [P, H]) for n in ("bias", "mup", "dt_bias", "a_log", "neg_a"))
            bo = s.sb("b_out", [P, D])
            v, r, u, q, p, t2 = (s.sb(n, [P, NT, H]) for n in ("v", "relu", "u", "q", "poly", "square"))
            parts = s.sb("parts", [P, NT, 3 * H], BF16)
            start = s.sb("start", [H, NT, P])
            inner = s.sb("inner", [H, NT, P])
            cpT = s.sb("cpT", [H, T])
            last_row = s.sb("last_row", [P, S])
            psD = s.ps("D")
            psR = [s.ps(f"R{j}", (P, 1024), BF16) for j in range(2)]
            psT = s.ps("T", (H, T))
            s_small, s_w, s_par, s_pc = s.sem("small"), s.sem("w"), s.sem("par"), s.sem("par_chain")
            s_c, s_whi, s_wlo, s_d, s_na, s_ex, s_pool, s_parts = (
                s.sem(n) for n in ("chain", "whi", "wlo", "d", "neg_a", "exp", "pool", "parts"))
            s_tr, s_ev, s_aT, s_cp, s_cpt, s_cps, s_tot, s_xb = (
                s.sem(n) for n in ("tr", "ev", "aT", "cp", "cpT", "cps", "tot", "xb"))
            block = s.block()

            @block.sync
            def _(sp):
                sp.dma_start(wd[:, :, :], w_in[:, ODT:ODT + H].rearrange("(k p) n -> p k n", p=P)).then_inc(s_w, 16)
                for dst, v_ in ((bi, row(b_in, ODT, ODT + H)), (mu, row(mup, ODT, ODT + H)), (db, row(dt_bias, 0, H)),
                                (al, row(a_log, 0, H)), (dsk, row(d_param, 0, H)), (bo, row(b_out, 0, D))):
                    sp.dma_start(dst[:, :], v_).then_inc(s_small, 16)
                with nc.allow_non_contiguous_dma(reason="parameters of one word a partition"):
                    for src, off, dst in ((conv_b, 0, cbx), (mup, OX, mux), (b_in, OX, bix), (norm_w, 0, nw)):
                        sp.dma_start(dst[:, 0:G * GK], src[off:off + DS].rearrange("(c p) -> p c", p=P)).then_inc(s_par, 16)
                    for src, off, dst in ((conv_b, DS, cbb), (mup, OB, mub), (b_in, OB, bib)):
                        for h in range(2):
                            sp.dma_start(dst[h * S:(h + 1) * S, 0:G], src[off + h * G * S:off + (h + 1) * G * S]
                                         .rearrange("(g s) -> s g", s=S)).then_inc(s_par, 16)
                sp.dma_start(cwx[:, 0:G * GK, :], conv_w[0:DS, :].rearrange("(c p) k -> p c k", p=P)).then_inc(s_par, 16)
                for h in range(2):
                    sp.dma_start(cwb[h * S:(h + 1) * S, 0:G, :], conv_w[DS + h * G * S:DS + (h + 1) * G * S, :]
                                 .rearrange("(g s) k -> s g k", s=S)).then_inc(s_par, 16)

            @block.gpsimd
            def _(pool):
                n = [0]
                link(pool, s_pool, n, nc.gpsimd.memset(sel[:, :], 1.0))
                for c in range(3):
                    rows = sel[32 * c:32 * c + 32, :].rearrange("r (e f) -> r e f", e=H)
                    link(pool, s_pool, n, nc.gpsimd.affine_select(
                        out=rows, in_=rows, compare_op=ALU.is_equal, fill=0.0, base=0,
                        pattern=[[-1, H], [0, P]], channel_multiplier=1))
                link(pool, s_pool, n, nc.gpsimd.memset(last_row[:, :], 1.0))
                link(pool, s_pool, n, nc.gpsimd.affine_select(
                    out=last_row[:, :], in_=last_row[:, :], compare_op=ALU.is_equal, fill=0.0, base=-(P - 1),
                    pattern=[[0, S]], channel_multiplier=1))
                for h in range(HG):
                    nc.gpsimd.tensor_copy(delta[:, h * P:(h + 1) * P], ident[:, :])
                link(pool, s_pool, n, nc.gpsimd.memset(start[:, :, :], 0.0))
                pool.wait_ge(s_small, 6 * 16)
                x3 = x[:, :].rearrange("p (t d) -> p t d", d=D)
                nc.gpsimd.tensor_tensor(x3, x3, bo[:, :].unsqueeze(1).to_broadcast([P, NT, D]), ALU.add)\
                    .then_inc(s_xb, 1)
                pool.wait_ge(s_par, 13 * 16)
                for a, w in ((cwx, GK), (cbx, GK), (mux, GK), (bix, GK), (nw, GK), (cwb, 1), (cbb, 1), (mub, 1), (bib, 1)):
                    last = nc.gpsimd.tensor_copy(a[:, G * w:(G + 1) * w], a[:, 0:w])
                last.then_inc(s_pc, 1)
                pool.wait_ge(s_pc, 1)
                nc.gpsimd.tensor_tensor(bix[:, :], bix[:, :], mux[:, :], ALU.mult).then_inc(s_pc, 1)
                nc.gpsimd.tensor_tensor(bib[:, :], bib[:, :], mub[:, :], ALU.mult).then_inc(s_pc, 1)

            @block.tensor
            def _(pe):
                pe.wait_ge(s_wlo, 1)
                for t in range(NT):
                    for k in range(KD):
                        last = product(nc, psD[:, t * H:(t + 1) * H], [a[:, k, t * P:(t + 1) * P] for a in xT],
                                       [a[:, k, :] for a in wr], k == 0, k == KD - 1)
                last.then_inc(s_d, 1)
                pe.wait_ge(s_ex, 2)
                for t in range(NT):
                    last = nc.tensor.transpose(psT[:, t * P:(t + 1) * P], v[:, t, :], ident[:, :])
                last.then_inc(s_aT, 1)
                pe.wait_ge(s_parts, 1)
                for t in range(NT):
                    last = nc.tensor.transpose(psR[t // 8][0:3 * H, t % 8 * P:(t % 8 + 1) * P], parts[:, t, :],
                                               M["ident16"][:, :])
                    if t % 8 == 7:
                        last.then_inc(s_tr, 1)
                pe.wait_ge(s_cp, 1)
                for t in range(NT):
                    last = nc.tensor.transpose(psD[:, t * H:(t + 1) * H], cpT[:, t * P:(t + 1) * P], ident[0:H, 0:H])
                last.then_inc(s_cpt, 1)
                pe.wait_ge(s_cps, 1)
                nc.tensor.matmul(psT[:, 0:W], last_row[:, :], cp[:, :, :].rearrange("p t h -> p (t h)"),
                                 start=True, stop=True).then_inc(s_tot, 1)

            @block.scalar
            def _(act):
                act.wait_ge(s_na, 1)
                nc.scalar.activation(na[:, :], al[:, :], ACT.Exp).then_inc(s_na, 1)
                act.wait_ge(s_c, 5)
                nc.scalar.activation(u[:, :, :], q[:, :, :], ACT.Exp).then_inc(s_ex, 1)
                act.wait_ge(s_na, 4)
                nc.scalar.activation(v[:, :, :], q[:, :, :], ACT.Exp).then_inc(s_ex, 1)
                for j in range(2):
                    act.wait_ge(s_tr, j + 1)
                    nc.scalar.activation(aT[:, j * 1024:(j + 1) * 1024], psR[j][0:3 * H, :], ACT.Copy).then_inc(s_ev, 1)

            @block.vector
            def _(dve):
                n = [0]

                def chain(instruction):
                    link(dve, s_c, n, instruction)

                def each(a):
                    return a[:, :].unsqueeze(1).to_broadcast([P, NT, H])

                dve.wait_ge(s_w, 16)
                nc.vector.tensor_copy(wr[0][:, :, :], wd[:, :, :]).then_inc(s_whi, 1)
                dve.wait_ge(s_whi, 1)
                nc.vector.tensor_tensor(wr[1][:, :, :], wd[:, :, :], wr[0][:, :, :], ALU.subtract).then_inc(s_wlo, 1)
                dve.wait_ge(s_small, 6 * 16)
                nc.vector.tensor_scalar(al[:, :], al[:, :], 80.0, None, ALU.min).then_inc(s_na, 1)
                dve.wait_ge(s_d, 1)
                ps3 = psD[:, :].rearrange("p (t h) -> p t h", h=H)
                chain(nc.vector.tensor_tensor(v[:, :, :], ps3, each(bi), ALU.add))
                chain(nc.vector.tensor_tensor(v[:, :, :], v[:, :, :], each(mu), ALU.mult))
                chain(nc.vector.tensor_tensor(v[:, :, :], v[:, :, :], each(db), ALU.add))
                chain(nc.vector.tensor_scalar(r[:, :, :], v[:, :, :], 0.0, None, ALU.max))
                chain(nc.vector.scalar_tensor_tensor(q[:, :, :], v[:, :, :], -1.0, v[:, :, :], ALU.mult, ALU.min))
                dve.wait_ge(s_ex, 1)
                chain(nc.vector.tensor_scalar(q[:, :, :], u[:, :, :], 2.0, None, ALU.add))
                chain(nc.vector.reciprocal(p[:, :, :], q[:, :, :]))
                chain(nc.vector.tensor_tensor(u[:, :, :], u[:, :, :], p[:, :, :], ALU.mult))
                chain(nc.vector.tensor_tensor(t2[:, :, :], u[:, :, :], u[:, :, :], ALU.mult))
                chain(nc.vector.tensor_scalar(p[:, :, :], t2[:, :, :], 1.0 / 15, None, ALU.mult))
                for d in (13, 11, 9, 7, 5, 3):
                    chain(nc.vector.scalar_tensor_tensor(p[:, :, :], p[:, :, :], 1.0 / d, t2[:, :, :], ALU.add, ALU.mult))
                chain(nc.vector.scalar_tensor_tensor(p[:, :, :], p[:, :, :], 1.0, u[:, :, :], ALU.add, ALU.mult))
                chain(nc.vector.scalar_tensor_tensor(dt[:, :, :], p[:, :, :], 2.0, r[:, :, :], ALU.mult, ALU.add))
                dve.wait_ge(s_na, 2)
                nc.vector.tensor_scalar(na[:, :], na[:, :], -1.0, None, ALU.mult).then_inc(s_na, 1)
                dve.wait_ge(s_na, 3)
                nc.vector.tensor_tensor(q[:, :, :], dt[:, :, :], each(na), ALU.mult).then_inc(s_na, 1)
                dve.wait_ge(s_ex, 2)
                chain(nc.vector.tensor_copy(parts[:, :, 0:H], v[:, :, :]))
                chain(nc.vector.tensor_tensor(p[:, :, :], v[:, :, :], parts[:, :, 0:H], ALU.subtract))
                chain(nc.vector.tensor_copy(parts[:, :, H:2 * H], p[:, :, :]))
                chain(nc.vector.tensor_tensor(u[:, :, :], p[:, :, :], parts[:, :, H:2 * H], ALU.subtract))
                nc.vector.tensor_copy(parts[:, :, 2 * H:3 * H], u[:, :, :]).then_inc(s_parts, 1)
                dve.wait_ge(s_aT, 1)
                dve.wait_ge(s_pool, 7)
                aT3 = psT[:, :].rearrange("h (t p) -> h t p", p=P)
                chain(nc.vector.tensor_copy(start[:, :, 0:1], aT3[:, :, 0:1]))
                chain(nc.vector.tensor_copy(inner[:, :, :], aT3))
                chain(nc.vector.memset(inner[:, :, 0:1], 0.0))
                nc.vector.tensor_tensor_scan(cpT[:, :], inner[:, :, :].rearrange("h t p -> h (t p)"),
                                             start[:, :, :].rearrange("h t p -> h (t p)"), 0.0, ALU.mult, ALU.add)\
                    .then_inc(s_cp, 1)
                dve.wait_ge(s_cpt, 1)
                nc.vector.tensor_copy(cp[:, :, :], ps3).then_inc(s_cps, 1)
                dve.wait_ge(s_ev, 2)
                nc.vector.memset(aT[:, :].rearrange("h (t p) -> h t p", p=P)[:, :, 0:1], 0.0)
                dve.wait_ge(s_tot, 1)
                nc.vector.tensor_copy(tot[:, :, :], psT[:, 0:W].rearrange("p (t h) -> p t h", h=H))

        with Stage(nc, name + "m") as s:
            raw_z, raw_x = (s.sb(n, [P, KD, GF]) for n in ("raw_z", "raw_x"))
            raw_bc = s.sb("raw_bc", [P, KD, 2 * S])
            raw_o = s.sb("raw_o", [P, GK, D])
            mup_z = s.sb("mup_z", [P, GF])
            bias_z = s.sb("bias_z", [1, GF])
            wz, wx, wb, wo, bz = ([[s.sb(f"{n}_{q}{j}", shape, F32R) for q in ("hi", "lo")] for j in range(2)]
                                  for n, shape in (("w_z", [P, KD, GF]), ("w_x", [P, KD, GF]), ("w_bc", [P, KD, 2 * S]),
                                                   ("w_o", [P, GK, D]), ("bias_z", [1, GF])))
            ones = s.sb("ones", [1, P], F32R)
            t0w, t0b = s.sb("tap_scale_x", [P, (G + 1) * GK]), s.sb("tap_bias_x", [P, (G + 1) * GK])
            t0wb, t0bb = s.sb("tap_scale_bc", [2 * S, G + 1]), s.sb("tap_bias_bc", [2 * S, G + 1])
            xr = [s.sb(f"padded{j}", [P, KW - 1 + L]) for j in range(2)]
            acc = [s.sb(f"conv{j}", [P, L]) for j in range(2)]
            feat = [[s.sb(f"x{k}_{j}", [P, L]) for k in range(GK)] for j in range(2)]
            bT, cT = ([s.sb(f"{n}T{j}", [S, L]) for j in range(2)] for n in "bc")
            lt = [s.sb(f"decay{j}", [P, HG, P]) for j in range(2)]
            cb = [s.sb(f"cb{j}", [P, P]) for j in range(2)]
            mt = [s.sb(f"mix{j}", [P, HG, P]) for j in range(2)]
            xs, xdt, xde, xd, ys, yo, yd, yg = ([s.sb(f"{n}{j}", [P, HG, PD]) for j in range(2)] for n in
                                                ("x_tok", "xdt", "xdt_decayed", "x_skip", "y", "y_off", "y_sum", "y_gated"))
            zs = [s.sb(f"z{j}", [P, GF]) for j in range(4)]
            bt = [s.sb(f"b_tok{j}", [P, S]) for j in range(2)]
            state = s.sb("state", [S, HG, PD])
            yt = [[s.sb(f"yT_{q}{j}", [P, GK, P], F32R) for q in ("hi", "lo")] for j in range(2)]
            sq = s.sb("squares", [P, GF])
            ssq, rstd = ([s.sb(f"{n}{j}", [P, 1]) for j in range(2)] for n in ("mean_square", "rstd"))
            psP, psA, psX, psZ, psY, psS, psT, psO = (s.ps(n) for n in
                                                      ("ps_proj", "ps_decay", "ps_x", "ps_cbz", "ps_y", "ps_state", "ps_yT", "ps_out"))
            (s_raw, s_prep, s_w, s_tap, s_pad, s_pr, s_xr, s_t0, s_cc, s_cv, s_ft) = (s.sem(n) for n in (
                "raw", "prep", "weights", "tap", "pad", "proj", "xr", "tap0", "conv_chain", "conv", "feat"))
            (s_a, s_z, s_xt, s_zs, s_xs, s_scan, s_xdt, s_mt, s_xe, s_y, s_st, s_yo, s_ys, s_sc, s_S) = (
                s.sem(n) for n in ("a", "z", "xt", "zs", "xs", "scan", "xdt", "mt", "xe", "y", "st", "yo", "ys",
                                   "state_chain", "state"))
            (s_yd, s_yg, s_yt, s_hi, s_sq, s_lo, s_rs, s_o, s_x) = (
                s.sem(n) for n in ("yd", "yg", "yt", "hi", "sq", "lo", "rs", "o", "x"))
            eps_c, half_c = s.sb("eps", [P, 1]), s.sb("minus_half", [P, 1])
            s_eps = s.sem("eps")
            s_act_passed, s_pool_passed = s.sem("act_passed"), s.sem("pool_passed")
            NB, NC = B, L // P
            N = 2 * NB * NC
            UNITS = 3
            NU = 2 * NB * UNITS
            NS = 2 * NB * (NC - 1)
            ROUNDS = G // 2
            LOADS = 7
            steps = [(slot, b, c) for slot in range(2) for b in range(NB) for c in range(NC)]
            tile = lambda n: steps[n][1] * NC + steps[n][2]
            st_at = lambda n: n // NC * (NC - 1) + n % NC
            block = s.block()

            def preparations(slot, g, first=False):
                pool = nc.gpsimd
                z = M["zero"]

                def hi(dst, src):
                    n = dst.shape
                    zero = z[0:n[0], :]
                    zero = (zero.unsqueeze(2) if len(n) == 3 else zero).to_broadcast(n)
                    return lambda: pool.tensor_tensor(dst, src, zero, ALU.add)

                def lo(dst, src, hi_):
                    return lambda: pool.tensor_tensor(dst, src, hi_, ALU.subtract)

                out = [lambda: pool.tensor_tensor(raw_z[:, :, :], raw_z[:, :, :],
                                                  mup_z[:, :].unsqueeze(1).to_broadcast([P, KD, GF]), ALU.mult),
                       lambda: pool.tensor_tensor(bias_z[:, :], bias_z[:, :], mup_z[0:1, :], ALU.mult),
                       lambda: pool.tensor_tensor(raw_o[:, :, :], raw_o[:, :, :],
                                                  nw[:, bass.ds(g * GK, GK)].unsqueeze(2).to_broadcast([P, GK, D]),
                                                  ALU.mult)]
                tensors = [(w[slot], r) for w, r in ((wz, raw_z), (wx, raw_x), (wb, raw_bc), (wo, raw_o))]
                out += [hi(w[0][:, :, :], r[:, :, :]) for w, r in tensors] + [hi(bz[slot][0][:, :], bias_z[:, :])]
                out += [lo(w[1][:, :, :], r[:, :, :], w[0][:, :, :]) for w, r in tensors]
                out += [lo(bz[slot][1][:, :], bias_z[:, :], bz[slot][0][:, :])]
                return out

            PREP = 13
            CARRY = {n + 1: (1, 2 * n, min(2 * n + 2, PREP)) for n in range(7)}
            CARRY.update({n + 20: (0, 2 * n, min(2 * n + 2, PREP)) for n in range(7)})

            @block.sync
            def _(sp):
                def load(g):
                    def cols(off, n):
                        return w_in[:, bass.ds(g * n + off, n)].rearrange("(k p) n -> p k n", p=P)

                    sp.dma_start(raw_z[:, :, :], cols(0, GF)).then_inc(s_raw, 16)
                    sp.dma_start(raw_x[:, :, :], cols(OX, GF)).then_inc(s_raw, 16)
                    sp.dma_start(raw_bc[:, :, 0:S], cols(OB, S)).then_inc(s_raw, 16)
                    sp.dma_start(raw_bc[:, :, S:2 * S], cols(OC, S)).then_inc(s_raw, 16)
                    sp.dma_start(raw_o[:, :, :], w_out[bass.ds(g * GF, GF), :].rearrange("(k p) n -> p k n", p=P))\
                        .then_inc(s_raw, 16)
                    one = bass.ds(g * GF, GF)
                    sp.dma_start(mup_z[:, :], mup[one].rearrange("(o n) -> o n", o=1).to_broadcast([P, GF]))\
                        .then_inc(s_raw, 16)
                    sp.dma_start(bias_z[:, :], b_in[one].rearrange("(o n) -> o n", o=1)).then_inc(s_raw, 16)

                load(0)
                with sp.Fori(0, ROUNDS - 1) as it:
                    for h in range(2):
                        sp.wait_ge(s_w, it * 2 + (h + 1))
                        load(it * 2 + (h + 1))
                sp.wait_ge(s_w, ROUNDS * 2 - 1)
                load(G - 1)
                sp.wait_ge(s_w, ROUNDS * 2)
                load(0)

            def prep(pool, slot, g, a, b, base, count):
                ops = preparations(slot, g)
                for n in range(a, b):
                    if n == 0:
                        pool.wait_ge(s_raw, count * (LOADS * 16) + LOADS * 16)
                    if n in (3, 8):
                        pool.wait_ge(s_prep, base + n)
                    if n == 2:
                        wait_apart(pool, s_prep, base + 2, s_pool_passed)
                    last = ops[n]()
                    last.then_inc(s_prep, 1)
                if b == PREP:
                    pool.wait_ge(s_prep, base + PREP)
                    pool.sem_inc(s_w, 1)

            @block.gpsimd
            def _(pool):
                pool.sem_inc(s_xe, 2)
                nc.gpsimd.memset(eps_c[:, :], EPS)
                nc.gpsimd.memset(half_c[:, :], -0.5)
                for j in range(2):
                    nc.gpsimd.memset(xr[j][:, 0:KW - 1], 0.0)
                nc.gpsimd.memset(ones[:, :].bitcast(F32), 1.0).then_inc(s_pad, 1)
                n = [0]
                for w, m, bi_, cb_, tw, tb in ((cwx, mux, bix, cbx, t0w, t0b), (cwb, mub, bib, cbb, t0wb, t0bb)):
                    nc.gpsimd.tensor_tensor(tw[:, :], w[:, :, KW - 1], m[:, :], ALU.mult)
                    link(pool, s_tap, n, nc.gpsimd.tensor_tensor(tb[:, :], w[:, :, KW - 1], bi_[:, :], ALU.mult))
                    link(pool, s_tap, n, nc.gpsimd.tensor_tensor(tb[:, :], tb[:, :], cb_[:, :], ALU.add))
                prep(pool, 0, 0, 0, PREP, 0, 0)
                with pool.Fori(0, ROUNDS) as it:
                    for n in range(N + 2):
                        if n < N:
                            slot, b, c = steps[n]
                            j = n % 2
                            wait_apart(pool, s_xs, it * N + (n + 2), s_pool_passed)
                            heads = bass.ds(it * (2 * HG) + slot * HG, HG)
                            nc.gpsimd.tensor_tensor(xd[j][:, :, :], xs[j][:, :, :],
                                                    dsk[:, heads].unsqueeze(2).to_broadcast([P, HG, PD]), ALU.mult)
                            pool.wait_ge(s_scan, it * N + (n + 2))
                            pool.wait_ge(s_zs, it * N + (n + 2))
                            nc.gpsimd.tensor_tensor(mt[j][:, :, :], lt[j][:, :, :],
                                                    cb[j][:, :].unsqueeze(1).to_broadcast([P, HG, P]), ALU.mult)\
                                .then_inc(s_mt, 1)
                            pool.wait_ge(s_xdt, it * N + (n + 2))
                            nc.gpsimd.tensor_tensor(xde[j][:, :, :], xdt[j][:, :, :],
                                                    lt[j][:, :, P - 1:P].to_broadcast([P, HG, PD]), ALU.mult)\
                                .then_inc(s_xe, 1)
                        if 1 <= n <= N:
                            p = n - 1
                            pool.wait_ge(s_ys, it * N + (p + 2))
                            pool.wait_ge(s_xe, it * N + (p + 3))
                            nc.gpsimd.tensor_tensor(yd[p % 2][:, :, :], ys[p % 2][:, :, :], xd[p % 2][:, :, :], ALU.add)\
                                .then_inc(s_yd, 1)
                        if n >= 2:
                            p = n - 2
                            pool.wait_ge(s_sq, it * N + (p + 1))
                            nc.gpsimd.tensor_tensor(ssq[p % 2][:, :], ssq[p % 2][:, :], eps_c[:, :], ALU.add)\
                                .then_inc(s_eps, 1)
                            pool.wait_ge(s_eps, it * N + (p + 1))
                            nc.gpsimd.tensor_tensor(rstd[p % 2][:, :], ssq[p % 2][:, :], half_c[:, :], ALU.pow)\
                                .then_inc(s_rs, 1)
                        if n in CARRY:
                            slot, a, e = CARRY[n]
                            if a == 0:
                                pool.wait_ge(s_o, it * N + (1 if slot else N // 2 + 1))
                            k = 1 if slot else 2
                            prep(pool, slot, it * 2 + 1 if slot else it * 2 + 2, a, e,
                                 it * (2 * PREP) + k * PREP, it * 2 + k)

            def unit_at(it, mm, c):
                return it * NU + (mm * UNITS + c)

            def cols_at(it, mm, c):
                return it * (2 * GK) + (mm // NB * GK + c)

            @block.tensor
            def _(pe):
                def project(it, mm, c, first=False):
                    slot, b = mm // NB % 2, mm % NB
                    if b == 0 and c == 0:
                        pe.wait_ge(s_w, it * 2 + (mm // NB + 1))
                    if not first:
                        pe.wait_ge(s_t0, unit_at(it, mm, c))
                    w = wb if c == 2 else wx
                    k0, m = (0, 2 * S) if c == 2 else (c * P, P)
                    for k in range(KD):
                        last = product(nc, psP[0:m, :], [a[:, k, k0:k0 + m] for a in w[slot]],
                                       [a[:, k, b * L:(b + 1) * L] for a in xT], k == 0, k == KD - 1)
                    last.then_inc(s_pr, 1)

                pe.sem_inc(s_o, 1)
                for c in range(UNITS):
                    project(0, 0, c, first=c == 0)
                with pe.Fori(0, ROUNDS) as it:
                    for n in range(N + 3):
                        if n < N:
                            slot, b, c = steps[n]
                            mm, tt = n // NC, tile(n)
                            if c < UNITS:
                                project(it, mm + 1, c)
                            if c == 0:
                                pe.wait_ge(s_ft, unit_at(it, mm + 1, 0))
                            chunk = slice(c * P, (c + 1) * P)
                            pe.wait_ge(s_scan, it * N + (n + 1))
                            for h in range(HG):
                                last = nc.tensor.matmul(psA[:, h * P:(h + 1) * P],
                                                        sel[:, bass.ds(it * (2 * HG * P) + (slot * HG + h) * P, P)],
                                                        aT[:, tt * P:(tt + 1) * P], start=True, stop=True)
                            last.then_inc(s_a, 1)
                            pe.wait_ge(s_zs, it * N + (n + 1))
                            nc.tensor.matmul(psZ[:, 0:P], bT[mm % 2][:, chunk], cT[mm % 2][:, chunk], start=True, stop=True)
                            for k in range(KD):
                                product(nc, psZ[:, P:P + GF], [a[:, k, tt * P:(tt + 1) * P] for a in xT],
                                        [a[:, k, :] for a in wz[slot]], k == 0, False)
                            nc.tensor.matmul(psZ[:, P:P + GF], ones[:, :], bz[slot][0][:, :], start=False, stop=False)
                            nc.tensor.matmul(psZ[:, P:P + GF], ones[:, :], bz[slot][1][:, :], start=False, stop=True)\
                                .then_inc(s_z, 1)
                            pe.wait_ge(s_xs, it * N + (n + 1))
                            pe.wait_ge(s_xdt, it * N + (n + 1))
                            for k in range(GK):
                                nc.tensor.transpose(psX[:, k * P:(k + 1) * P], feat[mm % 2][k][:, chunk], ident[:, :])
                            nc.tensor.transpose(psX[:, GF:GF + S], bT[mm % 2][:, chunk], ident[0:S, 0:S]).then_inc(s_xt, 1)
                        if 1 <= n <= N:
                            p = n - 1
                            slot, b, c = steps[p]
                            mm, j = p // NC, p % 2
                            pe.wait_ge(s_mt, it * N + (p + 1))
                            pe.wait_ge(s_ys, it * N + (p + 1))
                            if c > 0:
                                pe.wait_ge(s_S, it * NS + (st_at(p - 1) + 2))
                                nc.tensor.matmul(psY[:, GF:2 * GF], cT[mm % 2][:, c * P:(c + 1) * P],
                                                 state[:, :, :].rearrange("s h d -> s (h d)"), start=True, stop=True)
                            for h in range(HG):
                                last = nc.tensor.matmul(psY[:, h * PD:(h + 1) * PD], mt[j][:, h, :], xdt[j][:, h, :],
                                                        start=True, stop=True)
                            last.then_inc(s_y, 1)
                            if c < NC - 1:
                                pe.wait_ge(s_xe, it * N + (p + 3))
                                pe.wait_ge(s_S, it * NS + (st_at(p) + 1))
                                nc.tensor.matmul(psS[0:S, 0:GF], bt[j][:, :], xde[j][:, :, :].rearrange("p h d -> p (h d)"),
                                                 start=True, stop=True).then_inc(s_st, 1)
                        if n >= 3:
                            p = n - 3
                            pe.wait_ge(s_lo, it * N + (p + 2))
                            pe.wait_ge(s_x, it * N + (p + 1))
                            for k in range(GK):
                                last = product(nc, psO[:, 0:D], [a[:, k, :] for a in yt[p % 2]],
                                               [a[:, k, :] for a in wo[steps[p][0]]], k == 0, k == GK - 1)
                            last.then_inc(s_o, 1)
                        if 2 <= n < N + 2:
                            p = n - 2
                            pe.wait_ge(s_yg, it * N + (p + 1))
                            pe.wait_ge(s_lo, it * N + (p + 1))
                            for k in range(GK):
                                last = nc.tensor.transpose(
                                    psT[:, k * P:(k + 1) * P],
                                    yg[p % 2][:, :, :].rearrange("p h d -> p (h d)")[:, k * P:(k + 1) * P], ident[:, :])
                            last.then_inc(s_yt, 1)

            @block.scalar
            def _(act):
                def unit_in(it, mm, c, first=0):
                    u = unit_at(it, mm, c)
                    j = (mm * UNITS + c) % 2
                    if not first:
                        act.wait_ge(s_cv, u - 1)
                    wait_apart(act, s_pr, u + 1, s_act_passed)
                    m = 2 * S if c == 2 else P
                    col = bass.ds(it * 2 + mm // NB, 1) if c == 2 else bass.ds(cols_at(it, mm, c), 1)
                    mu_, bi_, tw, tb = (mub, bib, t0wb, t0bb) if c == 2 else (mux, bix, t0w, t0b)
                    nc.scalar.activation(xr[j][0:m, KW - 1:], psP[0:m, :], ACT.Identity, bias=bi_[:, col],
                                         scale=mu_[:, col]).then_inc(s_xr, 1)
                    nc.scalar.activation(acc[j][0:m, :], psP[0:m, :], ACT.Identity, bias=tb[:, col],
                                         scale=tw[:, col]).then_inc(s_t0, 1)

                def unit_out(it, mm, c, first=False):
                    u = unit_at(it, mm, c)
                    j = (mm * UNITS + c) % 2
                    act.wait_ge(s_cv, u + 1)
                    if c < 2:
                        nc.scalar.activation(feat[mm % 2][c][:, :], acc[j][:, :], ACT.Silu).then_inc(s_ft, 1)
                    else:
                        nc.scalar.activation(bT[mm % 2][:, :], acc[j][0:S, :], ACT.Silu)
                        nc.scalar.activation(cT[mm % 2][:, :], acc[j][S:2 * S, :], ACT.Silu).then_inc(s_ft, 1)

                act.sem_inc(s_zs, 1)
                act.sem_inc(s_xs, 1)
                act.wait_ge(s_tap, 4)
                act.wait_ge(s_pad, 1)
                for c in range(UNITS):
                    unit_in(0, 0, c, first=c < 2)
                    unit_out(0, 0, c)
                with act.Fori(0, ROUNDS) as it:
                    for n in range(N + 2):
                        if n < N:
                            slot, b, c = steps[n]
                            mm, j = n // NC, n % 2
                            if c < UNITS:
                                unit_in(it, mm + 1, c)
                            act.wait_ge(s_z, it * N + (n + 1))
                            act.wait_ge(s_xe, it * N + (n + 1))
                            nc.scalar.activation(zs[n % 4][:, :], psZ[:, P:P + GF], ACT.Silu)
                            nc.scalar.activation(cb[j][:, :], psZ[:, 0:P], ACT.Copy).then_inc(s_zs, 1)
                            act.wait_ge(s_xt, it * N + (n + 1))
                            act.wait_ge(s_xdt, it * N + (n + 2))
                            nc.scalar.activation(bt[j][:, :], psX[:, GF:GF + S], ACT.Copy)
                            nc.scalar.activation(xs[j][:, :, :], psX[:, 0:GF].rearrange("p (h d) -> p h d", h=HG),
                                                 ACT.Copy).then_inc(s_xs, 1)
                            if c < UNITS:
                                unit_out(it, mm + 1, c)
                        if n >= 2:
                            p = n - 2
                            act.wait_ge(s_yg, it * N + (p + 1))
                            nc.scalar.activation(sq[:, :], yg[p % 2][:, :, :].rearrange("p h d -> p (h d)"), ACT.Square,
                                                 scale=GF ** -0.5, accum_out=ssq[p % 2][:, :]).then_inc(s_sq, 1)
                            act.wait_ge(s_yt, it * N + (p + 1))
                            nc.scalar.activation(yt[p % 2][0][:, :, :], psT[:, 0:GF].rearrange("p (k t) -> p k t", k=GK),
                                                 ACT.Copy).then_inc(s_hi, 1)

            @block.vector
            def _(dve):
                def conv(it, mm, c):
                    u = unit_at(it, mm, c)
                    j = (mm * UNITS + c) % 2
                    m = 2 * S if c == 2 else P
                    dve.wait_ge(s_xr, u + 1)
                    dve.wait_ge(s_t0, u + 1)
                    w = cwb if c == 2 else cwx
                    col = bass.ds(it * 2 + mm // NB, 1) if c == 2 else bass.ds(cols_at(it, mm, c), 1)
                    for k in range(KW - 1):
                        tap = KW - 2 - k
                        if k:
                            dve.wait_ge(s_cc, it * (2 * NU) + ((mm * UNITS + c) * 2 + k))
                        nc.vector.scalar_tensor_tensor(
                            acc[j][0:m, :], xr[j][0:m, tap:tap + L], w[:, col, tap], acc[j][0:m, :],
                            ALU.mult, ALU.add).then_inc(s_cv if k == KW - 2 else s_cc, 1)

                for sem in (s_scan, s_xdt, s_ys, s_S, s_lo, s_x):
                    dve.sem_inc(sem, 1)
                for c in range(UNITS):
                    conv(0, 0, c)
                with dve.Fori(0, ROUNDS) as it:
                    for n in range(N + 3):
                        if 2 <= n < N + 2:
                            p = n - 2
                            dve.wait_ge(s_yd, it * N + (p + 1))
                            dve.wait_ge(s_zs, it * N + (p + 2))
                            nc.vector.tensor_tensor(yg[p % 2][:, :, :], yd[p % 2][:, :, :],
                                                    zs[p % 4][:, :].rearrange("p (h d) -> p h d", h=HG), ALU.mult)\
                                .then_inc(s_yg, 1)
                        if n < N:
                            slot, b, c = steps[n]
                            mm, tt, j = n // NC, tile(n), n % 2
                            heads = bass.ds(it * (2 * HG) + slot * HG, HG)
                            dve.wait_ge(s_a, it * N + (n + 1))
                            dve.wait_ge(s_xe, it * N + (n + 1))
                            nc.vector.tensor_tensor_scan(lt[j][:, :, :].rearrange("p h i -> p (h i)"), psA[:, :],
                                                         delta[:, :], 0.0, ALU.mult, ALU.add).then_inc(s_scan, 1)
                            dve.wait_ge(s_xt, it * N + (n + 1))
                            nc.vector.tensor_tensor(xdt[j][:, :, :], psX[:, 0:GF].rearrange("p (h d) -> p h d", h=HG),
                                                    dt[:, tt, heads].unsqueeze(2).to_broadcast([P, HG, PD]), ALU.mult)\
                                .then_inc(s_xdt, 1)
                            if c < UNITS:
                                conv(it, mm + 1, c)
                        if 1 <= n <= N:
                            p = n - 1
                            slot, b, c = steps[p]
                            tt, j = tile(p), p % 2
                            heads = bass.ds(it * (2 * HG) + slot * HG, HG)
                            dve.wait_ge(s_y, it * N + (p + 1))
                            y3 = psY[:, :].rearrange("p (o h d) -> p o h d", o=2, h=HG)
                            if c > 0:
                                nc.vector.tensor_tensor(yo[j][:, :, :], y3[:, 1],
                                                        cp[:, tt, heads].unsqueeze(2).to_broadcast([P, HG, PD]), ALU.mult)\
                                    .then_inc(s_yo, 1)
                                dve.wait_ge(s_yo, it * NS + (st_at(p - 1) + 1))
                                nc.vector.tensor_tensor(ys[j][:, :, :], y3[:, 0], yo[j][:, :, :], ALU.add).then_inc(s_ys, 1)
                            else:
                                nc.vector.tensor_copy(ys[j][:, :, :], y3[:, 0]).then_inc(s_ys, 1)
                            if c < NC - 1:
                                ps3 = psS[0:S, 0:GF].rearrange("s (h d) -> s h d", h=HG)
                                dve.wait_ge(s_st, it * NS + (st_at(p) + 1))
                                if c == 0:
                                    nc.vector.tensor_copy(state[:, :, :], ps3).then_inc(s_S, 1)
                                else:
                                    nc.vector.tensor_tensor(
                                        state[:, :, :], state[:, :, :],
                                        tot[:, tt, heads].unsqueeze(2).to_broadcast([S, HG, PD]), ALU.mult)\
                                        .then_inc(s_sc, 1)
                                    dve.wait_ge(s_sc, it * (2 * NB * (NC - 2)) + (p // NC * (NC - 2) + c))
                                    nc.vector.tensor_tensor(state[:, :, :], ps3, state[:, :, :], ALU.add).then_inc(s_S, 1)
                        if n >= 3:
                            p = n - 3
                            cols = slice(tile(p) * D, (tile(p) + 1) * D)
                            dve.wait_ge(s_o, it * N + (p + 2))
                            dve.wait_ge(s_rs, it * N + (p + 1))
                            nc.vector.scalar_tensor_tensor(x[:, cols], psO[:, 0:D], rstd[p % 2][:, 0:1], x[:, cols],
                                                           ALU.mult, ALU.add).then_inc(s_x, 1)
                        if 2 <= n < N + 2:
                            p = n - 2
                            dve.wait_ge(s_hi, it * N + (p + 1))
                            nc.vector.tensor_tensor(yt[p % 2][1][:, :, :], psT[:, 0:GF].rearrange("p (k t) -> p k t", k=GK),
                                                    yt[p % 2][0][:, :, :], ALU.subtract).then_inc(s_lo, 1)


def macaron(nc, hidden, m_in, f_in, s_in, e_in, out):
    with ExitStack() as ctx:
        M = common(nc, ctx)
        stage_load(nc, M, hidden)
        ffn0(nc, M, "f1", *f_in)
        norm_block(nc, M, "n2")
        mamba(nc, M, "ssm", *m_in)
        ffn0(nc, M, "f3", *f_in)
        ffn1(nc, M, "f4", *e_in)
        attention(nc, M, "at", *s_in)
        ffn1(nc, M, "f6", *e_in)
        stage_store(nc, M, out)


_MAMBA = ["L0_attn_" + n for n in ("W_in", "b_in", "conv_w", "conv_b", "A_log", "D_param", "dt_bias", "norm_w", "W_out",
                                   "b_out", "mup_vector")]
_FFN0 = ["L0_ffn_" + n for n in ("w_gate", "w1", "w3", "w2")]
_ATTN = ["L1_attn_" + n for n in ("Wqkv", "Wproj", "bproj")]
_FFN1 = ["L1_ffn_" + n for n in ("gate_w", "wg", "wu", "wd", "sg", "su", "sd")]


def kernel(**inputs):
    import numpy as _np
    import concourse.bacc as _bacc
    from concourse.bass_utils import run_bass_kernel_spmd as _run

    nc = _bacc.Bacc("TRN2", target_bir_lowering=False, num_devices=1)
    arrays, aps = {}, {}
    for name in ["L0_attn_hidden_states"] + _MAMBA + _FFN0 + _ATTN + _FFN1:
        a = _np.ascontiguousarray(inputs[name])
        arrays[f"in_{name}_dram"] = a
        aps[name] = nc.dram_tensor(f"in_{name}_dram", a.shape, mybir.dt.from_np(a.dtype), kind="ExternalInput").ap()
    out = nc.dram_tensor("out_0_dram", (B, L, D), F32, kind="ExternalOutput").ap()
    macaron(nc, aps["L0_attn_hidden_states"], *([aps[n] for n in g] for g in (_MAMBA, _FFN0, _ATTN, _FFN1)), out)
    r = _run(nc, [arrays], core_ids=[0])
    return r.results[0]["out_0_dram"]
```

```python
import concourse.bass as bass
from concourse import mybir
from contextlib import ExitStack

F32 = mybir.dt.float32
F32R = mybir.dt.float32r
BF16 = mybir.dt.bfloat16
ALU = mybir.AluOpType
ACT = mybir.ActivationFunctionType
AX = mybir.AxisListType.X
P = 128

B, L, D = 4, 512, 256
T = B * L
NT = T // P
KD = D // P
EPS = 1e-5

PASSES = ((0, 0), (0, 1), (1, 0))


class Stage:

    def __init__(self, nc, name):
        self.nc, self.name, self.stack, self.sems = nc, name, ExitStack(), []

    def __enter__(self):
        self.stack.__enter__()
        return self

    def __exit__(self, *a):
        self.stack.__exit__(*a)
        if self.sems and a[0] is None:
            self.nc.clear_and_free_semaphores(self.sems)
            self.nc.all_engine_barrier(sem_only=True)

    def sb(self, name, shape, dt=F32):
        return self.stack.enter_context(self.nc.sbuf_tensor(f"{self.name}_{name}", shape, dt))

    def ps(self, name, shape=(P, 512), dt=F32):
        return self.stack.enter_context(self.nc.psum_tensor(f"{self.name}_{name}", list(shape), dt))

    def sem(self, name):
        self.sems.append(self.nc.alloc_semaphore(f"{self.name}_{name}"))
        return self.sems[-1]

    def block(self):
        return self.stack.enter_context(self.nc.Block())


def link(eng, sem, count, instruction):
    count[0] += 1
    instruction.then_inc(sem, 1)
    eng.wait_ge(sem, count[0])


def wait_apart(eng, sem, value, passed):
    eng.wait_ge(sem, value)
    eng.sem_inc(passed, 1)


def product(nc, out, lhs, rhs, start, stop, **kw):
    for n, (a, b) in enumerate(PASSES):
        last = nc.tensor.matmul(out, lhs[a], rhs[b], start=start and n == 0, stop=stop and n == len(PASSES) - 1, **kw)
    return last


def stage_load(nc, M, x_dram, x_in):
    with Stage(nc, "load") as s:
        zero, done, done16 = s.sem("zero"), s.sem("const"), s.sem("const16")
        block = s.block()

        @block.sync
        def _(sp):
            x3 = M["x"][:, :].rearrange("p (t d) -> p t d", d=D)
            for b in range(B):
                sp.dma_start(x3[:, b * L // P:(b + 1) * L // P, :],
                             x_dram[b:b + 1, :, :].rearrange("b (t p) d -> p (b t) d", p=P)).then_inc(x_in[b], 16)

        @block.gpsimd
        def _(pool):
            nc.gpsimd.memset(M["ident"][:, :], 0.0).then_inc(zero, 1)
            pool.wait_ge(zero, 1)
            nc.gpsimd.affine_select(out=M["ident"][:, :], in_=M["ident"][:, :], compare_op=ALU.not_equal, fill=1.0,
                                    base=0, pattern=[[-1, P]], channel_multiplier=1).then_inc(done, 1)

        @block.vector
        def _(dve):
            nc.vector.memset(M["zero"][:, :], 0.0)
            dve.wait_ge(done, 1)
            nc.vector.tensor_copy(M["ident16"][:, :], M["ident"][:, :]).then_inc(done16, 1)


class Part:

    def sync(self, sp):
        pass

    def gpsimd(self, pool):
        pass

    def scalar(self, act):
        pass

    def tensor(self, pe):
        pass

    def vector(self, dve):
        pass


def run_block(nc, *parts):
    with nc.Block() as block:
        @block.sync
        def _(sp):
            for part in parts:
                part.sync(sp)

        @block.gpsimd
        def _(pool):
            for part in parts:
                part.gpsimd(pool)

        @block.scalar
        def _(act):
            for part in parts:
                part.scalar(act)

        @block.tensor
        def _(pe):
            for part in parts:
                part.tensor(pe)

        @block.vector
        def _(dve):
            for part in parts:
                part.vector(dve)


class Norm(Part):

    BATCH = 4
    behind = None

    def __init__(self, nc, M, s, x_loaded=None):
        self.nc, self.M, self.x_loaded = nc, M, x_loaded
        self.stats = s.sb("stats", [P, NT, 6])
        self.mv = s.sb("mean_var", [P, NT, 2])
        self.veps, self.rstd, self.shift = (s.sb(n, [P, NT]) for n in ("var_eps", "rstd", "shift"))
        self.half = s.sb("minus_half", [P, self.BATCH])
        self.xn = [s.sb(f"xn{j}", [P, D]) for j in range(4)]
        self.psT = [s.ps(f"T{j}") for j in range(4)]
        (self.s_half, self.s_stat, self.s_aggr, self.s_veps, self.s_rstd, self.s_shift, self.s_xn, self.s_tr, self.s_hi,
         self.s_lo) = (s.sem(n) for n in ("half", "stat", "aggr", "veps", "rstd", "shift", "xn", "transposed", "hi", "lo"))

    def gpsimd(self, pool):
        self.nc.gpsimd.memset(self.half[:, :], -0.5).then_inc(self.s_half, 1)
        pool.wait_ge(self.s_half, 1)
        for g in range(NT // self.BATCH):
            at = slice(g * self.BATCH, (g + 1) * self.BATCH)
            pool.wait_ge(self.s_veps, g + 1)
            self.nc.gpsimd.tensor_tensor(self.rstd[:, at], self.veps[:, at], self.half[:, :], ALU.pow)\
                .then_inc(self.s_rstd, 1)
            if g == 1 and self.behind:
                self.behind.weights(pool)

    def vector(self, dve):
        nc, x, xT = self.nc, self.M["x"], self.M["xT"]

        def lo(t):
            dve.wait_ge(self.s_hi, t + 1)
            cols = slice(t * P, (t + 1) * P)
            nc.vector.tensor_tensor(xT[1][:, :, cols], self.psT[t % 4][:, 0:D].rearrange("p (k t) -> p k t", k=KD),
                                    xT[0][:, :, cols], ALU.subtract).then_inc(self.s_lo, 1)

        def shift(g):
            at = slice(g * self.BATCH, (g + 1) * self.BATCH)
            dve.wait_ge(self.s_rstd, g + 1)
            nc.vector.scalar_tensor_tensor(self.shift[:, at], self.mv[:, at, 0], -1.0, self.rstd[:, at], ALU.mult,
                                           ALU.mult).then_inc(self.s_shift, 1)

        for g in range(NT // self.BATCH):
            if self.x_loaded:
                dve.wait_ge(self.x_loaded[g], 16)
            tiles = range(g * self.BATCH, (g + 1) * self.BATCH)
            for t in tiles:
                nc.vector.bn_stats(out=self.stats[:, t, :], in_=x[:, t * D:(t + 1) * D]).then_inc(self.s_stat, 1)
            for t in tiles:
                dve.wait_ge(self.s_stat, t + 1)
                nc.vector.bn_aggr(out=self.mv[:, t, :], in_=self.stats[:, t, :]).then_inc(self.s_aggr, 1)
            dve.wait_ge(self.s_aggr, tiles[-1] + 1)
            nc.vector.tensor_scalar(self.veps[:, tiles[0]:tiles[-1] + 1], self.mv[:, tiles[0]:tiles[-1] + 1, 1], EPS, None,
                                    ALU.add).then_inc(self.s_veps, 1)
            if g:
                shift(g - 1)
            if g > 1:
                lo(2 * g - 4)
                lo(2 * g - 3)
        for t in range(2 * (NT // self.BATCH) - 4, NT):
            if t == 5:
                shift(NT // self.BATCH - 1)
            lo(t)

    def scalar(self, act):
        nc, x, xT, behind = self.nc, self.M["x"], self.M["xT"], self.behind

        def normed(t):
            if t % self.BATCH == 0:
                act.wait_ge(self.s_shift, t // self.BATCH + 1)
            if t >= 4:
                act.wait_ge(self.s_tr, t - 3)
            nc.scalar.activation(self.xn[t % 4][:, :], x[:, t * D:(t + 1) * D], ACT.Identity,
                                 scale=self.rstd[:, t:t + 1], bias=self.shift[:, t:t + 1]).then_inc(self.s_xn, 1)

        def hi(t):
            act.wait_ge(self.s_tr, t + 1)
            nc.scalar.activation(xT[0][:, :, t * P:(t + 1) * P], self.psT[t % 4][:, 0:D].rearrange("p (k t) -> p k t", k=KD),
                                 ACT.Copy).then_inc(self.s_hi, 1)

        for t in range(NT + 2):
            if t < NT:
                normed(t)
            if t >= 2:
                hi(t - 2)
            if behind and t in (9, 13, 17):
                behind.copy(act, (t - 9) // 4)

    def tensor(self, pe):
        for t in range(NT):
            pe.wait_ge(self.s_xn, t + 1)
            if t >= 4:
                pe.wait_ge(self.s_lo, t - 3)
            for k in range(KD):
                last = self.nc.tensor.transpose(self.psT[t % 4][:, k * P:(k + 1) * P], self.xn[t % 4][:, k * P:(k + 1) * P],
                                                self.M["ident"][:, :])
            last.then_inc(self.s_tr, 1)
            if self.behind and t in (6, 10, 14):
                self.behind.block(pe, (t - 6) // 4)


class Logits(Part):

    def __init__(self, nc, M, s, norm, w_dram, E, squash, out):
        self.nc, self.M, self.norm, self.w_dram, self.E, self.squash, self.out = nc, M, norm, w_dram, E, squash, out
        norm.behind = self
        self.w = s.sb("l_w", [P, KD, E])
        self.wr = [s.sb(f"l_w_{q}", [P, KD, E], F32R) for q in ("hi", "lo")]
        self.lT = s.sb("l_T", [E, T])
        self.cap = s.sb("l_tanh", [P, NT * E])
        self.psL = [s.ps(f"L{b}") for b in range(T // 512)]
        self.s_w, self.s_whi, self.s_wlo, self.s_lT, self.s_out, self.s_tok, self.s_cap = (
            s.sem("l_" + n) for n in ("w", "w_hi", "w_lo", "product", "copied", "token_major", "tanh"))

    def sync(self, sp):
        sp.dma_start(self.w[:, :, :], self.w_dram.rearrange("(k p) e -> p k e", p=P)).then_inc(self.s_w, 16)

    def weights(self, pool):
        nc, zero = self.nc, self.M["zero"]
        pool.wait_ge(self.s_w, 16)
        nc.gpsimd.tensor_tensor(self.wr[0][:, :, :], self.w[:, :, :],
                                zero[:, :].unsqueeze(2).to_broadcast([P, KD, self.E]), ALU.add).then_inc(self.s_whi, 1)
        pool.wait_ge(self.s_whi, 1)
        nc.gpsimd.tensor_tensor(self.wr[1][:, :, :], self.w[:, :, :], self.wr[0][:, :, :], ALU.subtract)\
            .then_inc(self.s_wlo, 1)

    def block(self, pe, b):
        if b == 0:
            pe.wait_ge(self.s_wlo, 1)
        pe.wait_ge(self.norm.s_lo, 4 * b + 4)
        for k in range(KD):
            last = product(self.nc, self.psL[b][0:self.E, :], [a[:, k, :] for a in self.wr],
                           [a[:, k, b * 512:(b + 1) * 512] for a in self.M["xT"]], k == 0, k == KD - 1)
        last.then_inc(self.s_lT, 1)

    def copy(self, act, b):
        act.wait_ge(self.s_lT, b + 1)
        self.nc.scalar.activation(self.lT[:, b * 512:(b + 1) * 512], self.psL[b][0:self.E, :], ACT.Copy)\
            .then_inc(self.s_out, 1)

    def tensor(self, pe):
        nc, E, norm = self.nc, self.E, self.norm
        self.block(pe, T // 512 - 1)
        for t in range(NT):
            if t % 4 == 0:
                pe.wait_ge(self.s_out, t // 4 + 1)
            last = nc.tensor.transpose(norm.psT[0][:, t * E:(t + 1) * E], self.lT[:, t * P:(t + 1) * P],
                                       self.M["ident"][0:E, 0:E])
        last.then_inc(self.s_tok, 1)

    def scalar(self, act):
        nc, E = self.nc, self.E
        self.copy(act, T // 512 - 1)
        logits = self.norm.psT[0][:, 0:NT * E]
        act.wait_ge(self.s_tok, 1)
        if self.squash == "softcap":
            nc.scalar.activation(self.cap[:, :], logits, ACT.Tanh, scale=1.0 / 30.0).then_inc(self.s_cap, 1)
            act.wait_ge(self.s_cap, 1)
            nc.scalar.activation(self.out, self.cap[:, :], ACT.Exp, scale=30.0)
        elif self.squash == "sigmoid":
            nc.scalar.activation(self.out, logits, ACT.Sigmoid)
        else:
            nc.scalar.activation(self.out, logits, ACT.Copy)


class Route(Part):

    def __init__(self, nc, M, s, score, E, K, squash, route):
        self.nc, self.M, self.E, self.K, self.squash, self.route, self.p = nc, M, E, K, squash, route, score
        W = NT * E
        self.e = s.sb("work", [P, W])
        self.e2 = s.sb("work2", [P, W])
        self.first = s.sb("not_first", [P, W])
        self.top = s.sb("top", [P, NT * 8])
        self.small = [s.sb(f"small{c}", [P, NT]) for c in range(3)]
        self.s_first, self.s_dve, self.s_max, self.s_parts = (s.sem(n) for n in ("first", "chain", "max", "parts"))
        if squash == "sigmoid":
            self.parts = s.sb("parts", [P, NT, 3 * E], BF16)

    def by_tile(self, a):
        return a[:, :].rearrange("p (t e) -> p t e", e=self.E)

    def over(self, a):
        return a[:, :].unsqueeze(2).to_broadcast([P, NT, self.E])

    def gpsimd(self, pool):
        nc = self.nc
        nc.gpsimd.memset(self.first[:, :], 1.0).then_inc(self.s_first, 1)
        pool.wait_ge(self.s_first, 1)
        nc.gpsimd.memset(self.by_tile(self.first)[:, :, 0], 0.0).then_inc(self.s_first, 1)

    def vector(self, dve):
        nc, E, K, squash, route = self.nc, self.E, self.K, self.squash, self.route
        n = [0]

        def chain(instruction):
            link(dve, self.s_dve, n, instruction)

        dve.wait_ge(self.s_first, 2)
        if squash == "softcap":
            chain(nc.vector.tensor_reduce(self.small[0][:, :], self.by_tile(self.p), AX, ALU.add))
            chain(nc.vector.reciprocal(self.small[1][:, :], self.small[0][:, :]))
            chain(nc.vector.tensor_tensor(self.by_tile(self.p), self.by_tile(self.p), self.over(self.small[1]), ALU.mult))
        for t in range(NT):
            nc.vector.max(out=self.top[:, t * 8:(t + 1) * 8], in_=self.by_tile(self.p)[:, t, :]).then_inc(self.s_max, 1)
        dve.wait_ge(self.s_max, NT)
        kth = self.top[:, :].rearrange("p (t c) -> p t c", c=8)[:, :, K - 1:K].to_broadcast([P, NT, E])
        chain(nc.vector.tensor_tensor(self.by_tile(self.e), self.by_tile(self.p), kth, ALU.is_gt))
        chain(nc.vector.tensor_tensor(self.by_tile(self.e2), self.by_tile(self.p), kth, ALU.is_equal))
        chain(nc.vector.tensor_reduce(self.small[0][:, :], self.by_tile(self.e), AX, ALU.add))
        chain(nc.vector.tensor_scalar(self.small[1][:, :], self.small[0][:, :], -1.0, float(K), ALU.mult, ALU.add))
        chain(nc.vector.tensor_tensor_scan(self.first[:, :], self.first[:, :], self.e2[:, :], 0.0, ALU.mult, ALU.add))
        chain(nc.vector.tensor_tensor(self.by_tile(self.first), self.by_tile(self.first), self.over(self.small[1]), ALU.is_le))
        chain(nc.vector.tensor_tensor(self.e2[:, :], self.e2[:, :], self.first[:, :], ALU.mult))
        chain(nc.vector.tensor_tensor(self.e[:, :], self.e[:, :], self.e2[:, :], ALU.add))
        if squash == "softcap":
            chain(nc.vector.scalar_tensor_tensor(route[:, :], self.e[:, :], 0.5, self.p[:, :], ALU.mult, ALU.mult))
            return
        chain(nc.vector.tensor_tensor(self.e[:, :], self.e[:, :], self.p[:, :], ALU.mult))
        chain(nc.vector.tensor_reduce(self.small[0][:, :], self.by_tile(self.e), AX, ALU.add))
        chain(nc.vector.tensor_scalar(self.small[1][:, :], self.small[0][:, :], 1e-20, None, ALU.add))
        chain(nc.vector.reciprocal(self.small[2][:, :], self.small[1][:, :]))
        chain(nc.vector.tensor_tensor(self.by_tile(self.e), self.by_tile(self.e), self.over(self.small[2]), ALU.mult))
        chain(nc.vector.tensor_copy(self.parts[:, :, 0:E], self.by_tile(self.e)))
        chain(nc.vector.tensor_tensor(self.by_tile(self.e2), self.by_tile(self.e), self.parts[:, :, 0:E], ALU.subtract))
        chain(nc.vector.tensor_copy(self.parts[:, :, E:2 * E], self.by_tile(self.e2)))
        chain(nc.vector.tensor_tensor(self.by_tile(self.e), self.by_tile(self.e2), self.parts[:, :, E:2 * E], ALU.subtract))
        nc.vector.tensor_copy(self.parts[:, :, 2 * E:3 * E], self.by_tile(self.e)).then_inc(self.s_parts, 1)


class Spread(Part):

    def __init__(self, nc, M, s, route):
        self.nc, self.M, self.of = nc, M, route
        self.psR = [s.ps(f"R{n}", (P, 1024), BF16) for n in range(2)]
        self.s_tr = s.sem("parts_T")

    def tensor(self, pe):
        E = self.of.E
        pe.wait_ge(self.of.s_parts, 1)
        for t in range(NT):
            last = self.nc.tensor.transpose(self.psR[t // 8][0:3 * E, t % 8 * P:(t % 8 + 1) * P], self.of.parts[:, t, :],
                                            self.M["ident16"][:, :])
            if t % 8 == 7:
                last.then_inc(self.s_tr, 1)

    def scalar(self, act):
        for n in range(2):
            act.wait_ge(self.s_tr, n + 1)
            self.nc.scalar.activation(self.of.route[:, n * 1024:(n + 1) * 1024], self.psR[n][0:3 * self.of.E, :], ACT.Copy)


class FFN(Part):

    def __init__(self, nc, M, s, tag, groups, NF, load, weight=None, lanes=None, loads=3):
        self.nc, self.M, self.groups, self.NF, self.load, self.weight, self.lanes = nc, M, groups, NF, load, weight, lanes
        self.NB = T // 512
        self.sizes = [min(P, NF - c) for c in range(0, NF, P)]
        self.NC = NC = len(self.sizes)
        self.two = two = 2 if groups > 1 else 1
        self.rounds = groups // two
        self.steps = [(slot, b, c) for slot in range(two) for b in range(self.NB) for c in range(NC)]
        self.N = len(self.steps)
        self.LOADED = loads * 16
        self.NW = len(self.full(0))

        def sb(name, shape, dt=F32):
            return s.sb(tag + name, shape, dt)

        self.raw = [[sb(f"raw_{w}{j}", [P, 2, NF]) for w in "gu"] + [sb(f"raw_d{j}", [P, NC, D])] for j in range(two)]
        self.wts = [[[sb(f"{w}_{q}{j}", [P, 2, NF], F32R) for q in ("hi", "lo")] for w in "gu"]
                    + [[sb(f"d_{q}{j}", [P, NC, D], F32R) for q in ("hi", "lo")]] for j in range(two)]
        self.sg = [sb(f"silu{j}", [P, 512]) for j in range(2)]
        self.hf = [sb(f"h{j}", [P, 512]) for j in range(2)]
        self.hr = [[sb(f"h_{q}{j}", [P, 512], F32R) for q in ("hi", "lo")] for j in range(2)]
        self.s_raw = [s.sem(f"{tag}raw{j}") for j in range(two)]
        (self.s_whi, self.s_wlo, self.s_g, self.s_u, self.s_silu) = (
            s.sem(tag + n) for n in ("w_hi", "w_lo", "g", "u", "silu"))
        (self.s_h, self.s_hhi, self.s_hlo, self.s_down, self.s_out, self.s_mul) = (
            s.sem(tag + n) for n in ("h", "h_hi", "h_lo", "down", "out", "mul"))

    def take_psum(self, s):
        self.psG = [s.ps(f"G{j}") for j in range(2)]
        self.psU = [s.ps(f"U{j}") for j in range(2)]
        self.psO = s.ps("O", (P, 1024))
        self.psC = [s.ps(f"C{j}") for j in range(2)] if self.lanes else None

    def full(self, slot):
        gu = [(n, (slice(0, P), slice(0, 2), slice(0, self.NF))) for n in range(2)]
        if self.sizes[-1] == P:
            return gu + [(2, (slice(0, P), slice(0, self.NC), slice(0, D)))]
        return gu + [(2, (slice(0, k), c, slice(0, D))) for c, k in enumerate(self.sizes)]

    def prepare(self, pool, i, j):
        nc, raw, wts = self.nc, self.raw, self.wts
        pool.wait_ge(self.s_raw[j], i * self.LOADED + self.LOADED)
        for n, at in self.full(j):
            hi = wts[j][n][0][at]
            zero = self.M["zero"][0:hi.shape[0], :]
            if len(hi.shape) == 3:
                zero = zero.unsqueeze(2)
            nc.gpsimd.tensor_tensor(hi, raw[j][n][at], zero.to_broadcast(hi.shape), ALU.add).then_inc(self.s_whi, 1)
        for m, (n, at) in enumerate(self.full(j)):
            pool.wait_ge(self.s_whi, i * (self.NW * self.two) + (self.NW * j + m + 1))
            nc.gpsimd.tensor_tensor(wts[j][n][1][at], raw[j][n][at], wts[j][n][0][at],
                                    ALU.subtract).then_inc(self.s_wlo, 1)

    def sync(self, sp):
        raw, NW, two, rounds, load = self.raw, self.NW, self.two, self.rounds, self.load
        if rounds > 1:
            with sp.Fori(0, rounds - 1) as i:
                for j in range(two):
                    sp.wait_ge(self.s_wlo, i * (NW * two) + NW * (j + 1))
                    load(sp, raw[j], i * two + (two + j), self.s_raw[j])

    def gpsimd(self, pool):
        for j in range(1, self.two):
            self.prepare(pool, 0, j)
        if self.rounds > 1:
            with pool.Fori(1, self.rounds) as i:
                for j in range(self.two):
                    pool.wait_ge(self.s_down, i * self.N + (j + 1) * self.N // self.two)
                    self.prepare(pool, i, j)

    def scalar(self, act):
        nc, sg, hf, hr, psG, N = self.nc, self.sg, self.hf, self.hr, self.psG, self.N
        two, rounds = self.two, self.rounds
        steps, sizes = self.steps, self.sizes
        act.sem_inc(self.s_silu, 2)
        act.sem_inc(self.s_hhi, 2)
        with act.Fori(0, rounds) as i:
            for n, (slot, b, c) in enumerate(steps):
                k, j = sizes[c], n % 2
                act.wait_ge(self.s_g, i * N + (n + 1))
                act.wait_ge(self.s_h, i * N + (n + 1))
                nc.scalar.activation(sg[j][0:k, :], psG[j][0:k, :], ACT.Silu).then_inc(self.s_silu, 1)
                act.wait_ge(self.s_h, i * N + (n + 3))
                act.wait_ge(self.s_down, i * N + (n + N - 1))
                nc.scalar.activation(hr[j][0][0:k, :], hf[j][0:k, :], ACT.Copy).then_inc(self.s_hhi, 1)

    def tensor(self, pe):
        nc, wts, hr, psG, psU, psO = self.nc, self.wts, self.hr, self.psG, self.psU, self.psO
        psC, NW = self.psC, self.NW
        NC, NB, N, two, rounds, steps = self.NC, self.NB, self.N, self.two, self.rounds, self.steps
        sizes, lanes = self.sizes, self.lanes
        NF = self.NF
        xT = self.M["xT"]

        def up(i, n):
            slot, b, c = steps[n % N]
            k, j = sizes[c], n % 2
            toks = slice(b * 512, (b + 1) * 512)
            if b == 0 and c == 0:
                pe.wait_ge(self.s_wlo, i * (NW * two) + NW * (n // N * two + slot + 1))
            pe.wait_ge(self.s_silu, i * N + (n + 1))
            for w, ps, done in ((0, psG[j], self.s_g), (1, psU[j], self.s_u)):
                if w == 1:
                    pe.wait_ge(self.s_h, i * N + (n + 1))
                    if lanes:
                        nc.tensor.matmul(psC[j][0:k, :],
                                         lanes[0][:, bass.ds(i * (two * NF) + ((n // N * two + slot) * NF + c * P), P)],
                                         lanes[1][:, toks], start=True, stop=True)
                for kk in range(KD):
                    last = product(nc, ps[0:k, :], [a[:, kk, c * P:c * P + k] for a in wts[slot][w]],
                                   [a[:, kk, toks] for a in xT], kk == 0, kk == KD - 1)
                last.then_inc(done, 1)

        def down(i, n):
            slot, b, c = steps[n]
            k, j = sizes[c], n % 2
            pe.wait_ge(self.s_hlo, i * N + (n + 1))
            for t in range(4):
                if c == 0 and t % 2 == 0:
                    pe.wait_ge(self.s_out, i * (2 * two * NB) + (2 * (slot * NB + b) + t // 2 + 1))
                last = product(nc, psO[:, t * D:(t + 1) * D], [a[0:k, t * P:(t + 1) * P] for a in hr[j]],
                               [a[0:k, c, :] for a in wts[slot][2]], c == 0 and t % 2 == 0, c == NC - 1,
                               skip_group_check=True)
            last.then_inc(self.s_down, 1)

        pe.sem_inc(self.s_down, N)
        up(0, 0)
        if rounds > 1:
            with pe.Fori(0, rounds - 1) as i:
                for n in range(N):
                    up(i, n + 1)
                    down(i, n)
        for n in range(N):
            if n + 1 < N:
                up(rounds - 1, n + 1)
            down(rounds - 1, n)

    def vector(self, dve):
        nc, sg, hf, hr, psU, psO, psC, N = self.nc, self.sg, self.hf, self.hr, self.psU, self.psO, self.psC, self.N
        two, rounds, steps, sizes, groups, weight = self.two, self.rounds, self.steps, self.sizes, self.groups, self.weight
        lanes = self.lanes
        x = self.M["x"]

        def read_out(i, n):
            slot, b, c = steps[n]
            dve.wait_ge(self.s_down, i * N + (n + N + 1))
            if weight is None:
                for u in range(2):
                    cols = slice((b * 4 + 2 * u) * D, (b * 4 + 2 * u + 2) * D)
                    nc.vector.scalar_tensor_tensor(x[:, cols], psO[:, 2 * u * D:2 * (u + 1) * D], 0.5, x[:, cols],
                                                   ALU.mult, ALU.add).then_inc(self.s_out, 1)
                return
            for t in range(4):
                cols = slice((b * 4 + t) * D, (b * 4 + t + 1) * D)
                last = nc.vector.scalar_tensor_tensor(
                    x[:, cols], psO[:, t * D:(t + 1) * D],
                    weight[:, bass.ds(i * two + ((b * 4 + t) * groups + slot), 1)], x[:, cols], ALU.mult, ALU.add)
                if t % 2:
                    last.then_inc(self.s_out, 1)

        dve.sem_inc(self.s_h, 2)
        dve.sem_inc(self.s_out, 2)
        with dve.Fori(0, rounds) as i:
            for n, (slot, b, c) in enumerate(steps):
                k, j = sizes[c], n % 2
                dve.wait_ge(self.s_u, i * N + (n + 1))
                dve.wait_ge(self.s_silu, i * N + (n + 3))
                dve.wait_ge(self.s_hhi, i * N + (n + 1))
                if lanes:
                    nc.vector.tensor_tensor(sg[j][0:k, :], psU[j][0:k, :], sg[j][0:k, :], ALU.mult)\
                        .then_inc(self.s_mul, 1)
                    dve.wait_ge(self.s_mul, i * N + (n + 1))
                    nc.vector.tensor_tensor(hf[j][0:k, :], psC[j][0:k, :], sg[j][0:k, :], ALU.mult)\
                        .then_inc(self.s_h, 1)
                else:
                    nc.vector.tensor_tensor(hf[j][0:k, :], psU[j][0:k, :], sg[j][0:k, :], ALU.mult)\
                        .then_inc(self.s_h, 1)
                dve.wait_ge(self.s_hhi, i * N + (n + 3))
                dve.wait_ge(self.s_down, i * N + (n + N - 1))
                nc.vector.tensor_tensor(hr[j][1][0:k, :], hf[j][0:k, :], hr[j][0][0:k, :], ALU.subtract)\
                    .then_inc(self.s_hlo, 1)
                if c == 0 and n:
                    read_out(i, n - 1)
            read_out(i, N - 1)


class FirstWeights(Part):

    def __init__(self, ffn):
        self.ffn = ffn

    def sync(self, sp):
        for j in range(self.ffn.two):
            self.ffn.load(sp, self.ffn.raw[j], j, self.ffn.s_raw[j])

    def gpsimd(self, pool):
        self.ffn.prepare(pool, 0, 0)


class Extra(Part):

    def __init__(self, sync=None, gpsimd=None):
        if sync:
            self.sync = sync
        if gpsimd:
            self.gpsimd = gpsimd


def common(nc, ctx):
    def sb(name, shape, dt=F32):
        return ctx.enter_context(nc.sbuf_tensor(name, shape, dt))

    return {
        "x": sb("x", [P, NT * D]),
        "xT": [sb(f"xT_{q}", [P, KD, T], F32R) for q in ("hi", "lo")],
        "ident": sb("ident", [P, P]),
        "zero": sb("zero", [P, 1]),
        "ident16": sb("ident16", [P, P], BF16),
        "sel": sb("sel", [96, 32 * 96], BF16),
    }


def stage_store(nc, M, out_dram):
    with Stage(nc, "store") as s:
        x_out = s.sem("x_out")
        block = s.block()

        @block.sync
        def _(sp):
            sp.dma_start(out_dram.rearrange("b (t p) d -> p (b t) d", p=P),
                         M["x"][:, :].rearrange("p (t d) -> p t d", d=D)).then_inc(x_out, 16)
            sp.wait_ge(x_out, 16)


def select_columns(nc, M, s):
    made = s.sem("select")

    def work(pool):
        nc.gpsimd.memset(M["sel"][:, :], 1.0).then_inc(made, 1)
        for q in range(3):
            pool.wait_ge(made, q + 1)
            rows = M["sel"][32 * q:32 * q + 32, :].rearrange("r (e f) -> r e f", e=32)
            nc.gpsimd.affine_select(out=rows, in_=rows, compare_op=ALU.is_equal, fill=0.0, base=0,
                                    pattern=[[-1, 32], [0, 96]], channel_multiplier=1).then_inc(made, 1)

    return work


def ffn0(nc, M, name, gate, w1, w3, w2, x_loaded=None):
    E = w1.shape[0]

    def load(sp, raw, g, sem):
        one = bass.ds(g, 1)
        sp.dma_start(raw[0][:, :, :], w1[one, :, :].rearrange("e (k p) f -> p (e k) f", p=P)).then_inc(sem, 16)
        sp.dma_start(raw[1][:, :, :], w3[one, :, :].rearrange("e (k p) f -> p (e k) f", p=P)).then_inc(sem, 16)
        sp.dma_start(raw[2][:, :, :], w2[one, :, :].rearrange("e (c p) d -> p (e c) d", p=P)).then_inc(sem, 16)

    with Stage(nc, name) as s:
        weight = s.sb("route", [P, NT * E])
        score = s.sb("score", [P, NT * E])
        experts = FFN(nc, M, s, "e_", E, w1.shape[2], load, weight=weight)
        with Stage(nc, name + "n") as n:
            norm = Norm(nc, M, n, x_loaded)
            run_block(nc, norm, Logits(nc, M, n, norm, gate, E, "softcap", score[:, :]), FirstWeights(experts))
        with Stage(nc, name + "m") as m:
            experts.take_psum(m)
            extra = [Extra(gpsimd=select_columns(nc, M, m))] if x_loaded else []
            run_block(nc, Route(nc, M, m, score, E, 2, "softcap", weight), experts, *extra)


def ffn1(nc, M, name, gate, wg, wu, wd, sg, su, sd):
    E, F = wg.shape[0], wg.shape[2]
    PER = 4

    def load(sp, raw, g, sem):
        for n, w in ((0, wg), (1, wu)):
            for k in range(KD):
                sp.dma_start(raw[n][:, k, :].rearrange("p (e f) -> p e f", e=PER),
                             w[bass.ds(g * PER, PER), k * P:(k + 1) * P, :].rearrange("e p f -> p e f"))\
                    .then_inc(sem, 16)
        sp.dma_start(raw[2][:, :, :], wd.rearrange("e f d -> (e f) d")[bass.ds(g * (PER * F), PER * F), :]
                     .rearrange("(c p) d -> p c d", p=P)).then_inc(sem, 16)

    def load_shared(sp, raw, g, sem):
        for n, w in ((0, sg), (1, su)):
            sp.dma_start(raw[n][:, :, :], w.rearrange("(k p) f -> p k f", p=P)).then_inc(sem, 16)
        sp.dma_start(raw[2][:, 0, :], sd[0:P, :]).then_inc(sem, 16)
        sp.dma_start(raw[2][0:sd.shape[0] - P, 1, :], sd[P:, :]).then_inc(sem, 16)

    with Stage(nc, name) as s:
        weight = s.sb("route", [3 * E, T], BF16)
        experts = FFN(nc, M, s, "e_", E // PER, PER * F, load, lanes=(M["sel"], weight), loads=5)
        with Stage(nc, name + "s") as s2:
            score = s2.sb("score", [P, NT * E])
            shared = FFN(nc, M, s2, "s_", 1, sg.shape[1], load_shared, loads=4)
            with Stage(nc, name + "n") as n:
                norm = Norm(nc, M, n)
                run_block(nc, norm, Logits(nc, M, n, norm, gate, E, "sigmoid", score[:, :]), FirstWeights(shared))
            with Stage(nc, name + "m") as m:
                shared.take_psum(m)
                route = Route(nc, M, m, score, E, 6, "sigmoid", weight)
                run_block(nc, route, shared, Spread(nc, M, m, route), FirstWeights(experts))
        with Stage(nc, name + "x") as m:
            experts.take_psum(m)
            run_block(nc, experts)


def attention(nc, M, name, w_qkv, w_proj, b_proj):
    HEADS, HD = 16, 16
    PAIRS = HEADS // 2
    TB = L // P
    xT, x, ident = M["xT"], M["x"], M["ident"]
    with Stage(nc, name) as keep:
        wq = [keep.sb(f"wq_{q}", [P, KD, HEADS, 4, HD], F32R) for q in ("hi", "lo")]
        wk = [keep.sb(f"wk_{q}", [P, KD, HEADS, 4, HD], F32R) for q in ("hi", "lo")]
        wp = [keep.sb(f"wp_{q}", [P, 4, D], F32R) for q in ("hi", "lo")]
        v_all = keep.sb("v_all", [P, NT, HEADS, HD])
        neg_q, neg_k, one_k = (keep.sb(n, [P, 1]) for n in ("neg_q", "neg_k", "one_k"))

        with Stage(nc, name + "w") as s:
            wv = [s.sb(f"wv_{q}", [P, KD, HEADS, HD], F32R) for q in ("hi", "lo")]
            wn = s.sb("w_qkv", [P, 6, D])
            pn = s.sb("w_proj", [P, KD, D])
            pp = s.sb("w_proj_twice", [P, KD, 4, 4, 32])
            bias = s.sb("bias", [P, D])
            s_w, s_p, s_b, s_zero, s_pad = (s.sem(n) for n in ("w", "p", "b", "zero", "pad"))
            s_tw, s_tp, s_hi, s_lo, s_v, s_vout, s_mask, s_bias = (
                s.sem(n) for n in ("tw", "tp", "hi", "lo", "v", "v_out", "mask", "bias"))

            def loads(sp):
                sp.dma_start(wn[:, :, :], w_qkv.rearrange("(r p) n -> p r n", p=P)).then_inc(s_w, 16)
                sp.dma_start(pn[:, :, :], w_proj.rearrange("(r p) n -> p r n", p=P)).then_inc(s_p, 16)
                sp.dma_start(bias[:, :], b_proj.rearrange("(a n) -> a n", a=1).to_broadcast([P, D])).then_inc(s_b, 16)

            with Stage(nc, name + "n") as n:
                run_block(nc, Norm(nc, M, n), Extra(sync=loads))

            psW = [s.ps(f"W{k}", (P, 1024)) for k in range(KD)]
            psP = s.ps("Wp", (P, 1024))
            psV = [s.ps(f"V{j}") for j in range(2)]
            block = s.block()

            @block.gpsimd
            def _(pool):
                for w in wq + wk:
                    for k in range(KD):
                        last = nc.gpsimd.memset(w[:, k, :, 2, :].bitcast(F32), 0.0)
                last.then_inc(s_zero, 1)
                pool.wait_ge(s_b, 16)
                x3 = x[:, :].rearrange("p (t d) -> p t d", d=D)
                nc.gpsimd.tensor_tensor(x3, x3, bias[:, :].unsqueeze(1).to_broadcast([P, NT, D]), ALU.add)\
                    .then_inc(s_bias, 1)

            @block.tensor
            def _(pe):
                pe.wait_ge(s_w, 16)
                for k in range(KD):
                    for r in range(6):
                        last = nc.tensor.transpose(psW[k][:, r * P:(r + 1) * P], wn[:, r, k * P:(k + 1) * P],
                                                   ident[:, :])
                    last.then_inc(s_tw, 1)
                pe.wait_ge(s_pad, 1)
                for m in range(4):
                    for r in range(KD):
                        last = nc.tensor.transpose(psP[:, m * D + r * P:m * D + (r + 1) * P],
                                                   pp[:, r, m, :, :].rearrange("p a b -> p (a b)"), ident[:, :])
                last.then_inc(s_tp, 1)
                pe.wait_ge(s_lo, KD)
                for t in range(NT):
                    if t >= 2:
                        pe.wait_ge(s_vout, t - 1)
                    for k in range(KD):
                        last = product(nc, psV[t % 2][:, 0:D], [a[:, k, t * P:(t + 1) * P] for a in xT],
                                       [a[:, k, :, :].rearrange("p h d -> p (h d)") for a in wv],
                                       k == 0, k == KD - 1)
                    last.then_inc(s_v, 1)

            def columns(k, c):
                return psW[k][:, 0:768].rearrange("p (q m c d) -> p q m c d", q=4, c=3, d=HD)[:, :, :, c, :]

            def blocks(w, k):
                return [w[:, k, :, a, :].rearrange("p (m q) d -> p q m d", m=4) for a in (0, 1, 3)]

            def values(w, k):
                return w[:, k, :, :].rearrange("p (q m) d -> p q m d", m=4)

            @block.scalar
            def _(act):
                for k in range(KD):
                    act.wait_ge(s_tw, k + 1)
                    nc.scalar.activation(values(wv[0], k), columns(k, 2), ACT.Copy)
                    for w, c in ((wq, 0), (wk, 1)):
                        for dst in blocks(w[0], k):
                            last = nc.scalar.activation(dst, columns(k, c), ACT.Copy)
                    last.then_inc(s_hi, 1)
                act.wait_ge(s_tp, 1)
                nc.scalar.activation(wp[0][:, :, :].rearrange("p m n -> p (m n)"), psP[:, :], ACT.Copy).then_inc(s_hi, 1)
                for t in range(NT):
                    act.wait_ge(s_v, t + 1)
                    nc.scalar.activation(v_all[:, t, :, :].rearrange("p h d -> p (h d)"), psV[t % 2][:, 0:D], ACT.Copy)\
                        .then_inc(s_vout, 1)

            @block.vector
            def _(dve):
                n = [0]
                ones = ident[:, :].rearrange("p (h r) -> p h r", h=2)
                XY = mybir.AxisListType.XY
                link(dve, s_mask, n, nc.vector.tensor_reduce(one_k[:, :], ones[:, :, 32:34], XY, ALU.add))
                link(dve, s_mask, n, nc.vector.tensor_reduce(neg_q[:, :], ones[:, :, 48:64], XY, ALU.add))
                link(dve, s_mask, n, nc.vector.tensor_reduce(neg_k[:, :], ones[:, :, 16:32], XY, ALU.add))
                link(dve, s_mask, n, nc.vector.tensor_scalar(neg_q[:, :], neg_q[:, :], -1.0, None, ALU.mult))
                link(dve, s_mask, n, nc.vector.tensor_tensor(neg_k[:, :], one_k[:, :], neg_k[:, :], ALU.subtract))
                dve.wait_ge(s_p, 16)
                for r in range(KD):
                    for half in range(2):
                        last = nc.vector.tensor_copy(
                            pp[:, r, :, :, half * HD:(half + 1) * HD],
                            pn[:, r, :].rearrange("p (m h d) -> p m h d", m=4, h=4))
                last.then_inc(s_pad, 1)
                dve.wait_ge(s_zero, 1)
                for k in range(KD):
                    dve.wait_ge(s_hi, k + 1)
                    nc.vector.tensor_tensor(values(wv[1], k), columns(k, 2), values(wv[0], k), ALU.subtract)
                    for w, c in ((wq, 0), (wk, 1)):
                        for dst, hi in zip(blocks(w[1], k), blocks(w[0], k)):
                            last = nc.vector.tensor_tensor(dst, columns(k, c), hi, ALU.subtract)
                    last.then_inc(s_lo, 1)
                dve.wait_ge(s_hi, KD + 1)
                nc.vector.tensor_tensor(wp[1][:, :, :].rearrange("p m n -> p (m n)"), psP[:, :],
                                        wp[0][:, :, :].rearrange("p m n -> p (m n)"), ALU.subtract).then_inc(s_lo, 1)

        RING, LAG = 4, 3
        with Stage(nc, name + "m") as s:
            vb = s.sb("v_batch", [P, TB, HEADS, 64], F32R)
            qh = s.sb("q_hi", [P, 512], F32R)
            kh = s.sb("k_hi", [P, 512], F32R)
            qs = [s.sb(f"q_stack{j}", [P, 512], F32R) for j in range(4)]
            ks = [s.sb(f"k_stack{j}", [P, 512], F32R) for j in range(4)]
            q2 = [s.sb(f"q_shifted{j}", [P, 512], F32R) for j in range(2)]
            mx = [s.sb(f"row_max{j}", [P, 8]) for j in range(2)]
            mh = s.sb("neg_max_hi", [P, 8], F32R)
            mc = s.sb("neg_max_columns", [P, TB, 2, 64])
            pT = [s.sb(f"probs{u}", [P, 512]) for u in range(RING)]
            pr = [[s.sb(f"probs_{q}{u}", [P, 512], F32R) for q in ("hi", "lo")] for u in range(RING)]
            cu, su, cx = ([s.sb(f"{n}{j}", [P, 512]) for j in range(2)] for n in ("raw_ctx", "sums", "ctx"))
            rc = s.sb("recip", [P, 512])
            cr = [[s.sb(f"ctx_{q}{j}", [P, 512], F32R) for q in ("hi", "lo")] for j in range(2)]
            psQ, psK = s.ps("Q"), s.ps("K")
            psS = [s.ps(f"S{j}") for j in range(2)]
            psT = [s.ps(f"T{j}") for j in range(2)]
            psC = [s.ps(f"C{j}") for j in range(2)]
            (s_zero, s_vb, s_q, s_k, s_qh, s_kh, s_qs, s_ks, s_sc, s_mx, s_mc, s_mt, s_q2, s_st, s_exp, s_pv, s_cu, s_rc,
             s_ctx, s_chi, s_clo, s_o, s_x) = (s.sem(n) for n in (
                 "zero", "vb", "q", "k", "qh", "kh", "qs", "ks", "score", "max", "maxcols", "maxT", "q2", "scoreT",
                 "exp", "pv", "raw_ctx", "recip", "ctx", "ctx_hi", "ctx_lo", "o", "x"))
            s_chain, s_pool_passed, s_vhi, s_plo = (s.sem(n) for n in ("chain", "pool_passed", "v_hi", "probs_lo"))
            UN = 8
            NU = PAIRS * UN
            CHUNKS = HEADS // 4
            LAST = B - 1
            LEAD = 4
            FIRST, ROUND = range(-4, 3), range(3, 3 + PAIRS)

            def there(b, pair):
                return pair >= 0 and (b is not LAST or pair < PAIRS)

            def score_at(n, u):
                return (n + 2, u + LEAD) if u < UN - LEAD else (n + 3, u + LEAD - UN)

            def chunk_at(b, n):
                return n % 2 == 0 and n >= 2 and there(b, n - 2)

            def whole(eng, step):
                for n in FIRST:
                    step(0, n)
                with eng.Fori(0, LAST) as b:
                    for n in ROUND:
                        step(b, n)
                for n in ROUND:
                    step(LAST, n)

            block = s.block()

            @block.gpsimd
            def _(pool):
                def fill(b, n, count, after=None):
                    at = slice(2 * n, 2 * n + 2)
                    v5 = v_all[:, bass.ds(b * TB, TB), :, :].rearrange("p t (q m) d -> p t q m d", m=4)
                    v_pair = v5[:, :, n % 2 * 2:n % 2 * 2 + 2, n // 2, :]
                    zero = M["zero"][:, :].unsqueeze(2).unsqueeze(3).to_broadcast([P, TB, 2, HD])
                    if after is not None:
                        wait_apart(pool, s_pv, after, s_pool_passed)
                    nc.gpsimd.tensor_tensor(vb[:, :, at, 0:HD], v_pair, zero, ALU.add).then_inc(s_vhi, 1)
                    wait_apart(pool, s_vhi, count, s_pool_passed)
                    nc.gpsimd.tensor_tensor(vb[:, :, at, HD:2 * HD], v_pair, vb[:, :, at, 0:HD], ALU.subtract)\
                        .then_inc(s_vb, 1)

                def step(b, n):
                    for u in range(UN):
                        if there(b, n + 1):
                            pool.wait_ge(s_exp, b * NU + ((n + 1) * UN + u + 3))
                            j = u % RING
                            nc.gpsimd.tensor_tensor(pr[j][1][:, :], pT[j][:, :], pr[j][0][:, :], ALU.subtract)\
                                .then_inc(s_plo, 1)
                    if b is not LAST and n in ROUND:
                        fill(b + 1, n - 3, b * PAIRS + (n + 6), after=b * HEADS + (2 * n - 4))

                nc.gpsimd.memset(vb[:, :, :, 32:64].bitcast(F32), 1.0)
                nc.gpsimd.memset(mc[:, :, :, :], 0.0).then_inc(s_zero, 1)
                for n in range(PAIRS):
                    fill(0, n, n + 1)
                whole(pool, step)

            @block.tensor
            def _(pe):
                def project(b, n, w, first, last):
                    if first == 0:
                        pe.wait_ge(s_qs if w is wq else s_ks, b * PAIRS + (n + 1))
                        if w is wq and n - 4 in ROUND:
                            pe.wait_ge(s_x, b * PAIRS + (n - 6))
                        if w is wk and n >= 2:
                            pe.wait_ge(s_q2, b * PAIRS + n)
                    toks = bass.ds(b * L + n // PAIRS * L, L)
                    at = n % PAIRS
                    for p in range(first, last + 1):
                        k, (i, j) = p // 3, PASSES[p % 3]
                        done = nc.tensor.matmul((psQ if w is wq else psK)[:, :], w[i][:, k, 2 * at:2 * at + 2, :, :].rearrange("p h a d -> p (h a d)"),
                                                xT[j][:, k, toks], start=p == 0, stop=p == 5)
                    if last == 5:
                        done.then_inc(s_q if w is wq else s_k, 1)

                def score(b, n, u):
                    h, t, j = u // 4, u % 4, n % 4
                    rows = slice(64 * h, 64 * h + 64)
                    if u == 0:
                        pe.wait_ge(s_qs, b * PAIRS + (n + 2))
                        pe.wait_ge(s_ks, b * PAIRS + (n + 2))
                    pe.wait_ge(s_mx, b * NU + (n * UN + u + 1))
                    nc.tensor.matmul(psS[u % 2][:, :], qs[j][rows, t * P:(t + 1) * P], ks[j][rows, :],
                                     start=True, stop=True).then_inc(s_sc, 1)

                def maxima(b, n):
                    pe.wait_ge(s_mc, b * PAIRS + (n + 1))
                    pe.wait_ge(s_q2, b * PAIRS + (n + 1))
                    if there(b, n + 1):
                        pe.wait_ge(s_ks, b * PAIRS + (n + 3))
                    for t in range(TB):
                        last = nc.tensor.transpose(psK[:, t * P:(t + 1) * P],
                                                   mc[:, t, :, :].rearrange("p h c -> p (h c)"), ident[:, :])
                    last.then_inc(s_mt, 1)

                def scoreT(b, n, u):
                    h, t = u // 4, u % 4
                    rows = slice(64 * h, 64 * h + 64)
                    if u == 0:
                        pe.wait_ge(s_q2, b * PAIRS + (n + 2))
                    pe.wait_ge(s_exp, b * NU + (n * UN + u + 1))
                    nc.tensor.matmul(psT[u % 2][:, :], ks[n % 4][rows, t * P:(t + 1) * P], q2[n % 2][rows, :],
                                     start=True, stop=True).then_inc(s_st, 1)

                def values(b, n, u):
                    h, t = u // 4, u % 4
                    if u == 0:
                        pe.wait_ge(s_vb, b * PAIRS + (n + 1))
                    pe.wait_ge(s_plo, b * NU + (n * UN + u + 1))
                    if t == 0:
                        pe.wait_ge(s_cu, b * HEADS + (2 * n + h + 1))
                    for q in range(2):
                        last = nc.tensor.matmul(psC[h][0:64, :], vb[:, t, n % PAIRS * 2 + h, :], pr[u % RING][q][:, :],
                                                start=t == 0 and q == 0, stop=t == TB - 1 and q == 1)
                    if t == TB - 1:
                        last.then_inc(s_pv, 1)

                def output(b, n, tile):
                    m, u = (n - 3) // 2, (n - 3) % 2
                    if tile == 0:
                        pe.wait_ge(s_clo, b * CHUNKS + (m + 1))
                        pe.wait_ge(s_x, b * PAIRS + (n - 2))
                        if there(b, n + 4):
                            pe.wait_ge(s_qs, b * PAIRS + (n + 6))
                    t = 2 * u + tile
                    last = product(nc, psQ[:, tile * D:(tile + 1) * D], [a[:, t * P:(t + 1) * P] for a in cr[m % 2]],
                                   [a[:, bass.ds(b, 1), :].rearrange("p a n -> p (a n)") for a in wp], True, True)
                    if tile == 1:
                        last.then_inc(s_o, 1)

                def step(b, n):
                    for u in range(UN):
                        if there(b, n + 1):
                            scoreT(b, n + 1, u)
                        if there(b, score_at(n, u)[0]):
                            score(b, *score_at(n, u))
                        if there(b, n + 4):
                            if u in (2, 3):
                                project(b, n + 4, wq, 3 * u - 6, 3 * u - 4)
                            if u in (6, 7):
                                project(b, n + 4, wk, 3 * u - 18, 3 * u - 16)
                        pair, unit = (n + 1, u - LAG) if u >= LAG else (n, u - LAG + UN)
                        if there(b, pair):
                            values(b, pair, unit)
                        if u == 4 and there(b, n + 2):
                            maxima(b, n + 2)
                    if n in ROUND:
                        output(b, n, 0)
                        output(b, n, 1)

                pe.sem_inc(s_o, 4)
                whole(pe, step)

            @block.scalar
            def _(act):
                def exp(b, n, u):
                    act.wait_ge(s_st, b * NU + (n * UN + u + 1))
                    j = u % RING
                    nc.scalar.activation(pT[j][:, :], psT[u % 2][:, :], ACT.Exp, scale=HD ** -0.5)
                    nc.scalar.activation(pr[j][0][:, :], psT[u % 2][:, :], ACT.Exp, scale=HD ** -0.5).then_inc(s_exp, 1)

                def read(b, n, h):
                    m, q = n // 2, (2 * n + h) % 4
                    act.wait_ge(s_pv, b * HEADS + (2 * n + h + 1))
                    act.wait_ge(s_ctx, b * CHUNKS + (m + 1))
                    nc.scalar.activation(su[m % 2][32 * q:32 * q + 32, :], psC[h][32:64, :], ACT.Copy)
                    nc.scalar.activation(cu[m % 2][32 * q:32 * q + 32, :], psC[h][0:32, :], ACT.Copy).then_inc(s_cu, 1)

                def q_hi(b, n):
                    act.wait_ge(s_q, b * PAIRS + (n + 1))
                    act.wait_ge(s_qs, b * PAIRS + (n + 1))
                    nc.scalar.activation(qh[:, :], psQ[:, :], ACT.Copy).then_inc(s_qh, 1)

                def k_hi(b, n):
                    act.wait_ge(s_k, b * PAIRS + (n + 1))
                    act.wait_ge(s_ks, b * PAIRS + (n + 1))
                    nc.scalar.activation(kh[:, :], psK[:, :], ACT.Identity, bias=one_k[:, 0:1]).then_inc(s_kh, 1)

                def context_hi(b, m):
                    act.wait_ge(s_ctx, b * CHUNKS + (m + 3))
                    act.wait_ge(s_o, b * PAIRS + (2 * m + 2))
                    nc.scalar.activation(cr[m % 2][0][:, :], cx[m % 2][:, :], ACT.Copy).then_inc(s_chi, 1)

                def step(b, n):
                    for u in range(UN):
                        if there(b, n + 1):
                            exp(b, n + 1, u)
                        if u == 0 and there(b, n + 3):
                            k_hi(b, n + 3)
                        if u == 2 and chunk_at(b, n - 1):
                            context_hi(b, (n - 3) // 2)
                        if u == 4 and there(b, n + 4):
                            q_hi(b, n + 4)
                        if u in (1, LAG + 1) and there(b, n):
                            read(b, n, u // LAG)

                act.sem_inc(s_exp, 2)
                act.sem_inc(s_cu, 2)
                whole(act, step)

            @block.vector
            def _(dve):
                def row_max(b, n, u):
                    dve.wait_ge(s_sc, b * NU + (n * UN + u + 1))
                    nc.vector.tensor_reduce(mx[n % 2][:, u:u + 1], psS[u % 2][:, :], AX, ALU.max).then_inc(s_mx, 1)

                def max_columns(b, n):
                    dve.wait_ge(s_mx, b * NU + (n * UN + UN + 2))
                    nc.vector.tensor_scalar(mh[:, :], mx[n % 2][:, :], -1.0, None, ALU.mult).then_inc(s_chain, 1)
                    dve.wait_ge(s_chain, b * PAIRS + (n + 1))
                    cols = mc[:, :, :, :].rearrange("p t h c -> p h t c")
                    by_head = [a[:, :].rearrange("p (h t) -> p h t", h=2) for a in (mx[n % 2], mh)]
                    nc.vector.tensor_copy(cols[:, :, :, 32], by_head[1])
                    nc.vector.scalar_tensor_tensor(cols[:, :, :, 33], by_head[0], -1.0, by_head[1],
                                                   ALU.mult, ALU.subtract).then_inc(s_mc, 1)

                def shift(b, n):
                    dve.wait_ge(s_mt, b * PAIRS + (n + 1))
                    nc.vector.tensor_tensor(q2[n % 2][:, :], psK[:, :], qs[n % 4][:, :], ALU.add).then_inc(s_q2, 1)

                def stack_q(b, n):
                    dve.wait_ge(s_qh, b * PAIRS + (n + 1))
                    nc.vector.scalar_tensor_tensor(qs[n % 4][:, :], qh[:, :], neg_q[:, 0:1], psQ[:, :],
                                                   ALU.mult, ALU.add).then_inc(s_qs, 1)

                def stack_k(b, n):
                    dve.wait_ge(s_kh, b * PAIRS + (n + 1))
                    nc.vector.scalar_tensor_tensor(ks[n % 4][:, :], kh[:, :], neg_k[:, 0:1], psK[:, :],
                                                   ALU.mult, ALU.add).then_inc(s_ks, 1)

                def invert(b, m, part):
                    if part == 0:
                        dve.wait_ge(s_cu, b * HEADS + (4 * m + 6))
                    cols = slice(part * P, (part + 1) * P)
                    nc.vector.reciprocal(rc[:, cols], su[m % 2][:, cols]).then_inc(s_rc, 1)

                def normalize(b, m):
                    dve.wait_ge(s_rc, b * (4 * CHUNKS) + (4 * m + 4))
                    nc.vector.tensor_tensor(cx[m % 2][:, :], cu[m % 2][:, :], rc[:, :], ALU.mult).then_inc(s_ctx, 1)

                def context_lo(b, m):
                    dve.wait_ge(s_chi, b * CHUNKS + (m + 1))
                    nc.vector.tensor_tensor(cr[m % 2][1][:, :], cx[m % 2][:, :], cr[m % 2][0][:, :], ALU.subtract)\
                        .then_inc(s_clo, 1)

                def output(b, n):
                    m, u = (n - 3) // 2, (n - 3) % 2
                    dve.wait_ge(s_o, b * PAIRS + (n + 2))
                    cols = slice((m * TB + 2 * u) * D, (m * TB + 2 * u + 2) * D)
                    nc.vector.tensor_tensor(x[:, cols], psQ[:, :], x[:, cols], ALU.add).then_inc(s_x, 1)

                def step(b, n):
                    for u in range(UN):
                        if there(b, score_at(n, u)[0]):
                            row_max(b, *score_at(n, u))
                        if u == 0 and there(b, n + 3):
                            stack_k(b, n + 3)
                        if u == 1 and chunk_at(b, n - 1):
                            normalize(b, (n - 3) // 2)
                        if u == 3 and there(b, n + 2):
                            max_columns(b, n + 2)
                        if u == 4 and chunk_at(b, n - 1):
                            context_lo(b, (n - 3) // 2)
                        if u == 5 and there(b, n + 2):
                            shift(b, n + 2)
                        if u == 6 and there(b, n + 4):
                            stack_q(b, n + 4)
                        if u == 7 and chunk_at(b, n + 1):
                            invert(b, (n - 1) // 2, 0)
                        if u in (1, 2, 4) and chunk_at(b, n):
                            invert(b, (n - 2) // 2, (1, 2, 4).index(u) + 1)
                    if n in ROUND:
                        output(b, n)

                dve.wait_ge(s_zero, 1)
                dve.sem_inc(s_mx, 2)
                dve.sem_inc(s_ctx, 2)
                dve.sem_inc(s_q2, 1)
                dve.sem_inc(s_qs, 1)
                dve.sem_inc(s_ks, 1)
                dve.sem_inc(s_x, 1)
                whole(dve, step)


def mamba(nc, M, name, w_in, b_in, conv_w, conv_b, a_log, d_param, dt_bias, norm_w, w_out, b_out, mup):
    H, PD, G, S, KW = 32, 64, 8, 32, 4
    DS = H * PD
    GF = DS // G
    HG = H // G
    GK = GF // P
    OX, OB, OC, ODT = DS, 2 * DS, 2 * DS + G * S, 2 * DS + 2 * G * S
    W = NT * H
    x, xT, ident = M["x"], M["xT"], M["ident"]
    with Stage(nc, name) as keep:
        dt = keep.sb("dt", [P, NT, H])
        cp = keep.sb("decay_from_start", [P, NT, H])
        tot = keep.sb("decay_of_chunk", [S, NT, H])
        aT = keep.sb("decay_parts", [3 * H, T], BF16)
        sel = keep.sb("select_head", [3 * H, H * P], BF16)
        delta = keep.sb("delta", [P, HG * P])
        cwx, cbx, mux, bix = (keep.sb(n, [P, (G + 1) * GK] + e) for n, e in
                              (("conv_w_x", [KW]), ("conv_b_x", []), ("mup_x", []), ("bias_x", [])))
        cwb, cbb, mub, bib = (keep.sb(n, [2 * S, G + 1] + e) for n, e in
                              (("conv_w_bc", [KW]), ("conv_b_bc", []), ("mup_bc", []), ("bias_bc", [])))
        dsk = keep.sb("d_skip", [P, H])
        nw = keep.sb("norm_w", [P, (G + 1) * GK])

        raw_z, raw_x = (keep.sb(n, [P, KD, GF]) for n in ("raw_z", "raw_x"))
        raw_bc = keep.sb("raw_bc", [P, KD, 2 * S])
        raw_o = keep.sb("raw_o", [P, GK, D])
        mup_z = keep.sb("mup_z", [P, GF])
        bias_z = keep.sb("bias_z", [1, GF])
        wz, wx, wb, wo, bz = ([[keep.sb(f"{n}_{q}{j}", shape, F32R) for q in ("hi", "lo")] for j in range(2)]
                              for n, shape in (("w_z", [P, KD, GF]), ("w_x", [P, KD, GF]), ("w_bc", [P, KD, 2 * S]),
                                               ("w_o", [P, GK, D]), ("bias_z", [1, GF])))
        LOADS, PREP = 7, 13
        s_raw, s_prep, s_w, s_pool_passed = (keep.sem(n) for n in ("raw", "prep", "weights", "pool_passed"))

        def prepare(pool, slot, g, n):
            if n == 0:
                return nc.gpsimd.tensor_tensor(raw_z[:, :, :], raw_z[:, :, :],
                                               mup_z[:, :].unsqueeze(1).to_broadcast([P, KD, GF]), ALU.mult)
            if n == 1:
                return nc.gpsimd.tensor_tensor(bias_z[:, :], bias_z[:, :], mup_z[0:1, :], ALU.mult)
            if n == 2:
                return nc.gpsimd.tensor_tensor(raw_o[:, :, :], raw_o[:, :, :],
                                               nw[:, bass.ds(g * GK, GK)].unsqueeze(2).to_broadcast([P, GK, D]), ALU.mult)
            w = ((wz, raw_z), (wx, raw_x), (wb, raw_bc), (wo, raw_o), (bz, bias_z))[(n - 3) % 5]
            hi, lo, raw = w[0][slot][0], w[0][slot][1], w[1]
            every = (slice(None),) * len(raw.shape)
            if n >= 8:
                return nc.gpsimd.tensor_tensor(lo[every], raw[every], hi[every], ALU.subtract)
            zero = M["zero"][0:raw.shape[0], :]
            if len(raw.shape) == 3:
                zero = zero.unsqueeze(2)
            return nc.gpsimd.tensor_tensor(hi[every], raw[every], zero.to_broadcast(list(raw.shape)), ALU.add)

        def prep(pool, slot, g, a, b, base, count):
            for n in range(a, b):
                if n == 0:
                    pool.wait_ge(s_raw, count * (LOADS * 16) + LOADS * 16)
                if n in (3, 8):
                    pool.wait_ge(s_prep, base + n)
                if n == 2:
                    wait_apart(pool, s_prep, base + 2, s_pool_passed)
                prepare(pool, slot, g, n).then_inc(s_prep, 1)
            if b == PREP:
                pool.wait_ge(s_prep, base + PREP)
                pool.sem_inc(s_w, 1)

        def load(sp, g):
            def cols(off, n):
                return w_in[:, bass.ds(g * n + off, n)].rearrange("(k p) n -> p k n", p=P)

            sp.dma_start(raw_z[:, :, :], cols(0, GF)).then_inc(s_raw, 16)
            sp.dma_start(raw_x[:, :, :], cols(OX, GF)).then_inc(s_raw, 16)
            sp.dma_start(raw_bc[:, :, 0:S], cols(OB, S)).then_inc(s_raw, 16)
            sp.dma_start(raw_bc[:, :, S:2 * S], cols(OC, S)).then_inc(s_raw, 16)
            sp.dma_start(raw_o[:, :, :], w_out[bass.ds(g * GF, GF), :].rearrange("(k p) n -> p k n", p=P))\
                .then_inc(s_raw, 16)
            one = bass.ds(g * GF, GF)
            sp.dma_start(mup_z[:, :], mup[one].rearrange("(o n) -> o n", o=1).to_broadcast([P, GF]))\
                .then_inc(s_raw, 16)
            sp.dma_start(bias_z[:, :], b_in[one].rearrange("(o n) -> o n", o=1)).then_inc(s_raw, 16)

        def row(v, a, b):
            return v[a:b].rearrange("(o n) -> o n", o=1).to_broadcast([P, b - a])

        with Stage(nc, name + "d") as s:
            bi, mu, db, al, na = (s.sb(n, [P, H]) for n in ("bias", "mup", "dt_bias", "a_log", "neg_a"))
            bo = s.sb("b_out", [P, D])
            v, r, u, q, p, t2 = (s.sb(n, [P, NT, H]) for n in ("v", "relu", "u", "q", "poly", "square"))
            parts = s.sb("parts", [P, NT, 3 * H], BF16)
            start = s.sb("start", [H, NT, P])
            inner = s.sb("inner", [H, NT, P])
            cpT = s.sb("cpT", [H, T])
            last_row = s.sb("last_row", [P, S])
            s_small, s_par, s_pc = s.sem("small"), s.sem("par"), s.sem("par_chain")
            s_c, s_na, s_ex, s_pool, s_parts = (s.sem(n) for n in ("chain", "neg_a", "exp", "pool", "parts"))
            s_tr, s_ev, s_aT, s_cp, s_cpt, s_cps, s_tot, s_xb = (
                s.sem(n) for n in ("tr", "ev", "aT", "cp", "cpT", "cps", "tot", "xb"))

            def loads(sp):
                for dst, v_ in ((bi, row(b_in, ODT, ODT + H)), (mu, row(mup, ODT, ODT + H)), (db, row(dt_bias, 0, H)),
                                (al, row(a_log, 0, H)), (dsk, row(d_param, 0, H)), (bo, row(b_out, 0, D))):
                    sp.dma_start(dst[:, :], v_).then_inc(s_small, 16)
                with nc.allow_non_contiguous_dma(reason="parameters of one word a partition"):
                    for src, off, dst in ((conv_b, 0, cbx), (mup, OX, mux), (b_in, OX, bix), (norm_w, 0, nw)):
                        sp.dma_start(dst[:, 0:G * GK], src[off:off + DS].rearrange("(c p) -> p c", p=P)).then_inc(s_par, 16)
                    for src, off, dst in ((conv_b, DS, cbb), (mup, OB, mub), (b_in, OB, bib)):
                        for h in range(2):
                            sp.dma_start(dst[h * S:(h + 1) * S, 0:G], src[off + h * G * S:off + (h + 1) * G * S]
                                         .rearrange("(g s) -> s g", s=S)).then_inc(s_par, 16)
                sp.dma_start(cwx[:, 0:G * GK, :], conv_w[0:DS, :].rearrange("(c p) k -> p c k", p=P)).then_inc(s_par, 16)
                for h in range(2):
                    sp.dma_start(cwb[h * S:(h + 1) * S, 0:G, :], conv_w[DS + h * G * S:DS + (h + 1) * G * S, :]
                                 .rearrange("(g s) k -> s g k", s=S)).then_inc(s_par, 16)

            def constants(pool):
                n = [0]
                link(pool, s_pool, n, nc.gpsimd.memset(sel[:, :], 1.0))
                for c in range(3):
                    rows = sel[32 * c:32 * c + 32, :].rearrange("r (e f) -> r e f", e=H)
                    link(pool, s_pool, n, nc.gpsimd.affine_select(
                        out=rows, in_=rows, compare_op=ALU.is_equal, fill=0.0, base=0,
                        pattern=[[-1, H], [0, P]], channel_multiplier=1))
                link(pool, s_pool, n, nc.gpsimd.memset(last_row[:, :], 1.0))
                link(pool, s_pool, n, nc.gpsimd.affine_select(
                    out=last_row[:, :], in_=last_row[:, :], compare_op=ALU.is_equal, fill=0.0, base=-(P - 1),
                    pattern=[[0, S]], channel_multiplier=1))
                for h in range(HG):
                    nc.gpsimd.tensor_copy(delta[:, h * P:(h + 1) * P], ident[:, :])
                link(pool, s_pool, n, nc.gpsimd.memset(start[:, :, :], 0.0))
                pool.wait_ge(s_par, 13 * 16)
                for a, w in ((cwx, GK), (cbx, GK), (mux, GK), (bix, GK), (nw, GK), (cwb, 1), (cbb, 1), (mub, 1), (bib, 1)):
                    last = nc.gpsimd.tensor_copy(a[:, G * w:(G + 1) * w], a[:, 0:w])
                last.then_inc(s_pc, 1)
                pool.wait_ge(s_pc, 1)
                nc.gpsimd.tensor_tensor(bix[:, :], bix[:, :], mux[:, :], ALU.mult).then_inc(s_pc, 1)
                nc.gpsimd.tensor_tensor(bib[:, :], bib[:, :], mub[:, :], ALU.mult).then_inc(s_pc, 1)

            with Stage(nc, name + "n") as n:
                norm = Norm(nc, M, n)
                run_block(nc, norm, Logits(nc, M, n, norm, w_in[:, ODT:ODT + H], H, None,
                                           v[:, :, :].rearrange("p t h -> p (t h)")),
                          Extra(sync=loads, gpsimd=constants), Extra(sync=lambda sp: load(sp, 0)))

            psD = s.ps("D")
            psR = [s.ps(f"R{j}", (P, 1024), BF16) for j in range(2)]
            psT = s.ps("T", (H, T))
            block = s.block()

            @block.gpsimd
            def _(pool):
                pool.wait_ge(s_small, 6 * 16)
                x3 = x[:, :].rearrange("p (t d) -> p t d", d=D)
                nc.gpsimd.tensor_tensor(x3, x3, bo[:, :].unsqueeze(1).to_broadcast([P, NT, D]), ALU.add)\
                    .then_inc(s_xb, 1)
                prep(pool, 0, 0, 0, PREP, 0, 0)

            @block.tensor
            def _(pe):
                pe.wait_ge(s_ex, 2)
                for t in range(NT):
                    last = nc.tensor.transpose(psT[:, t * P:(t + 1) * P], v[:, t, :], ident[:, :])
                last.then_inc(s_aT, 1)
                pe.wait_ge(s_parts, 1)
                for t in range(NT):
                    last = nc.tensor.transpose(psR[t // 8][0:3 * H, t % 8 * P:(t % 8 + 1) * P], parts[:, t, :],
                                               M["ident16"][:, :])
                    if t % 8 == 7:
                        last.then_inc(s_tr, 1)
                pe.wait_ge(s_cp, 1)
                for t in range(NT):
                    last = nc.tensor.transpose(psD[:, t * H:(t + 1) * H], cpT[:, t * P:(t + 1) * P], ident[0:H, 0:H])
                last.then_inc(s_cpt, 1)
                pe.wait_ge(s_cps, 1)
                nc.tensor.matmul(psT[:, 0:W], last_row[:, :], cp[:, :, :].rearrange("p t h -> p (t h)"),
                                 start=True, stop=True).then_inc(s_tot, 1)

            @block.scalar
            def _(act):
                act.wait_ge(s_na, 1)
                nc.scalar.activation(na[:, :], al[:, :], ACT.Exp).then_inc(s_na, 1)
                act.wait_ge(s_c, 5)
                nc.scalar.activation(u[:, :, :], q[:, :, :], ACT.Exp).then_inc(s_ex, 1)
                act.wait_ge(s_na, 4)
                nc.scalar.activation(v[:, :, :], q[:, :, :], ACT.Exp).then_inc(s_ex, 1)
                for j in range(2):
                    act.wait_ge(s_tr, j + 1)
                    nc.scalar.activation(aT[:, j * 1024:(j + 1) * 1024], psR[j][0:3 * H, :], ACT.Copy).then_inc(s_ev, 1)

            @block.vector
            def _(dve):
                n = [0]

                def chain(instruction):
                    link(dve, s_c, n, instruction)

                def each(a):
                    return a[:, :].unsqueeze(1).to_broadcast([P, NT, H])

                dve.wait_ge(s_small, 6 * 16)
                nc.vector.tensor_scalar(al[:, :], al[:, :], 80.0, None, ALU.min).then_inc(s_na, 1)
                ps3 = psD[:, :].rearrange("p (t h) -> p t h", h=H)
                chain(nc.vector.tensor_tensor(v[:, :, :], v[:, :, :], each(bi), ALU.add))
                chain(nc.vector.tensor_tensor(v[:, :, :], v[:, :, :], each(mu), ALU.mult))
                chain(nc.vector.tensor_tensor(v[:, :, :], v[:, :, :], each(db), ALU.add))
                chain(nc.vector.tensor_scalar(r[:, :, :], v[:, :, :], 0.0, None, ALU.max))
                chain(nc.vector.scalar_tensor_tensor(q[:, :, :], v[:, :, :], -1.0, v[:, :, :], ALU.mult, ALU.min))
                dve.wait_ge(s_ex, 1)
                chain(nc.vector.tensor_scalar(q[:, :, :], u[:, :, :], 2.0, None, ALU.add))
                chain(nc.vector.reciprocal(p[:, :, :], q[:, :, :]))
                chain(nc.vector.tensor_tensor(u[:, :, :], u[:, :, :], p[:, :, :], ALU.mult))
                chain(nc.vector.tensor_tensor(t2[:, :, :], u[:, :, :], u[:, :, :], ALU.mult))
                chain(nc.vector.tensor_scalar(p[:, :, :], t2[:, :, :], 1.0 / 15, None, ALU.mult))
                for d in (13, 11, 9, 7, 5, 3):
                    chain(nc.vector.scalar_tensor_tensor(p[:, :, :], p[:, :, :], 1.0 / d, t2[:, :, :], ALU.add, ALU.mult))
                chain(nc.vector.scalar_tensor_tensor(p[:, :, :], p[:, :, :], 1.0, u[:, :, :], ALU.add, ALU.mult))
                chain(nc.vector.scalar_tensor_tensor(dt[:, :, :], p[:, :, :], 2.0, r[:, :, :], ALU.mult, ALU.add))
                dve.wait_ge(s_na, 2)
                nc.vector.tensor_scalar(na[:, :], na[:, :], -1.0, None, ALU.mult).then_inc(s_na, 1)
                dve.wait_ge(s_na, 3)
                nc.vector.tensor_tensor(q[:, :, :], dt[:, :, :], each(na), ALU.mult).then_inc(s_na, 1)
                dve.wait_ge(s_ex, 2)
                chain(nc.vector.tensor_copy(parts[:, :, 0:H], v[:, :, :]))
                chain(nc.vector.tensor_tensor(p[:, :, :], v[:, :, :], parts[:, :, 0:H], ALU.subtract))
                chain(nc.vector.tensor_copy(parts[:, :, H:2 * H], p[:, :, :]))
                chain(nc.vector.tensor_tensor(u[:, :, :], p[:, :, :], parts[:, :, H:2 * H], ALU.subtract))
                nc.vector.tensor_copy(parts[:, :, 2 * H:3 * H], u[:, :, :]).then_inc(s_parts, 1)
                dve.wait_ge(s_aT, 1)
                dve.wait_ge(s_pool, 7)
                aT3 = psT[:, :].rearrange("h (t p) -> h t p", p=P)
                chain(nc.vector.tensor_copy(start[:, :, 0:1], aT3[:, :, 0:1]))
                chain(nc.vector.tensor_copy(inner[:, :, :], aT3))
                chain(nc.vector.memset(inner[:, :, 0:1], 0.0))
                nc.vector.tensor_tensor_scan(cpT[:, :], inner[:, :, :].rearrange("h t p -> h (t p)"),
                                             start[:, :, :].rearrange("h t p -> h (t p)"), 0.0, ALU.mult, ALU.add)\
                    .then_inc(s_cp, 1)
                dve.wait_ge(s_cpt, 1)
                nc.vector.tensor_copy(cp[:, :, :], ps3).then_inc(s_cps, 1)
                dve.wait_ge(s_ev, 2)
                nc.vector.memset(aT[:, :].rearrange("h (t p) -> h t p", p=P)[:, :, 0:1], 0.0)
                dve.wait_ge(s_tot, 1)
                nc.vector.tensor_copy(tot[:, :, :], psT[:, 0:W].rearrange("p (t h) -> p t h", h=H))

        with Stage(nc, name + "m") as s:
            ones = s.sb("ones", [1, P], F32R)
            t0w, t0b = s.sb("tap_scale_x", [P, (G + 1) * GK]), s.sb("tap_bias_x", [P, (G + 1) * GK])
            t0wb, t0bb = s.sb("tap_scale_bc", [2 * S, G + 1]), s.sb("tap_bias_bc", [2 * S, G + 1])
            xr = [s.sb(f"padded{j}", [P, KW - 1 + L]) for j in range(2)]
            acc = [s.sb(f"conv{j}", [P, L]) for j in range(2)]
            feat = [[s.sb(f"x{k}_{j}", [P, L]) for k in range(GK)] for j in range(2)]
            bT, cT = ([s.sb(f"{n}T{j}", [S, L]) for j in range(2)] for n in "bc")
            lt = [s.sb(f"decay{j}", [P, HG, P]) for j in range(2)]
            cb = [s.sb(f"cb{j}", [P, P]) for j in range(2)]
            mt = [s.sb(f"mix{j}", [P, HG, P]) for j in range(2)]
            xs, xdt, xde, xd, ys, yo, yd, yg = ([s.sb(f"{n}{j}", [P, HG, PD]) for j in range(2)] for n in
                                                ("x_tok", "xdt", "xdt_decayed", "x_skip", "y", "y_off", "y_sum", "y_gated"))
            zs = [s.sb(f"z{j}", [P, GF]) for j in range(4)]
            bt = [s.sb(f"b_tok{j}", [P, S]) for j in range(2)]
            state = s.sb("state", [S, HG, PD])
            yt = [[s.sb(f"yT_{q}{j}", [P, GK, P], F32R) for q in ("hi", "lo")] for j in range(2)]
            sq = s.sb("squares", [P, GF])
            ssq, rstd = ([s.sb(f"{n}{j}", [P, 1]) for j in range(2)] for n in ("mean_square", "rstd"))
            psP, psA, psX, psZ, psY, psS, psT, psO = (s.ps(n) for n in
                                                      ("ps_proj", "ps_decay", "ps_x", "ps_cbz", "ps_y", "ps_state", "ps_yT", "ps_out"))
            (s_tap, s_pad, s_pr, s_xr, s_t0, s_cc, s_cv, s_ft) = (s.sem(n) for n in (
                "tap", "pad", "proj", "xr", "tap0", "conv_chain", "conv", "feat"))
            (s_a, s_z, s_xt, s_zs, s_xs, s_scan, s_xdt, s_mt, s_xe, s_y, s_st, s_yo, s_ys, s_sc, s_S) = (
                s.sem(n) for n in ("a", "z", "xt", "zs", "xs", "scan", "xdt", "mt", "xe", "y", "st", "yo", "ys",
                                   "state_chain", "state"))
            (s_yd, s_yg, s_yt, s_hi, s_sq, s_lo, s_rs, s_o, s_x) = (
                s.sem(n) for n in ("yd", "yg", "yt", "hi", "sq", "lo", "rs", "o", "x"))
            eps_c, half_c = s.sb("eps", [P, 1]), s.sb("minus_half", [P, 1])
            s_eps = s.sem("eps")
            s_act_passed = s.sem("act_passed")
            NB, NC = B, L // P
            N = 2 * NB * NC
            UNITS = 3
            NU = 2 * NB * UNITS
            NS = 2 * NB * (NC - 1)
            ROUNDS = G // 2
            TAPS = ((0, 1, 2), (3, 4), (5, 6), (7, 8))
            steps = [(slot, b, c) for slot in range(2) for b in range(NB) for c in range(NC)]
            tile = lambda n: steps[n][1] * NC + steps[n][2]
            st_at = lambda n: n // NC * (NC - 1) + n % NC
            block = s.block()

            CARRY = {n + 1: (1, 2 * n, min(2 * n + 2, PREP)) for n in range(7)}
            CARRY.update({n + 20: (0, 2 * n, min(2 * n + 2, PREP)) for n in range(7)})

            @block.sync
            def _(sp):
                with sp.Fori(0, ROUNDS - 1) as it:
                    for h in range(2):
                        sp.wait_ge(s_w, it * 2 + (h + 1))
                        load(sp, it * 2 + (h + 1))
                sp.wait_ge(s_w, ROUNDS * 2 - 1)
                load(sp, G - 1)
                sp.wait_ge(s_w, ROUNDS * 2)
                load(sp, 0)

            @block.gpsimd
            def _(pool):
                pool.sem_inc(s_xe, 2)
                nc.gpsimd.memset(eps_c[:, :], EPS)
                nc.gpsimd.memset(half_c[:, :], -0.5)
                for j in range(2):
                    nc.gpsimd.memset(xr[j][:, 0:KW - 1], 0.0)
                nc.gpsimd.memset(ones[:, :].bitcast(F32), 1.0).then_inc(s_pad, 1)
                n = [0]
                for w, m, bi_, cb_, tw, tb in ((cwx, mux, bix, cbx, t0w, t0b), (cwb, mub, bib, cbb, t0wb, t0bb)):
                    nc.gpsimd.tensor_tensor(tw[:, :], w[:, :, KW - 1], m[:, :], ALU.mult)
                    link(pool, s_tap, n, nc.gpsimd.tensor_tensor(tb[:, :], w[:, :, KW - 1], bi_[:, :], ALU.mult))
                    link(pool, s_tap, n, nc.gpsimd.tensor_tensor(tb[:, :], tb[:, :], cb_[:, :], ALU.add))
                with pool.Fori(0, ROUNDS) as it:
                    for n in range(N + 2):
                        if n < N:
                            slot, b, c = steps[n]
                            j = n % 2
                            pool.wait_ge(s_scan, it * N + (n + 2))
                            pool.wait_ge(s_zs, it * N + (n + 2))
                            nc.gpsimd.tensor_tensor(mt[j][:, :, :], lt[j][:, :, :],
                                                    cb[j][:, :].unsqueeze(1).to_broadcast([P, HG, P]), ALU.mult)\
                                .then_inc(s_mt, 1)
                            wait_apart(pool, s_xs, it * N + (n + 2), s_pool_passed)
                            heads = bass.ds(it * (2 * HG) + slot * HG, HG)
                            nc.gpsimd.tensor_tensor(xd[j][:, :, :], xs[j][:, :, :],
                                                    dsk[:, heads].unsqueeze(2).to_broadcast([P, HG, PD]), ALU.mult)
                            pool.wait_ge(s_xdt, it * N + (n + 2))
                            nc.gpsimd.tensor_tensor(xde[j][:, :, :], xdt[j][:, :, :],
                                                    lt[j][:, :, P - 1:P].to_broadcast([P, HG, PD]), ALU.mult)\
                                .then_inc(s_xe, 1)
                        if 1 <= n <= N:
                            p = n - 1
                            pool.wait_ge(s_ys, it * N + (p + 2))
                            pool.wait_ge(s_xe, it * N + (p + 3))
                            nc.gpsimd.tensor_tensor(yd[p % 2][:, :, :], ys[p % 2][:, :, :], xd[p % 2][:, :, :], ALU.add)\
                                .then_inc(s_yd, 1)
                        if n >= 2:
                            p = n - 2
                            pool.wait_ge(s_sq, it * N + (p + 1))
                            nc.gpsimd.tensor_tensor(ssq[p % 2][:, :], ssq[p % 2][:, :], eps_c[:, :], ALU.add)\
                                .then_inc(s_eps, 1)
                            pool.wait_ge(s_eps, it * N + (p + 1))
                            nc.gpsimd.tensor_tensor(rstd[p % 2][:, :], ssq[p % 2][:, :], half_c[:, :], ALU.pow)\
                                .then_inc(s_rs, 1)
                        if n in CARRY:
                            slot, a, e = CARRY[n]
                            if a == 0:
                                pool.wait_ge(s_o, it * N + (1 if slot else N // 2 + 1))
                            k = 1 if slot else 2
                            prep(pool, slot, it * 2 + 1 if slot else it * 2 + 2, a, e,
                                 it * (2 * PREP) + k * PREP, it * 2 + k)

            def unit_at(it, mm, c):
                return it * NU + (mm * UNITS + c)

            def cols_at(it, mm, c):
                return it * (2 * GK) + (mm // NB * GK + c)

            @block.tensor
            def _(pe):
                def project(it, mm, c, first=False):
                    slot, b = mm // NB % 2, mm % NB
                    if b == 0 and c == 0:
                        pe.wait_ge(s_w, it * 2 + (mm // NB + 1))
                    if not first:
                        pe.wait_ge(s_t0, unit_at(it, mm, c))
                    w = wb if c == 2 else wx
                    k0, m = (0, 2 * S) if c == 2 else (c * P, P)
                    for k in range(KD):
                        last = product(nc, psP[0:m, :], [a[:, k, k0:k0 + m] for a in w[slot]],
                                       [a[:, k, b * L:(b + 1) * L] for a in xT], k == 0, k == KD - 1)
                    last.then_inc(s_pr, 1)

                def decays(it, n):
                    slot, tt = steps[n][0], tile(n)
                    pe.wait_ge(s_scan, it * N + (n + 1))
                    for h in range(HG):
                        last = nc.tensor.matmul(psA[:, h * P:(h + 1) * P],
                                                sel[:, bass.ds(it * (2 * HG * P) + (slot * HG + h) * P, P)],
                                                aT[:, tt * P:(tt + 1) * P], start=True, stop=True)
                    last.then_inc(s_a, 1)

                def gate(it, n):
                    (slot, b, c), mm, tt = steps[n], n // NC, tile(n)
                    chunk = slice(c * P, (c + 1) * P)
                    if c == 0:
                        pe.wait_ge(s_ft, unit_at(it, mm + 1, 0))
                    pe.wait_ge(s_zs, it * N + (n + 1))
                    nc.tensor.matmul(psZ[:, 0:P], bT[mm % 2][:, chunk], cT[mm % 2][:, chunk], start=True, stop=True)
                    for k in range(KD):
                        product(nc, psZ[:, P:P + GF], [a[:, k, tt * P:(tt + 1) * P] for a in xT],
                                [a[:, k, :] for a in wz[slot]], k == 0, False)
                    nc.tensor.matmul(psZ[:, P:P + GF], ones[:, :], bz[slot][0][:, :], start=False, stop=False)
                    nc.tensor.matmul(psZ[:, P:P + GF], ones[:, :], bz[slot][1][:, :], start=False, stop=True)\
                        .then_inc(s_z, 1)

                def tokens(it, n):
                    mm, c = n // NC, steps[n][2]
                    chunk = slice(c * P, (c + 1) * P)
                    pe.wait_ge(s_xs, it * N + (n + 1))
                    pe.wait_ge(s_xdt, it * N + (n + 1))
                    for k in range(GK):
                        nc.tensor.transpose(psX[:, k * P:(k + 1) * P], feat[mm % 2][k][:, chunk], ident[:, :])
                    nc.tensor.transpose(psX[:, GF:GF + S], bT[mm % 2][:, chunk], ident[0:S, 0:S]).then_inc(s_xt, 1)

                def mix(it, p):
                    (slot, b, c), mm, j = steps[p], p // NC, p % 2
                    pe.wait_ge(s_mt, it * N + (p + 1))
                    pe.wait_ge(s_xdt, it * N + (p + 2))
                    pe.wait_ge(s_xs, it * N + (p + 2))
                    pe.wait_ge(s_ys, it * N + (p + 1))
                    if c > 0:
                        pe.wait_ge(s_S, it * NS + (st_at(p - 1) + 2))
                        nc.tensor.matmul(psY[:, GF:2 * GF], cT[mm % 2][:, c * P:(c + 1) * P],
                                         state[:, :, :].rearrange("s h d -> s (h d)"), start=True, stop=True)
                    for h in range(HG):
                        last = nc.tensor.matmul(psY[:, h * PD:(h + 1) * PD], mt[j][:, h, :], xdt[j][:, h, :],
                                                start=True, stop=True)
                    last.then_inc(s_y, 1)
                    if c < NC - 1:
                        pe.wait_ge(s_xe, it * N + (p + 3))
                        pe.wait_ge(s_S, it * NS + (st_at(p) + 1))
                        nc.tensor.matmul(psS[0:S, 0:GF], bt[j][:, :], xde[j][:, :, :].rearrange("p h d -> p (h d)"),
                                         start=True, stop=True).then_inc(s_st, 1)

                def turn(it, p):
                    pe.wait_ge(s_yg, it * N + (p + 1))
                    pe.wait_ge(s_lo, it * N + (p + 1))
                    for k in range(GK):
                        last = nc.tensor.transpose(
                            psT[:, k * P:(k + 1) * P],
                            yg[p % 2][:, :, :].rearrange("p h d -> p (h d)")[:, k * P:(k + 1) * P], ident[:, :])
                    last.then_inc(s_yt, 1)

                def output(it, p):
                    pe.wait_ge(s_lo, it * N + (p + 2))
                    pe.wait_ge(s_x, it * N + (p + 1))
                    for k in range(GK):
                        last = product(nc, psO[:, 0:D], [a[:, k, :] for a in yt[p % 2]],
                                       [a[:, k, :] for a in wo[steps[p][0]]], k == 0, k == GK - 1)
                    last.then_inc(s_o, 1)

                pe.sem_inc(s_o, 1)
                for c in range(UNITS):
                    project(0, 0, c, first=c == 0)
                with pe.Fori(0, ROUNDS) as it:
                    for n in range(N + 3):
                        if n < N and steps[n][2] < UNITS:
                            project(it, n // NC + 1, steps[n][2])
                        if n < N:
                            decays(it, n)
                        if n < N:
                            gate(it, n)
                        if n < N:
                            tokens(it, n)
                        if 1 <= n <= N:
                            mix(it, n - 1)
                        if n >= 3:
                            output(it, n - 3)
                        if 2 <= n < N + 2:
                            turn(it, n - 2)

            @block.scalar
            def _(act):
                def unit_in(it, mm, c, first=0):
                    u = unit_at(it, mm, c)
                    j = (mm * UNITS + c) % 2
                    if not first:
                        act.wait_ge(s_cv, u - 1)
                        act.wait_ge(s_ft, u - 1)
                    wait_apart(act, s_pr, u + 1, s_act_passed)
                    m = 2 * S if c == 2 else P
                    col = bass.ds(it * 2 + mm // NB, 1) if c == 2 else bass.ds(cols_at(it, mm, c), 1)
                    mu_, bi_, tw, tb = (mub, bib, t0wb, t0bb) if c == 2 else (mux, bix, t0w, t0b)
                    nc.scalar.activation(xr[j][0:m, KW - 1:], psP[0:m, :], ACT.Identity, bias=bi_[:, col],
                                         scale=mu_[:, col]).then_inc(s_xr, 1)
                    nc.scalar.activation(acc[j][0:m, :], psP[0:m, :], ACT.Identity, bias=tb[:, col],
                                         scale=tw[:, col]).then_inc(s_t0, 1)

                def unit_out(it, mm, c, first=False):
                    u = unit_at(it, mm, c)
                    j = (mm * UNITS + c) % 2
                    act.wait_ge(s_cv, u + 1)
                    if c < 2:
                        nc.scalar.activation(feat[mm % 2][c][:, :], acc[j][:, :], ACT.Silu).then_inc(s_ft, 1)
                    else:
                        nc.scalar.activation(bT[mm % 2][:, :], acc[j][0:S, :], ACT.Silu)
                        nc.scalar.activation(cT[mm % 2][:, :], acc[j][S:2 * S, :], ACT.Silu).then_inc(s_ft, 1)

                act.sem_inc(s_zs, 1)
                act.sem_inc(s_xs, 1)
                act.wait_ge(s_tap, 4)
                act.wait_ge(s_pad, 1)
                for c in range(UNITS):
                    unit_in(0, 0, c, first=c < 2)
                    unit_out(0, 0, c)
                with act.Fori(0, ROUNDS) as it:
                    for n in range(N + 2):
                        if n < N:
                            slot, b, c = steps[n]
                            mm, j = n // NC, n % 2
                            if c < UNITS:
                                unit_in(it, mm + 1, c)
                            act.wait_ge(s_z, it * N + (n + 1))
                            act.wait_ge(s_xe, it * N + (n + 1))
                            nc.scalar.activation(zs[n % 4][:, :], psZ[:, P:P + GF], ACT.Silu)
                            nc.scalar.activation(cb[j][:, :], psZ[:, 0:P], ACT.Copy).then_inc(s_zs, 1)
                            act.wait_ge(s_xt, it * N + (n + 1))
                            act.wait_ge(s_xdt, it * N + (n + 2))
                            nc.scalar.activation(bt[j][:, :], psX[:, GF:GF + S], ACT.Copy)
                            nc.scalar.activation(xs[j][:, :, :], psX[:, 0:GF].rearrange("p (h d) -> p h d", h=HG),
                                                 ACT.Copy).then_inc(s_xs, 1)
                            if c > 0:
                                unit_out(it, mm + 1, c - 1)
                        if n >= 2:
                            p = n - 2
                            act.wait_ge(s_yg, it * N + (p + 1))
                            nc.scalar.activation(sq[:, :], yg[p % 2][:, :, :].rearrange("p h d -> p (h d)"), ACT.Square,
                                                 scale=GF ** -0.5, accum_out=ssq[p % 2][:, :]).then_inc(s_sq, 1)
                            act.wait_ge(s_yt, it * N + (p + 1))
                            nc.scalar.activation(yt[p % 2][0][:, :, :], psT[:, 0:GF].rearrange("p (k t) -> p k t", k=GK),
                                                 ACT.Copy).then_inc(s_hi, 1)

            @block.vector
            def _(dve):
                def tap(it, mm, q):
                    c, k = q // (KW - 1), q % (KW - 1)
                    u = unit_at(it, mm, c)
                    j = (mm * UNITS + c) % 2
                    m = 2 * S if c == 2 else P
                    if k == 0:
                        dve.wait_ge(s_xr, u + 1)
                        dve.wait_ge(s_t0, u + 1)
                    else:
                        dve.wait_ge(s_cc, it * (2 * NU) + ((mm * UNITS + c) * 2 + k))
                    w = cwb if c == 2 else cwx
                    col = bass.ds(it * 2 + mm // NB, 1) if c == 2 else bass.ds(cols_at(it, mm, c), 1)
                    t = KW - 2 - k
                    nc.vector.scalar_tensor_tensor(
                        acc[j][0:m, :], xr[j][0:m, t:t + L], w[:, col, t], acc[j][0:m, :],
                        ALU.mult, ALU.add).then_inc(s_cv if k == KW - 2 else s_cc, 1)

                for sem in (s_scan, s_xdt, s_ys, s_S, s_lo, s_x):
                    dve.sem_inc(sem, 1)
                for q in range(UNITS * (KW - 1)):
                    tap(0, 0, q)
                with dve.Fori(0, ROUNDS) as it:
                    for n in range(N + 3):
                        if 2 <= n < N + 2:
                            p = n - 2
                            dve.wait_ge(s_yd, it * N + (p + 1))
                            dve.wait_ge(s_zs, it * N + (p + 2))
                            nc.vector.tensor_tensor(yg[p % 2][:, :, :], yd[p % 2][:, :, :],
                                                    zs[p % 4][:, :].rearrange("p (h d) -> p h d", h=HG), ALU.mult)\
                                .then_inc(s_yg, 1)
                        if n < N:
                            slot, b, c = steps[n]
                            mm, tt, j = n // NC, tile(n), n % 2
                            heads = bass.ds(it * (2 * HG) + slot * HG, HG)
                            tap(it, mm + 1, TAPS[c][0])
                            dve.wait_ge(s_a, it * N + (n + 1))
                            dve.wait_ge(s_xe, it * N + (n + 1))
                            nc.vector.tensor_tensor_scan(lt[j][:, :, :].rearrange("p h i -> p (h i)"), psA[:, :],
                                                         delta[:, :], 0.0, ALU.mult, ALU.add).then_inc(s_scan, 1)
                            dve.wait_ge(s_xt, it * N + (n + 1))
                            nc.vector.tensor_tensor(xdt[j][:, :, :], psX[:, 0:GF].rearrange("p (h d) -> p h d", h=HG),
                                                    dt[:, tt, heads].unsqueeze(2).to_broadcast([P, HG, PD]), ALU.mult)\
                                .then_inc(s_xdt, 1)
                            for q in TAPS[c][1:]:
                                tap(it, mm + 1, q)
                        if 1 <= n <= N:
                            p = n - 1
                            slot, b, c = steps[p]
                            tt, j = tile(p), p % 2
                            heads = bass.ds(it * (2 * HG) + slot * HG, HG)
                            dve.wait_ge(s_y, it * N + (p + 1))
                            y3 = psY[:, :].rearrange("p (o h d) -> p o h d", o=2, h=HG)
                            if c > 0:
                                nc.vector.tensor_tensor(yo[j][:, :, :], y3[:, 1],
                                                        cp[:, tt, heads].unsqueeze(2).to_broadcast([P, HG, PD]), ALU.mult)\
                                    .then_inc(s_yo, 1)
                                dve.wait_ge(s_yo, it * NS + (st_at(p - 1) + 1))
                                nc.vector.tensor_tensor(ys[j][:, :, :], y3[:, 0], yo[j][:, :, :], ALU.add).then_inc(s_ys, 1)
                            else:
                                nc.vector.tensor_copy(ys[j][:, :, :], y3[:, 0]).then_inc(s_ys, 1)
                            if c < NC - 1:
                                ps3 = psS[0:S, 0:GF].rearrange("s (h d) -> s h d", h=HG)
                                dve.wait_ge(s_st, it * NS + (st_at(p) + 1))
                                if c == 0:
                                    nc.vector.tensor_copy(state[:, :, :], ps3).then_inc(s_S, 1)
                                else:
                                    nc.vector.tensor_tensor(
                                        state[:, :, :], state[:, :, :],
                                        tot[:, tt, heads].unsqueeze(2).to_broadcast([S, HG, PD]), ALU.mult)\
                                        .then_inc(s_sc, 1)
                                    dve.wait_ge(s_sc, it * (2 * NB * (NC - 2)) + (p // NC * (NC - 2) + c))
                                    nc.vector.tensor_tensor(state[:, :, :], ps3, state[:, :, :], ALU.add).then_inc(s_S, 1)
                        if n >= 3:
                            p = n - 3
                            cols = slice(tile(p) * D, (tile(p) + 1) * D)
                            dve.wait_ge(s_o, it * N + (p + 2))
                            dve.wait_ge(s_rs, it * N + (p + 1))
                            nc.vector.scalar_tensor_tensor(x[:, cols], psO[:, 0:D], rstd[p % 2][:, 0:1], x[:, cols],
                                                           ALU.mult, ALU.add).then_inc(s_x, 1)
                        if 2 <= n < N + 2:
                            p = n - 2
                            dve.wait_ge(s_hi, it * N + (p + 1))
                            nc.vector.tensor_tensor(yt[p % 2][1][:, :, :], psT[:, 0:GF].rearrange("p (k t) -> p k t", k=GK),
                                                    yt[p % 2][0][:, :, :], ALU.subtract).then_inc(s_lo, 1)


def macaron(nc, hidden, m_in, f_in, s_in, e_in, out):
    with ExitStack() as ctx:
        M = common(nc, ctx)
        with Stage(nc, "in") as s:
            x_in = [s.sem(f"x{b}") for b in range(B)]
            stage_load(nc, M, hidden, x_in)
            ffn0(nc, M, "f1", *f_in, x_loaded=x_in)
        mamba(nc, M, "ssm", *m_in)
        ffn0(nc, M, "f3", *f_in)
        ffn1(nc, M, "f4", *e_in)
        attention(nc, M, "at", *s_in)
        ffn1(nc, M, "f6", *e_in)
        stage_store(nc, M, out)


_MAMBA = ["L0_attn_" + n for n in ("W_in", "b_in", "conv_w", "conv_b", "A_log", "D_param", "dt_bias", "norm_w", "W_out",
                                   "b_out", "mup_vector")]
_FFN0 = ["L0_ffn_" + n for n in ("w_gate", "w1", "w3", "w2")]
_ATTN = ["L1_attn_" + n for n in ("Wqkv", "Wproj", "bproj")]
_FFN1 = ["L1_ffn_" + n for n in ("gate_w", "wg", "wu", "wd", "sg", "su", "sd")]


def kernel(**inputs):
    import numpy as _np
    import concourse.bacc as _bacc
    from concourse.bass_utils import run_bass_kernel_spmd as _run

    nc = _bacc.Bacc("TRN2", target_bir_lowering=False, num_devices=1)
    arrays, aps = {}, {}
    for name in ["L0_attn_hidden_states"] + _MAMBA + _FFN0 + _ATTN + _FFN1:
        a = _np.ascontiguousarray(inputs[name])
        arrays[f"in_{name}_dram"] = a
        aps[name] = nc.dram_tensor(f"in_{name}_dram", a.shape, mybir.dt.from_np(a.dtype), kind="ExternalInput").ap()
    out = nc.dram_tensor("out_0_dram", (B, L, D), F32, kind="ExternalOutput").ap()
    macaron(nc, aps["L0_attn_hidden_states"], *([aps[n] for n in g] for g in (_MAMBA, _FFN0, _ATTN, _FFN1)), out)
    r = _run(nc, [arrays], core_ids=[0])
    return r.results[0]["out_0_dram"]
```
